# Optimizing a Trainium2 kernel written in Bass

```python
import numpy as np
import jax
import jax.numpy as jnp

def _softmax(x, axis=-1):
    return jax.nn.softmax(x, axis=axis)

def _gelu(x):
    return jax.nn.gelu(x, approximate=True)

def _silu(x):
    return jax.nn.silu(x)

def _sigmoid(x):
    return jax.nn.sigmoid(x)

def _layernorm(x, axis=-1, eps=1e-05):
    m = jnp.mean(x, axis=axis, keepdims=True)
    v = jnp.var(x, axis=axis, keepdims=True)
    return (x - m) / jnp.sqrt(v + eps)

def _scatter_add(tgt, idx, src, axis=0):
    return tgt.at[idx].add(src)

def _segment_sum(src, seg, n):
    return jax.ops.segment_sum(src, seg, n)
kernel_name = 'mk_recurrent_d2_jaxref_r4_396089'

def setup_inputs(seed: int=0):
    np.random.seed(seed)
    _w = jnp.asarray

    def _L0_attn_setup():
        import jax, jax.numpy as jnp
        import numpy as np
        B, L, D, H = (2, 512, 256, 16)
        C = D // H
        SCALE = 1.0 / np.sqrt(D).astype(np.float32)
        key = jax.random.key(seed)
        ks = jax.random.split(key, 5)
        return {'x': jax.random.normal(ks[0], (B, L, D), dtype=jnp.float32), 'w_qkv': jax.random.normal(ks[1], (3 * D, D), dtype=jnp.float32) * (1.0 / np.sqrt(D)), 'b_qkv': jax.random.normal(ks[2], (3 * D,), dtype=jnp.float32) * 0.02, 'w_o': jax.random.normal(ks[3], (D, D), dtype=jnp.float32) * (1.0 / np.sqrt(D)), 'b_o': jax.random.normal(ks[4], (D,), dtype=jnp.float32) * 0.02}
    _L0_attn_in = _L0_attn_setup()

    def _L0_ffn_setup():
        import jax, jax.numpy as jnp
        import numpy as np
        B, T, D, R, KEXP = (4, 1024, 256, 64, 8)
        RH = max(D, 32)
        SCALE = 0.02

        def _fused_branch(Q_side, K_side, V, W, U, b, router_w1, router_b1, router_w2, router_b2, expert_bias):
            xV = jnp.einsum('btd,kdr->btkr', Q_side, V)
            yW = jnp.einsum('btd,kdr->btkr', K_side, W)
            cum_yW = jnp.cumsum(yW, axis=1)
            prod = xV * cum_yW
            h = jax.nn.gelu(Q_side @ router_w1.T + router_b1, approximate=False)
            logits = h @ router_w2.T + router_b2 + expert_bias
            weights = jax.nn.softmax(logits, axis=-1)
            out = jnp.einsum('btkr,kdr->btd', prod * weights[..., None], U)
            out = out + weights @ b
            n_valid = jnp.arange(1, Q_side.shape[1] + 1, dtype=Q_side.dtype)
            return out / n_valid[None, :, None]
        key = jax.random.key(seed)
        ks = jax.random.split(key, 20)
        x = jax.random.normal(ks[0], (B, T, D), dtype=jnp.float32)
        W_Q = jax.random.normal(ks[1], (D, D), dtype=jnp.float32) * (1.0 / np.sqrt(D))
        W_K = jax.random.normal(ks[2], (D, D), dtype=jnp.float32) * (1.0 / np.sqrt(D))
        W_O = jax.random.normal(ks[3], (D, D), dtype=jnp.float32) * (1.0 / np.sqrt(D))
        W_inv = jnp.eye(D, dtype=jnp.float32) + 0.01 * jax.random.normal(ks[4], (D, D), dtype=jnp.float32)
        V_fwd = jax.random.normal(ks[5], (KEXP, D, R), dtype=jnp.float32) * SCALE
        W_fwd = jax.random.normal(ks[6], (KEXP, D, R), dtype=jnp.float32) * SCALE
        U_fwd = jax.random.normal(ks[7], (KEXP, D, R), dtype=jnp.float32) * SCALE
        b_fwd = jnp.zeros((KEXP, D), dtype=jnp.float32)
        V_inv = jax.random.normal(ks[8], (KEXP, D, R), dtype=jnp.float32) * SCALE
        W_inv_exp = jax.random.normal(ks[9], (KEXP, D, R), dtype=jnp.float32) * SCALE
        U_inv = jax.random.normal(ks[10], (KEXP, D, R), dtype=jnp.float32) * SCALE
        b_inv = jnp.zeros((KEXP, D), dtype=jnp.float32)
        router_w1 = jax.random.normal(ks[11], (RH, D), dtype=jnp.float32) * (1.0 / np.sqrt(D))
        router_b1 = jnp.zeros((RH,), dtype=jnp.float32)
        router_w2 = jax.random.normal(ks[12], (KEXP, RH), dtype=jnp.float32) * (1.0 / np.sqrt(RH))
        router_b2 = jnp.zeros((KEXP,), dtype=jnp.float32)
        alpha_bi = jnp.asarray(0.5, dtype=jnp.float32)
        expert_bias = jnp.zeros((KEXP,), dtype=jnp.float32)
        return dict(x=x, W_Q=W_Q, W_K=W_K, W_O=W_O, W_inv=W_inv, V_fwd=V_fwd, W_fwd=W_fwd, U_fwd=U_fwd, b_fwd=b_fwd, V_inv=V_inv, W_inv_exp=W_inv_exp, U_inv=U_inv, b_inv=b_inv, router_w1=router_w1, router_b1=router_b1, router_w2=router_w2, router_b2=router_b2, alpha_bi=alpha_bi, expert_bias=expert_bias)
    _L0_ffn_in = _L0_ffn_setup()

    def _L1_attn_setup():
        import jax, jax.numpy as jnp
        import numpy as np
        B, S, D = (2, 512, 256)
        H = 16
        HD = D // H
        WINDOW = 128
        SCALE = HD ** (-0.5)

        def _local_mask(seq_len):
            idx = jnp.arange(seq_len)
            band = jnp.abs(idx[:, None] - idx[None, :]) <= WINDOW // 2
            return jnp.where(band, 0.0, -jnp.inf).astype(jnp.float32)
        key = jax.random.key(seed)
        ks = jax.random.split(key, 5)
        x = jax.random.normal(ks[0], (B, S, D), dtype=jnp.float32)
        w_qkv = jax.random.normal(ks[1], (D, 3 * D), dtype=jnp.float32) * D ** (-0.5)
        b_qkv = jax.random.normal(ks[2], (3 * D,), dtype=jnp.float32) * 0.02
        w_out = jax.random.normal(ks[3], (D, D), dtype=jnp.float32) * D ** (-0.5)
        b_out = jax.random.normal(ks[4], (D,), dtype=jnp.float32) * 0.02
        return {'x': x, 'w_qkv': w_qkv, 'b_qkv': b_qkv, 'w_out': w_out, 'b_out': b_out}
    _L1_attn_in = _L1_attn_setup()

    def _L1_ffn_setup():
        import jax, jax.numpy as jnp
        import numpy as np
        key = jax.random.key(seed)
        ks = jax.random.split(key, 5)
        B, S, D_in, D_out, E, R = (4, 256, 256, 256, 8, 16)
        x = jax.random.normal(ks[0], (B, S, D_in), dtype=jnp.float32)
        weight = jax.random.normal(ks[1], (D_out, D_in), dtype=jnp.float32) / np.sqrt(D_in)
        gate_w = jax.random.normal(ks[2], (E, D_in), dtype=jnp.float32) / np.sqrt(D_in)
        lora_U = jax.random.normal(ks[3], (E, R, D_in), dtype=jnp.float32) / np.sqrt(D_in)
        lora_V = jax.random.normal(ks[4], (E, D_out, R), dtype=jnp.float32) / np.sqrt(R)
        return {'x': x, 'weight': weight, 'gate_w': gate_w, 'lora_U': lora_U, 'lora_V': lora_V}
    _L1_ffn_in = _L1_ffn_setup()
    _d = {'L0_attn_x': _L0_attn_in['x'], 'L0_attn_w_qkv': _L0_attn_in['w_qkv'], 'L0_attn_b_qkv': _L0_attn_in['b_qkv'], 'L0_attn_w_o': _L0_attn_in['w_o'], 'L0_attn_b_o': _L0_attn_in['b_o'], 'L0_ffn_W_Q': _L0_ffn_in['W_Q'], 'L0_ffn_W_K': _L0_ffn_in['W_K'], 'L0_ffn_W_O': _L0_ffn_in['W_O'], 'L0_ffn_W_inv': _L0_ffn_in['W_inv'], 'L0_ffn_V_fwd': _L0_ffn_in['V_fwd'], 'L0_ffn_W_fwd': _L0_ffn_in['W_fwd'], 'L0_ffn_U_fwd': _L0_ffn_in['U_fwd'], 'L0_ffn_b_fwd': _L0_ffn_in['b_fwd'], 'L0_ffn_V_inv': _L0_ffn_in['V_inv'], 'L0_ffn_W_inv_exp': _L0_ffn_in['W_inv_exp'], 'L0_ffn_U_inv': _L0_ffn_in['U_inv'], 'L0_ffn_b_inv': _L0_ffn_in['b_inv'], 'L0_ffn_router_w1': _L0_ffn_in['router_w1'], 'L0_ffn_router_b1': _L0_ffn_in['router_b1'], 'L0_ffn_router_w2': _L0_ffn_in['router_w2'], 'L0_ffn_router_b2': _L0_ffn_in['router_b2'], 'L0_ffn_alpha_bi': _L0_ffn_in['alpha_bi'], 'L0_ffn_expert_bias': _L0_ffn_in['expert_bias'], 'L1_attn_w_qkv': _L1_attn_in['w_qkv'], 'L1_attn_b_qkv': _L1_attn_in['b_qkv'], 'L1_attn_w_out': _L1_attn_in['w_out'], 'L1_attn_b_out': _L1_attn_in['b_out'], 'L1_ffn_weight': _L1_ffn_in['weight'], 'L1_ffn_gate_w': _L1_ffn_in['gate_w'], 'L1_ffn_lora_U': _L1_ffn_in['lora_U'], 'L1_ffn_lora_V': _L1_ffn_in['lora_V']}
    _x0 = _d['L0_attn_x']
    _d['L0_attn_x'] = jax.random.normal(jax.random.fold_in(jax.random.key(seed), 1), (2, 2048, 256), dtype=_x0.dtype)
    del _x0
    return _d

def reference(L0_attn_x, L0_attn_w_qkv, L0_attn_b_qkv, L0_attn_w_o, L0_attn_b_o, L0_ffn_W_Q, L0_ffn_W_K, L0_ffn_W_O, L0_ffn_W_inv, L0_ffn_V_fwd, L0_ffn_W_fwd, L0_ffn_U_fwd, L0_ffn_b_fwd, L0_ffn_V_inv, L0_ffn_W_inv_exp, L0_ffn_U_inv, L0_ffn_b_inv, L0_ffn_router_w1, L0_ffn_router_b1, L0_ffn_router_w2, L0_ffn_router_b2, L0_ffn_alpha_bi, L0_ffn_expert_bias, L1_attn_w_qkv, L1_attn_b_qkv, L1_attn_w_out, L1_attn_b_out, L1_ffn_weight, L1_ffn_gate_w, L1_ffn_lora_U, L1_ffn_lora_V):

    def _L0_attn_ref(x, w_qkv, b_qkv, w_o, b_o):
        import jax, jax.numpy as jnp
        import numpy as np
        B, L, D, H = (2, 512, 256, 16)
        C = D // H
        SCALE = 1.0 / np.sqrt(D).astype(np.float32)
        b, l, d = x.shape
        h, c = (H, d // H)
        qkv = jnp.einsum('bld,ed->ble', x, w_qkv) + b_qkv
        q, k, v = jnp.split(qkv, 3, axis=-1)
        q = q.reshape(b, l, h, c)
        k = k.reshape(b, l, h, c)
        v = v.reshape(b, l, h, c)
        attn = jax.nn.softmax(jnp.einsum('blhc,bmhc->bhlm', q, k) * SCALE, axis=-1)
        heads = jnp.einsum('bhlm,bmhc->blhc', attn, v).reshape(b, l, d)
        return jnp.einsum('bld,ed->ble', heads, w_o) + b_o + x

    def _L0_ffn_ref(x, W_Q, W_K, W_O, W_inv, V_fwd, W_fwd, U_fwd, b_fwd, V_inv, W_inv_exp, U_inv, b_inv, router_w1, router_b1, router_w2, router_b2, alpha_bi, expert_bias):
        import jax, jax.numpy as jnp
        import numpy as np
        B, T, D, R, KEXP = (4, 1024, 256, 64, 8)
        RH = max(D, 32)
        SCALE = 0.02

        def _fused_branch(Q_side, K_side, V, W, U, b, router_w1, router_b1, router_w2, router_b2, expert_bias):
            xV = jnp.einsum('btd,kdr->btkr', Q_side, V)
            yW = jnp.einsum('btd,kdr->btkr', K_side, W)
            cum_yW = jnp.cumsum(yW, axis=1)
            prod = xV * cum_yW
            h = jax.nn.gelu(Q_side @ router_w1.T + router_b1, approximate=False)
            logits = h @ router_w2.T + router_b2 + expert_bias
            weights = jax.nn.softmax(logits, axis=-1)
            out = jnp.einsum('btkr,kdr->btd', prod * weights[..., None], U)
            out = out + weights @ b
            n_valid = jnp.arange(1, Q_side.shape[1] + 1, dtype=Q_side.dtype)
            return out / n_valid[None, :, None]
        Q = x @ W_Q.T
        K = x @ W_K.T
        invQ = Q @ W_inv.T
        invK = K @ W_inv.T
        fwd = _fused_branch(Q, K, V_fwd, W_fwd, U_fwd, b_fwd, router_w1, router_b1, router_w2, router_b2, expert_bias)
        inv = _fused_branch(invQ, invK, W_inv_exp, V_inv, U_inv, b_inv, router_w1, router_b1, router_w2, router_b2, expert_bias)
        out = fwd + alpha_bi * inv
        return out @ W_O.T

    def _L1_attn_ref(x, w_qkv, b_qkv, w_out, b_out):
        import jax, jax.numpy as jnp
        import numpy as np
        B, S, D = (2, 512, 256)
        H = 16
        HD = D // H
        WINDOW = 128
        SCALE = HD ** (-0.5)

        def _local_mask(seq_len):
            idx = jnp.arange(seq_len)
            band = jnp.abs(idx[:, None] - idx[None, :]) <= WINDOW // 2
            return jnp.where(band, 0.0, -jnp.inf).astype(jnp.float32)
        b, s, _ = x.shape
        qkv = x @ w_qkv + b_qkv
        qkv = qkv.reshape(b, s, 3, H, HD).transpose(2, 0, 3, 1, 4)
        q, k, v = (qkv[0], qkv[1], qkv[2])
        mask = _local_mask(s)
        scores = jnp.einsum('bhqd,bhkd->bhqk', q, k) * SCALE + mask
        attn = jax.nn.softmax(scores, axis=-1)
        out = jnp.einsum('bhqk,bhkd->bhqd', attn, v)
        out = out.transpose(0, 2, 1, 3).reshape(b, s, D)
        return out @ w_out + b_out

    def _L1_ffn_ref(x, weight, gate_w, lora_U, lora_V):
        import jax, jax.numpy as jnp
        import numpy as np
        scaling = 1.0 / lora_U.shape[1]
        B, S, D_in = x.shape
        xt = x.reshape(-1, D_in)
        gate = jax.nn.softmax(xt @ gate_w.T, axis=-1)
        base = xt @ weight.T
        t = jnp.einsum('nh,erh->ner', xt, lora_U)
        lora = jnp.einsum('ne,eor,ner->no', gate, lora_V, t)
        out = base + scaling * lora
        return out.reshape(B, S, -1)
    x = L0_attn_x
    xn = _layernorm(x, axis=-1)
    s = _L0_attn_ref(xn, L0_attn_w_qkv, L0_attn_b_qkv, L0_attn_w_o, L0_attn_b_o)
    g = _silu(_L0_ffn_ref(xn, L0_ffn_W_Q, L0_ffn_W_K, L0_ffn_W_O, L0_ffn_W_inv, L0_ffn_V_fwd, L0_ffn_W_fwd, L0_ffn_U_fwd, L0_ffn_b_fwd, L0_ffn_V_inv, L0_ffn_W_inv_exp, L0_ffn_U_inv, L0_ffn_b_inv, L0_ffn_router_w1, L0_ffn_router_b1, L0_ffn_router_w2, L0_ffn_router_b2, L0_ffn_alpha_bi, L0_ffn_expert_bias))
    x = x + s * g
    xn = _layernorm(x, axis=-1)
    s = _L1_attn_ref(xn, L1_attn_w_qkv, L1_attn_b_qkv, L1_attn_w_out, L1_attn_b_out)
    g = _silu(_L1_ffn_ref(xn, L1_ffn_weight, L1_ffn_gate_w, L1_ffn_lora_U, L1_ffn_lora_V))
    x = x + s * g
    return x

_drawn_inputs = setup_inputs


def setup_inputs(seed=0):
    import zlib

    import numpy as np

    out = dict(_drawn_inputs(seed))
    spreads = {'L0_ffn_b_fwd': (0.0, 0.1),
     'L0_ffn_b_inv': (0.0, 0.1),
     'L0_ffn_router_b1': (0.0, 0.1),
     'L0_ffn_router_b2': (0.0, 0.1),
     'L0_ffn_expert_bias': (0.0, 0.1)}
    factors = {}
    for name, (base, spread) in spreads.items():
        noise = np.random.default_rng([zlib.crc32(name.encode()), seed]).standard_normal(out[name].shape)
        drawn = base * np.exp(spread * noise) if base else spread * noise
        out[name] = jnp.asarray(drawn.astype(out[name].dtype))
    for name, factor in factors.items():
        out[name] = (out[name] * factor).astype(out[name].dtype)
    return out
```

```python
from contextlib import ExitStack

import concourse.bass as bass
from concourse import mybir

F32 = mybir.dt.float32
F32R = mybir.dt.float32r
BF16 = mybir.dt.bfloat16
I32 = mybir.dt.int32
ALU = mybir.AluOpType
ACT = mybir.ActivationFunctionType
AX = mybir.AxisListType

P = 128
B, T, D, H = 2, 2048, 256, 16
C = D // H
DK = D // P
CH = 512
NCH = T // CH
TT = CH // P
KT = T // P
E, R = 8, 64
KR = E * R
E1, R1 = 8, 16
G = 4
NG = B * H // G
VW = 32
REACH = 64
WIN = P + 2 * REACH
TP = T + 2 * P
EPS = 1e-5
NEG = -1e30
ROWS = 6 * C
ROW_PAD = ROWS
ROW_M = ROWS + 1
NROWS = ROWS + 3
PART_ROWS = [(0, 0, 0), (C, 1, 0), (2 * C, 2, 0), (3 * C, 0, 1), (4 * C, 1, 1), (5 * C, 0, 2)]
DMA = 16

ds = bass.ds


def wait_apart(eng, sem, value, passed):
    eng.wait_ge(sem, value)
    eng.sem_inc(passed, 1)


def f32(ap):
    return ap.bitcast(F32)


def split_matmul(nc, out, stationary, moving, n_k, start, stop):
    last = None
    passes = [(k, s, m) for k in range(n_k) for s, m in ((0, 0), (0, 1), (1, 0))]
    for n, (k, s, m) in enumerate(passes):
        last = nc.tensor.matmul(out, stationary(s, k), moving(m, k), start=start and n == 0,
                                stop=stop and n == len(passes) - 1, skip_group_check=True)
    return last


class Names:

    def __init__(self, nc, ctx, tag):
        self.nc, self.ctx, self.tag = nc, ctx, tag
        self.sems = []
        ctx.callback(self.release)

    def release(self):
        if self.sems:
            self.nc.clear_and_free_semaphores(self.sems)
            self.nc.all_engine_barrier()

    def sb(self, name, shape, dt=F32):
        return self.ctx.enter_context(self.nc.sbuf_tensor(f"{self.tag}_{name}", shape, dt))

    def ps(self, name, cols):
        return self.ctx.enter_context(self.nc.psum_tensor(f"{self.tag}_{name}", [P, cols], F32))

    def sem(self, name):
        sem = self.nc.alloc_semaphore(name=f"{self.tag}_{name}")
        self.sems.append(sem)
        return sem



def phase_weights(nc, W, I):
    with ExitStack() as ctx:
        n = Names(nc, ctx, "w")
        square = {k: n.sb(k, [P, DK, D]) for k in ("WQ", "WK", "WinvT", "W1T", "WOT", "WIQ", "WIK")}
        wide = {k: n.sb(k, [P, DK, KR]) for k in ("Vf", "Wf", "Vi", "Wi", "Uf", "Ui")}
        bT = n.sb("bT", [P, DK, 2 * E])
        raw_qkv = n.sb("raw_qkv", [P, 2, DK, 3 * D])
        raw_o = n.sb("raw_o", [P, 2, DK, D])
        raw_g = n.sb("raw_g", [P, DK, E1 + E1 * R1 + D])
        raw_v = n.sb("raw_v", [P, 1, D])
        pos = n.sb("pos", [P, KT], I32)
        posf = n.sb("posf", [P, KT])
        lb = n.sb("lb", [64, 2])
        bank = n.ps("bank", 8 * CH)
        loaded = n.sem("loaded")
        drawn = n.sem("drawn")
        product = n.sem("product")
        high = n.sem("high")
        low = n.sem("low")
        step = n.sem("step")

        loads = [(square["WQ"][:], I["W_Q"], DK), (square["WK"][:], I["W_K"], DK),
                 (square["WinvT"][:], I["W_invT"], DK), (square["W1T"][:], I["router_w1T"], DK),
                 (square["WOT"][:], I["W_OT"], DK),
                 (wide["Vf"][:], I["V_fwd"], DK), (wide["Wf"][:], I["W_fwd"], DK),
                 (wide["Vi"][:], I["W_inv_exp"], DK), (wide["Wi"][:], I["V_inv"], DK),
                 (wide["Uf"][:], I["U_fwd"], DK), (wide["Ui"][:], I["U_inv"], DK),
                 (bT[:, :, 0:E], I["b_fwdT"], DK), (bT[:, :, E:2 * E], I["b_invT"], DK),
                 (raw_qkv[:, 0], I["w_qkvT_0"], DK), (raw_qkv[:, 1], I["w_qkv_1"], DK),
                 (raw_o[:, 0], I["w_oT_0"], DK), (raw_o[:, 1], I["w_out_1"], DK),
                 (raw_g[:, :, 0:E1], I["gateT"], DK),
                 (raw_g[:, :, E1:E1 + E1 * R1], I["lora_UT"], DK),
                 (raw_g[:, :, E1 + E1 * R1:], I["weightT"], DK),
                 (raw_v[:], I["lora_V"], 1),
                 (W["w2"][:], I["router_w2T"], DK)]
        rows = [(W["bqk"][:, l, :], I["b_qkv"][l][0:2 * D].rearrange("(m p) -> p m", p=P)) for l in (0, 1)]
        rows += [(W["bv"][:, l, :], I["b_qkv"][l][2 * D:3 * D].unsqueeze(0).broadcast_to([P, D])) for l in (0, 1)]
        rows += [(W["bo"][:, l, :], I["b_o"][l].unsqueeze(0).broadcast_to([P, D])) for l in (0, 1)]
        rows += [(W["b1"][:], I["router_b1"].rearrange("(m p) -> p m", p=P))]
        rows += [(W["alpha"][:], I["alpha"].unsqueeze(0).broadcast_to([P, 1]))]
        rows += [(lb[32 * r:32 * r + E, j:j + 1], I[k].rearrange("(p o) -> p o", o=1))
                 for r in (0, 1) for j, k in enumerate(("router_b2", "expert_bias"))]
        n_loads = len(loads) + len(rows)

        WQ, WK, WIQ, WIK = (square[k] for k in ("WQ", "WK", "WIQ", "WIK"))

        block = ctx.enter_context(nc.Block())

        @block.sync
        def _(sp):
            for dst, src, k in loads:
                sp.dma_start(dst, src.rearrange("(k p) n -> p k n", p=P)).then_inc(loaded, DMA)

        @block.scalar
        def _(act):
            with nc.allow_non_contiguous_dma("biases, a few hundred bytes"):
                for dst, src in rows:
                    act.dma_start(dst, src).then_inc(loaded, DMA)
            for m, dst in ((0, WIQ), (1, WIK)):
                act.wait_ge(product, m + 1)
                nc.scalar.activation(dst[:].rearrange("p k n -> p (k n)"), bank[:, m * CH:(m + 1) * CH],
                                     ACT.Copy).then_inc(high, 1)
            for j in range(N_SPLIT):
                act.wait_ge(product, 3 + j)
                dst = split_target(W, j)
                nc.scalar.activation(dst(0), bank[:, (2 + j % 6) * CH:(3 + j % 6) * CH],
                                     ACT.Copy).then_inc(high, 1)
            act.wait_ge(product, 3 + N_SPLIT)
            nc.scalar.activation(W["bO"][:], bank[0:2 * E, 0:D], ACT.Copy).then_inc(high, 1)
            act.wait_ge(loaded, DMA * n_loads)
            for dst, src in plain_splits(W, raw_qkv, raw_o, raw_g, raw_v):
                nc.scalar.activation(dst(0), src, ACT.Copy).then_inc(high, 1)

        @block.tensor
        def _(pe):
            pe.wait_ge(loaded, DMA * n_loads)
            for m, src in ((0, WQ), (1, WK)):
                for t in range(DK):
                    for k in range(DK):
                        last = nc.tensor.matmul(bank[:, m * CH + t * D:m * CH + (t + 1) * D],
                                                square["WinvT"][:, k, t * P:(t + 1) * P], src[:, k, :],
                                                start=(k == 0), stop=(k == DK - 1), skip_group_check=True)
                last.then_inc(product, 1)
            pe.wait_ge(high, 2)
            j = 0
            for left, right in ((WQ, "Vf"), (WIQ, "Vi"), (WK, "Wf"), (WIK, "Wi")):
                for t in range(DK):
                    if j >= 6:
                        pe.wait_ge(low, j - 5)
                    for k in range(DK):
                        last = nc.tensor.matmul(bank[:, (2 + j % 6) * CH:(3 + j % 6) * CH],
                                                left[:, k, t * P:(t + 1) * P], wide[right][:, k, :],
                                                start=(k == 0), stop=(k == DK - 1))
                    last.then_inc(product, 1)
                    j += 1
            for t in range(DK):
                pe.wait_ge(low, j - 5)
                for r, left in enumerate((WQ, WIQ)):
                    for k in range(DK):
                        o = (2 + j % 6) * CH + r * D
                        last = nc.tensor.matmul(bank[:, o:o + D], left[:, k, t * P:(t + 1) * P],
                                                square["W1T"][:, k, :], start=(k == 0),
                                                stop=(k == DK - 1), skip_group_check=True)
                last.then_inc(product, 1)
                j += 1
            for half in range(4):
                u = wide["Uf" if half < 2 else "Ui"]
                pe.wait_ge(low, j - 5)
                for r in range(2):
                    m = 2 * (half % 2) + r
                    for k in range(DK):
                        o = (2 + j % 6) * CH + r * D
                        last = nc.tensor.matmul(bank[:, o:o + D], u[:, k, m * P:(m + 1) * P],
                                                square["WOT"][:, k, :], start=(k == 0),
                                                stop=(k == DK - 1), skip_group_check=True)
                last.then_inc(product, 1)
                j += 1
            for k in range(DK):
                last = nc.tensor.matmul(bank[0:2 * E, 0:D], bT[:, k, :], square["WOT"][:, k, :],
                                        start=(k == 0), stop=(k == DK - 1))
            last.then_inc(product, 1)

        @block.vector
        def _(dve):
            for j in range(N_SPLIT):
                dve.wait_ge(high, 3 + j)
                dst = split_target(W, j)
                nc.vector.tensor_tensor(dst(1), bank[:, (2 + j % 6) * CH:(3 + j % 6) * CH], f32(dst(0)),
                                        ALU.subtract).then_inc(low, 1)
            for i, (dst, src) in enumerate(plain_splits(W, raw_qkv, raw_o, raw_g, raw_v)):
                dve.wait_ge(high, 4 + N_SPLIT + i)
                nc.vector.tensor_tensor(dst(1), src, f32(dst(0)), ALU.subtract).then_inc(low, 1)
            dve.wait_ge(drawn, N_DRAWN)
            nc.vector.tensor_copy(posf[:], pos[:]).then_inc(step, 1)
            nc.vector.tensor_copy(W["mask_bf"][:], W["mask"][:]).then_inc(step, 1)
            for r in (0, 1):
                nc.vector.tensor_tensor(W["b2"][32 * r:32 * r + E, :], lb[32 * r:32 * r + E, 0:1],
                                        lb[32 * r:32 * r + E, 1:2], ALU.add).then_inc(step, 1)
            nc.vector.tensor_copy(W["ident_bf"][:], W["ident"][:]).then_inc(step, 1)
            dve.wait_ge(step, 1)
            nc.vector.reciprocal(W["inv_n"][:], posf[:]).then_inc(step, 1)

        @block.gpsimd
        def _(pool):
            pool.memset(W["ident"][:], 0.0).then_inc(drawn, 1)
            pool.memset(W["mask"][:], 0.0).then_inc(drawn, 1)
            pool.memset(W["ones"][:], 1.0).then_inc(drawn, 1)
            pool.memset(W["half"][:], -0.5).then_inc(drawn, 1)
            pool.iota(pos[:], [[P, KT]], base=1, channel_multiplier=1).then_inc(drawn, 1)
            pool.wait_ge(drawn, 5)
            pool.affine_select(out=W["ident"][:], in_=W["ident"][:], compare_op=ALU.not_equal, fill=1.0,
                               base=0, pattern=[[-1, P]], channel_multiplier=1).then_inc(drawn, 1)
            pool.affine_select(out=W["mask"][:], in_=W["mask"][:], compare_op=ALU.is_ge, fill=NEG,
                               base=0, pattern=[[1, WIN]], channel_multiplier=-1).then_inc(drawn, 1)
            pool.wait_ge(drawn, 7)
            pool.affine_select(out=W["mask"][:], in_=W["mask"][:], compare_op=ALU.is_ge, fill=NEG,
                               base=2 * REACH, pattern=[[-1, WIN]], channel_multiplier=1).then_inc(drawn, 1)


N_DRAWN = 8
N_SPLIT = 14


def split_target(W, j):
    if j < 8:
        name, branch, t = ("AQ" if j < 4 else "BK"), (j // 2) % 2, j % 2
        return lambda part: W[name][:, part, t, branch * KR:(branch + 1) * KR]
    if j < 10:
        return lambda part: W["RT"][:, part, j - 8, :]
    m = 2 * (j - 10)
    return lambda part: W["UO"][:, part, m:m + 2, :].rearrange("p m n -> p (m n)")


def plain_splits(W, raw_qkv, raw_o, raw_g, raw_v):
    out = []
    for l in (0, 1):
        out.append((lambda part, l=l: W[f"qkv{l}"][:, part], raw_qkv[:, l]))
        out.append((lambda part, l=l: W[f"o{l}"][:, part], raw_o[:, l]))
    out.append((lambda part: W["gate"][:, part], raw_g[:]))
    out.append((lambda part: W["loraV"][:, part], raw_v[:]))
    return out



def phase_project(nc, W, S, x_dram, layer):
    first = layer == 0
    with ExitStack() as ctx:
        n = Names(nc, ctx, f"p{layer}")
        stats = n.sb("stats", [P, 2, TT, 6])
        mean_var = n.sb("mean_var", [P, 2, TT, 2])
        var_eps = n.sb("var_eps", [P, 2, TT])
        rstd = n.sb("rstd", [P, 2, TT])
        xn = n.sb("xn", [P, 2, TT, D])
        xT = n.sb("xT", [P, 2, 2, DK, CH], F32R)
        cum = n.sb("cum", [P, DK, CH])
        carry = n.sb("carry", [P, 2, DK])
        cT = n.sb("cT", [P, 2, 2, DK, CH], F32R) if first else None
        parts = n.sb("parts", [P, 4, 3, CH], BF16)
        rest = n.sb("rest", [P, 2, CH])
        v_out = n.sb("v_out", [P, 2, TT, H, VW])
        gelu = n.sb("gelu", [P, 2, DK, CH]) if first else None
        logT = n.sb("logT", [64, CH]) if first else None
        ps_t = n.ps("ps_t", DK * CH)
        ps_qk = n.ps("ps_qk", 2 * CH)
        ps_v = n.ps("ps_v", CH)
        ps_h = n.ps("ps_h", 2 * CH)
        ps_l = n.ps("ps_l", CH)

        x_loaded = [n.sem(f"x_loaded{u}") for u in range(2)]
        stat = n.sem("stat")
        eps_ready = n.sem("eps_ready")
        rstd_ready = n.sem("rstd_ready")
        xn_ready = n.sem("xn_ready")
        t_ready = n.sem("t_ready")
        t_high = n.sem("t_high")
        t_low = n.sem("t_low")
        cum_done = n.sem("cum_done")
        carry_done = n.sem("carry_done")
        c_high = n.sem("c_high")
        c_low = n.sem("c_low")
        qk_ready = n.sem("qk_ready")
        part1 = n.sem("part1")
        rest_ready = n.sem("rest_ready")
        part2 = n.sem("part2")
        part3 = n.sem("part3")
        v_ready = n.sem("v_ready")
        v_done = n.sem("v_done")
        v_clear = n.sem("v_clear")
        h_ready = n.sem("h_ready")
        gelu_done = n.sem("gelu_done")
        log_ready = n.sem("log_ready")
        logT_clear = n.sem("logT_clear")
        logT_done = n.sem("logT_done")
        lt_ready = n.sem("lt_ready")
        log_done = n.sem("log_done")
        xn_stored = [n.sem(f"xn_stored{u}") for u in range(2)]
        passed = n.sem("passed")
        stored = [n.sem(f"stored{u}") for u in range(2)]
        parts_stored = [n.sem(f"parts_stored{m}") for m in range(4)]
        chunk_stores = DMA * (TT + 2 * DK * (2 if first else 1))
        t_read = cum_done if first else t_low
        t_low_seed, cum_seed = (0, DK) if first else (DK, 0)

        block = ctx.enter_context(nc.Block())

        def load(sp, i, u):
            c = 2 * i + u
            if not isinstance(c, int) or c > 1:
                wait_apart(sp, t_ready, c - 1, passed)
                if first:
                    wait_apart(sp, xn_stored[u], DMA * i, passed)
            sp.dma_start(xn[:, u], x_dram[u, ds(i * CH, CH), :].rearrange("(t p) d -> p t d", p=P)
                         ).then_inc(x_loaded[u], DMA)

        def store_xn(sp, i):
            for u in range(2 if first else 0):
                wait_apart(sp, xn_ready, TT * (2 * i + u + 1), passed)
                sp.dma_start(S["xn"][u, ds(i * CH, CH), :].rearrange("(t p) d -> p t d", p=P), xn[:, u]
                             ).then_inc(xn_stored[u], DMA)

        def store(sp, i, u):
            c = 2 * i + u
            tok = ds(i * CH, CH)
            wait_apart(sp, t_low, t_low_seed + DK * (c + 1), passed)
            for part in range(2):
                for k in range(DK):
                    sp.dma_start(S["xT"][u, part, k, :, tok], f32(xT[:, u, part, k, :])
                                 ).then_inc(stored[u], DMA)
            if first:
                wait_apart(sp, c_low, DK * (c + 1), passed)
                for part in range(2):
                    for k in range(DK):
                        sp.dma_start(S["cT"][u, part, k, :, tok], f32(cT[:, u, part, k, :])
                                     ).then_inc(stored[u], DMA)
            for m in range(4):
                wait_apart(sp, part3, 2 + 4 * c + m + 1, passed)
                sp.dma_start(S["parts"][m // 2, u, :, (m % 2) * P:(m % 2 + 1) * P, tok].rearrange("a p t -> p a t"),
                             parts[:, m]).then_inc(parts_stored[m], DMA)
            wait_apart(sp, v_done, 1 + 2 * (c + 1), passed)
            for t in range(TT):
                sp.dma_start(S["v"][u, :, :, ds(i * TT + t, 1), :].rearrange("g p o n -> p g (o n)"),
                             v_out[:, u, t].rearrange("p (g h) w -> p g (h w)", g=H // G)
                             ).then_inc(stored[u], DMA)

        @block.sync
        def _(sp):
            for u in range(2):
                sp.sem_inc(stored[u], chunk_stores)
            for m in range(4):
                sp.sem_inc(parts_stored[m], DMA)
            load(sp, 0, 0)
            load(sp, 0, 1)
            with sp.Fori(0, NCH - 1) as i:
                store_xn(sp, i)
                load(sp, i + 1, 0)
                load(sp, i + 1, 1)
                store(sp, i, 0)
                store(sp, i, 1)
            store_xn(sp, NCH - 1)
            store(sp, NCH - 1, 0)
            store(sp, NCH - 1, 1)
            for u in range(2):
                wait_apart(sp, stored[u], chunk_stores * (NCH + 1), passed)
                if first:
                    wait_apart(sp, xn_stored[u], DMA * NCH, passed)
            for m in range(4):
                wait_apart(sp, parts_stored[m], DMA * (2 * NCH + 1), passed)

        @block.gpsimd
        def _(pool):
            def third_parts(i, u):
                for m in range(4):
                    pool.wait_ge(part2, 4 * (2 * i + u) + m + 1)
                    pool.tensor_tensor(parts[:, m, 2, :], rest[:, m % 2, :], parts[:, m, 1, :],
                                       ALU.subtract).then_inc(part3, 1)

            def inverse_root(c, u):
                pool.wait_ge(eps_ready, c + 1)
                pool.tensor_tensor(rstd[:, u], var_eps[:, u], W["half"][:, 0:TT], ALU.pow
                                   ).then_inc(rstd_ready, 1)

            pool.sem_inc(part3, 2)
            inverse_root(0, 0)
            inverse_root(1, 1)
            with pool.Fori(0, NCH - 1) as i:
                third_parts(i, 0)
                third_parts(i, 1)
                inverse_root(2 * i + 2, 0)
                inverse_root(2 * i + 3, 1)
            third_parts(NCH - 1, 0)
            third_parts(NCH - 1, 1)

        @block.vector
        def _(dve):
            def statistics(i, u):
                c = 2 * i + u
                dve.wait_ge(x_loaded[u], DMA * (i + 1))
                for t in range(TT):
                    nc.vector.bn_stats(stats[:, u, t], xn[:, u, t]).then_inc(stat, 1)
                wait_apart(dve, stat, (TT + 1) * c + TT, passed)
                for t in range(TT):
                    last = nc.vector.bn_aggr(mean_var[:, u, t], stats[:, u, t])
                last.then_inc(stat, 1)
                dve.wait_ge(stat, (TT + 1) * (c + 1))
                nc.vector.tensor_scalar(var_eps[:, u], mean_var[:, u, :, 1], EPS, None, ALU.add
                                        ).then_inc(eps_ready, 1)

            def normalise(i, u):
                c = 2 * i + u
                dve.wait_ge(rstd_ready, c + 1)
                for t in range(TT):
                    nc.vector.tensor_scalar(xn[:, u, t], xn[:, u, t], mean_var[:, u, t, 0:1],
                                            rstd[:, u, t:t + 1], ALU.subtract, ALU.mult).then_inc(xn_ready, 1)

            def transposed(i, u):
                c = 2 * i + u
                if first:
                    dve.wait_ge(carry_done, c + 1)
                for k in range(DK):
                    dve.wait_ge(t_high, DK * c + k + 1)
                    nc.vector.tensor_tensor(xT[:, u, 1, k, :], ps_t[:, k * CH:(k + 1) * CH],
                                            f32(xT[:, u, 0, k, :]), ALU.subtract).then_inc(t_low, 1)
                    if first:
                        nc.vector.tensor_tensor_scan(cum[:, k, :], W["ones"][:, 0:CH],
                                                     ps_t[:, k * CH:(k + 1) * CH], carry[:, u, k:k + 1],
                                                     ALU.mult, ALU.add).then_inc(cum_done, 1)
                if first:
                    dve.wait_ge(cum_done, cum_seed + DK * (c + 1))
                    nc.vector.tensor_copy(carry[:, u, :], cum[:, :, CH - 1]).then_inc(carry_done, 1)
                    for k in range(DK):
                        dve.wait_ge(c_high, DK * c + k + 1)
                        nc.vector.tensor_tensor(cT[:, u, 1, k, :], cum[:, k, :], f32(cT[:, u, 0, k, :]),
                                                ALU.subtract).then_inc(c_low, 1)

            def rests(i, u):
                for m in range(4):
                    j = 4 * (2 * i + u) + m
                    dve.wait_ge(part1, j + 1)
                    dve.wait_ge(part3, j + 1)
                    nc.vector.scalar_tensor_tensor(rest[:, m % 2, :], ps_qk[:, (m % 2) * CH:(m % 2 + 1) * CH],
                                                   W["bqk"][:, layer, m:m + 1], parts[:, m, 0, :],
                                                   ALU.add, ALU.subtract).then_inc(rest_ready, 1)

            def values(i, u):
                for half in range(2):
                    dve.wait_ge(v_ready, 2 * (2 * i + u) + half + 1)
                    nc.vector.tensor_tensor(
                        v_out[:, u, 2 * half:2 * half + 2, :, 0:C],
                        ps_v[:].rearrange("p (t h c) -> p t h c", t=2, c=C),
                        W["bv"][:, layer].rearrange("p (h c) -> p h c", c=C).unsqueeze(1)
                        .broadcast_to([P, 2, H, C]), ALU.add).then_inc(v_done, 1)

            def logits(i, u):
                c = 2 * i + u
                dve.wait_ge(lt_ready, 1 + c + 1)
                for r in range(2):
                    last = nc.vector.tensor_copy(
                        W["logits"][:, u, ds(i * TT, TT), r, :],
                        ps_l[:].rearrange("p (t n) -> p t n", t=TT)[:, :, 32 * r:32 * r + E])
                last.then_inc(log_done, 1)

            def chunk_pair(i, more):
                transposed(i, 0)
                rests(i, 0)
                values(i, 0)
                transposed(i, 1)
                if first:
                    logits(i, 0)
                rests(i, 1)
                if more:
                    statistics(i + 1, 0)
                    statistics(i + 1, 1)
                values(i, 1)
                if more:
                    normalise(i + 1, 0)
                    normalise(i + 1, 1)
                if first:
                    logits(i, 1)

            dve.sem_inc(t_read, DK)
            dve.sem_inc(rest_ready, 2)
            dve.sem_inc(v_done, 1)
            dve.sem_inc(log_done, 1)
            nc.vector.memset(v_out[:], 1.0).then_inc(v_clear, 1)
            dve.wait_ge(v_clear, 1)
            if first:
                nc.vector.memset(carry[:], 0.0).then_inc(carry_done, 1)
            statistics(0, 0)
            statistics(0, 1)
            normalise(0, 0)
            normalise(0, 1)
            with dve.Fori(0, NCH - 1) as i:
                chunk_pair(i, True)
            chunk_pair(NCH - 1, False)

        @block.scalar
        def _(act):
            def chunk(i, u):
                c = 2 * i + u
                act.wait_ge(stored[u], chunk_stores * (i + 1))
                for k in range(DK):
                    act.wait_ge(t_ready, c + 1)
                    nc.scalar.activation(xT[:, u, 0, k, :], ps_t[:, k * CH:(k + 1) * CH], ACT.Copy
                                         ).then_inc(t_high, 1)
                if first:
                    for k in range(DK):
                        act.wait_ge(cum_done, cum_seed + DK * c + k + 1)
                        nc.scalar.activation(cT[:, u, 0, k, :], cum[:, k, :], ACT.Copy).then_inc(c_high, 1)
                for m in range(4):
                    j = 4 * c + m
                    act.wait_ge(qk_ready, j + 1)
                    act.wait_ge(parts_stored[m], DMA * (c + 1))
                    nc.scalar.activation(parts[:, m, 0, :], ps_qk[:, (m % 2) * CH:(m % 2 + 1) * CH],
                                         ACT.Identity, bias=W["bqk"][:, layer, m:m + 1]).then_inc(part1, 1)
                    act.wait_ge(rest_ready, 2 + j + 1)
                    nc.scalar.activation(parts[:, m, 1, :], rest[:, m % 2, :], ACT.Copy).then_inc(part2, 1)

            def router(i, u):
                c = 2 * i + u
                for r in range(2):
                    for m in range(DK):
                        act.wait_ge(h_ready, 4 * c + 2 * r + m + 1)
                        o = (m % 2) * CH
                        nc.scalar.activation(gelu[:, r, m, :], ps_h[:, o:o + CH], ACT.Gelu,
                                             bias=W["b1"][:, m:m + 1]).then_inc(gelu_done, 1)
                act.wait_ge(log_ready, c + 1)
                act.wait_ge(lt_ready, c + 1)
                for r in range(2):
                    last = nc.scalar.activation(logT[32 * r:32 * r + E, :], ps_l[32 * r:32 * r + E, :],
                                                ACT.Identity, bias=W["b2"][32 * r:32 * r + E, :])
                    last.then_inc(logT_done, 1)

            act.sem_inc(gelu_done, 2)
            if first:
                nc.scalar.activation(logT[:], W["ones"][0:64, 0:CH], ACT.Copy).then_inc(logT_clear, 1)
                act.wait_ge(logT_clear, 1)
            with act.Fori(0, NCH) as i:
                for u in range(2):
                    chunk(i, u)
                    if first:
                        router(i, u)

        @block.tensor
        def _(pe):
            def transposes(i, u):
                c = 2 * i + u
                pe.wait_ge(xn_ready, TT * (c + 1))
                pe.wait_ge(t_read, DK * (c + 1))
                for k in range(DK):
                    for t in range(TT):
                        last = nc.tensor.transpose(ps_t[:, k * CH + t * P:k * CH + (t + 1) * P],
                                                   xn[:, u, t, k * P:(k + 1) * P], W["ident"][:])
                last.then_inc(t_ready, 1)

            def qkv(i, u):
                c = 2 * i + u
                pe.wait_ge(t_low, t_low_seed + DK * (c + 1))
                w = W[f"qkv{layer}"]
                for m in range(4):
                    pe.wait_ge(rest_ready, 4 * c + m + 1)
                    split_matmul(nc, ps_qk[:, (m % 2) * CH:(m % 2 + 1) * CH],
                                 lambda s, k: w[:, s, k, m * P:(m + 1) * P],
                                 lambda s, k: xT[:, u, s, k, :], DK, True, True).then_inc(qk_ready, 1)
                for half in range(2):
                    pe.wait_ge(v_done, 2 * c + half + 1)
                    for t in range(2):
                        tok = (2 * half + t) * P
                        last = split_matmul(nc, ps_v[:, t * D:(t + 1) * D],
                                            lambda s, k: xT[:, u, s, k, tok:tok + P],
                                            lambda s, k: w[:, s, k, 2 * D:3 * D], DK, True, True)
                    last.then_inc(v_ready, 1)

            def router(i, u):
                c = 2 * i + u
                for r in range(2):
                    for m in range(DK):
                        pe.wait_ge(gelu_done, 4 * c + 2 * r + m + 1)
                        split_matmul(nc, ps_h[:, m * CH:(m + 1) * CH],
                                     lambda s, k: W["RT"][:, s, k, r * D + m * P:r * D + (m + 1) * P],
                                     lambda s, k: xT[:, u, s, k, :], DK, True, True).then_inc(h_ready, 1)
                pe.wait_ge(gelu_done, 2 + 4 * (c + 1))
                pe.wait_ge(log_done, c + 1)
                for m in range(DK):
                    for r in range(2):
                        last = nc.tensor.matmul(ps_l[32 * r:32 * r + E, :], W["w2"][:, m, :], gelu[:, r, m, :],
                                                start=(m == 0), stop=(m == DK - 1), skip_group_check=True)
                last.then_inc(log_ready, 1)
                wait_apart(pe, logT_done, 2 * (c + 1), passed)
                for t in range(TT):
                    last = nc.tensor.transpose(ps_l[:, t * P:t * P + 64], logT[:, t * P:(t + 1) * P],
                                               W["ident"][0:64, 0:64])
                last.then_inc(lt_ready, 1)

            pe.sem_inc(lt_ready, 1)
            with pe.Fori(0, NCH) as i:
                transposes(i, 0)
                qkv(i, 0)
                transposes(i, 1)
                if first:
                    router(i, 0)
                qkv(i, 1)
                if first:
                    router(i, 1)



def load_group(sp, K, Q, S, kq_loaded, g, par, k_cols, k_off):
    b, f0 = g // NG2, (g % NG2) * G * C
    for row, k_part, q_part in PART_ROWS:
        def rows_of(which, part, t0, n):
            return S["parts"][which, ds(b, 1), part, ds(f0, G * C), t0:t0 + n].rearrange(
                "o (h c) t -> c (o h) t", h=G)
        dst = K[row:row + C, ds(par * (G * k_cols), G * k_cols)].rearrange("c (h t) -> c h t", h=G)
        sp.dma_start(dst[:, :, k_off:k_off + T], rows_of(1, k_part, 0, T)).then_inc(kq_loaded, DMA)
        for qc in range(NCH):
            dst = Q[row:row + C, ds(par * (G * T) + qc * G * CH, G * CH)]
            sp.dma_start(dst.rearrange("c (h t) -> c h t", h=G), rows_of(0, q_part, qc * CH, CH)
                         ).then_inc(kq_loaded, DMA)


GROUP_LOADS = len(PART_ROWS) * (1 + NCH)
NG2 = NG // B
NIT = NG * NCH


def phase_attend_full(nc, W, S):
    scale = 1.0 / D ** 0.5
    NS = 2 * KT
    NA = G * TT * (T // CH)
    with ExitStack() as ctx:
        n = Names(nc, ctx, "a0")
        K = n.sb("K", [NROWS, 2 * G * T], BF16)
        Q = n.sb("Q", [NROWS, 2 * G * T], BF16)
        V = n.sb("V", [P, KT, G * VW])
        prob = n.sb("prob", [P, 4, 2 * CH])
        maxes = n.sb("maxes", [P, NA])
        neg_max = n.sb("neg_max", [P, G * TT])
        m_parts = n.sb("m_parts", [G * TT, 2, P], BF16)
        oT = n.sb("oT", [P, CH])
        recip = n.sb("recip", [P, TT, G])
        o_out = n.sb("o_out", [P, TT, G, C])
        ps_a = n.ps("ps_a", 2 * CH)
        ps_s = n.ps("ps_s", 4 * CH)
        ps_o = n.ps("ps_o", CH)
        ps_m = n.ps("ps_m", CH)

        passed = n.sem("passed")
        rows_set = n.sem("rows_set")
        kq_loaded = n.sem("kq_loaded")
        v_loaded = [n.sem(f"v_loaded{q}") for q in range(4)]
        a_ready = n.sem("a_ready")
        a_done = n.sem("a_done")
        nm_ready = n.sem("nm_ready")
        mT_ready = n.sem("mT_ready")
        m_high = n.sem("m_high")
        m_low = n.sem("m_low")
        m_loaded = n.sem("m_loaded")
        s_ready = n.sem("s_ready")
        exp_done = n.sem("exp_done")
        pv_done = n.sem("pv_done")
        oT_ready = n.sem("oT_ready")
        o_turned = n.sem("o_turned")
        o_recip = n.sem("o_recip")
        o_done = n.sem("o_done")
        o_stored = n.sem("o_stored")
        out_clear = n.sem("out_clear")

        block = ctx.enter_context(nc.Block())

        def load_v(sp, g, q):
            sp.dma_start(V[:, 4 * q:4 * q + 4, :],
                         S["v"][ds(g // NG2, 1), ds(g % NG2, 1), :, 4 * q:4 * q + 4, :]
                         .rearrange("a b p t n -> p (a b t) n")).then_inc(v_loaded[q], DMA)

        @block.sync
        def _(sp):
            load_group(sp, K, Q, S, kq_loaded, 0, 0, T, 0)
            for q in range(4):
                load_v(sp, 0, q)
            wait_apart(sp, kq_loaded, GROUP_LOADS * DMA, passed)
            load_group(sp, K, Q, S, kq_loaded, 1, 1, T, 0)

            def values(g):
                for q in range(4):
                    wait_apart(sp, pv_done, 2 + KT * (NCH * g - 1) + 4 * (q + 1), passed)
                    load_v(sp, g, q)

            with sp.Fori(1, NG - 1) as g:
                values(g)
                wait_apart(sp, kq_loaded, GROUP_LOADS * DMA * (g + 1), passed)
                load_group(sp, K, Q, S, kq_loaded, g + 1, (g + 1) % 2, T, 0)
            values(NG - 1)

        @block.gpsimd
        def _(pool):
            def store_maxima(c):
                pool.wait_ge(m_low, c + 1)
                for part in range(2):
                    pool.dma_start(Q[ROW_M + part:ROW_M + part + 1, ds((c % (2 * NCH)) * (G * CH), G * CH)],
                                   m_parts[:, part, :]).then_inc(m_loaded, DMA)

            def store_output(it):
                pool.wait_ge(o_done, 1 + it + 1)
                pool.dma_start(S["att"][ds(it, 1)].rearrange("o (a p) c -> p (o a) c", p=P),
                               o_out[:].rearrange("p a h c -> p a (h c)")).then_inc(o_stored, DMA)

            pool.memset(o_out[:], 1.0).then_inc(out_clear, 1)
            pool.wait_ge(out_clear, 1)
            pool.memset(K[ROW_PAD:NROWS, :], 1.0).then_inc(rows_set, 1)
            pool.wait_ge(rows_set, 1)
            pool.memset(Q[ROW_PAD:NROWS, :], 1.0).then_inc(rows_set, 1)
            pool.wait_ge(rows_set, 2)
            pool.memset(K[ROW_PAD:ROW_PAD + 1, :], 0.0).then_inc(rows_set, 1)
            pool.wait_ge(rows_set, 3)
            pool.dma_start(S["att"][0:1].rearrange("o (a p) c -> p (o a) c", p=P),
                           o_out[:].rearrange("p a h c -> p a (h c)")).then_inc(o_stored, DMA)
            store_maxima(0)
            with pool.Fori(0, NIT - 1) as it:
                store_maxima(it + 1)
                store_output(it)
            store_output(NIT - 1)
            store_output(NIT)
            pool.wait_ge(o_stored, DMA * (NIT + 2))

        @block.vector
        def _(dve):
            def split_maxima(c):
                dve.wait_ge(mT_ready, c + 1)
                if not isinstance(c, int) or c > 0:
                    dve.wait_ge(m_loaded, 2 * DMA * c)
                nc.vector.tensor_copy(m_parts[:, 0, :], ps_m[0:G * TT, 0:P]).then_inc(m_high, 1)
                dve.wait_ge(m_high, c + 1)
                nc.vector.tensor_tensor(m_parts[:, 1, :], ps_m[0:G * TT, 0:P], m_parts[:, 0, :],
                                        ALU.subtract).then_inc(m_low, 1)

            def maxima(c, lo, hi):
                if lo == 0 and (not isinstance(c, int) or c > 0):
                    dve.wait_ge(nm_ready, c)
                for k in range(lo, hi):
                    dve.wait_ge(a_ready, NA * c + k + 1)
                    nc.vector.tensor_reduce(maxes[:, k:k + 1], ps_a[:, (k % 2) * CH:(k % 2 + 1) * CH],
                                            AX.X, ALU.max).then_inc(a_done, 1)

            def whole_maxima(c):
                dve.wait_ge(a_done, 2 + NA * (c + 1))
                if not isinstance(c, int) or c > 0:
                    dve.wait_ge(mT_ready, c)
                nc.vector.tensor_reduce(neg_max[:], maxes[:].rearrange("p (q k) -> p q k", k=T // CH),
                                        AX.X, ALU.max, negate=True).then_inc(nm_ready, 1)

            def normalise(it):
                dve.wait_ge(o_turned, it + 1)
                turned = ps_m[:].rearrange("p (a h w) -> p a h w", a=TT, h=G)
                nc.vector.reciprocal(recip[:], turned[:, :, :, C]).then_inc(o_recip, 1)
                dve.wait_ge(o_recip, it + 1)
                dve.wait_ge(o_stored, DMA * (it + 1))
                nc.vector.tensor_tensor(o_out[:], turned[:, :, :, 0:C],
                                        recip[:].unsqueeze(3).broadcast_to([P, TT, G, C]), ALU.mult
                                        ).then_inc(o_done, 1)

            dve.sem_inc(a_done, 2)
            dve.sem_inc(o_done, 1)
            maxima(0, 0, NA)
            whole_maxima(0)
            split_maxima(0)
            maxima(1, 0, NA)
            whole_maxima(1)
            with dve.Fori(0, NIT - 2) as it:
                maxima(it + 2, 0, 4)
                split_maxima(it + 1)
                maxima(it + 2, 4, 16)
                normalise(it)
                maxima(it + 2, 16, NA)
                whole_maxima(it + 2)
            split_maxima(NIT - 1)
            for it in (NIT - 2, NIT - 1, NIT):
                normalise(it)

        @block.scalar
        def _(act):
            def iteration(it):
                for j in range(NS):
                    act.wait_ge(s_ready, NS * it + j + 1)
                    if j % 2 == 0:
                        act.wait_ge(pv_done, KT * it + j // 2 + 1)
                    nc.scalar.activation(prob[:, j % 4, :], ps_s[:, (j % 2) * 2 * CH:(j % 2 + 1) * 2 * CH],
                                         ACT.Exp, scale=scale).then_inc(exp_done, 1)
                act.wait_ge(pv_done, 2 + KT * (it + 1))
                act.wait_ge(o_turned, it + 1)
                nc.scalar.activation(oT[:], ps_o[:], ACT.Copy).then_inc(oT_ready, 1)

            act.sem_inc(exp_done, 2)
            nc.scalar.activation(oT[:], W["ones"][:], ACT.Copy).then_inc(oT_ready, 1)
            with act.Fori(0, NIT) as it:
                iteration(it)

        @block.tensor
        def _(pe):
            def maximum_scores(c, k):
                h, qt, kc = k // (TT * NCH), (k // NCH) % TT, k % NCH
                half = ((c // NCH) % 2) * (G * T)
                q0 = (c % (2 * NCH)) * (G * CH) + h * CH + qt * P
                k0 = half + h * T + kc * CH
                pe.wait_ge(a_done, NA * c + k + 1)
                nc.tensor.matmul(ps_a[:, (k % 2) * CH:(k % 2 + 1) * CH], Q[0:ROW_M, ds(q0, P)],
                                 K[0:ROW_M, ds(k0, CH)], start=True, stop=True).then_inc(a_ready, 1)

            def turn_maxima(c):
                pe.wait_ge(nm_ready, c + 1)
                if not isinstance(c, int) or c > 0:
                    pe.wait_ge(m_low, c)
                    pe.wait_ge(o_done, c)
                nc.tensor.transpose(ps_m[0:G * TT, 0:P], neg_max[:], W["ident"][:]).then_inc(mT_ready, 1)

            def turn_output(it, m_users):
                pe.wait_ge(oT_ready, it + 1)
                pe.wait_ge(m_low, m_users)
                pe.wait_ge(o_done, it + 1)
                for a in range(TT):
                    last = nc.tensor.transpose(ps_m[:, a * P:(a + 1) * P], oT[:, a * P:(a + 1) * P],
                                               W["ident"][:])
                last.then_inc(o_turned, 1)

            def scores(it, j):
                half = ((it // NCH) % 2) * (G * T)
                pe.wait_ge(exp_done, NS * it + j + 1)
                for r in range(2):
                    h = 2 * (j % 2) + r
                    last = nc.tensor.matmul(
                        ps_s[:, (2 * (j % 2) + r) * CH:(2 * (j % 2) + r + 1) * CH],
                        K[:, ds(half + h * T + (j // 2) * P, P)],
                        Q[:, ds((it % (2 * NCH)) * (G * CH) + h * CH, CH)], start=True, stop=True)
                last.then_inc(s_ready, 1)

            def add_values(it, kt):
                if kt % 4 == 0:
                    pe.wait_ge(v_loaded[kt // 4], DMA * (it // NCH + 1))
                if kt == 0:
                    pe.wait_ge(oT_ready, it + 1)
                pe.wait_ge(exp_done, 2 + NS * it + 2 * kt + 2)
                for h in range(G):
                    slot = (2 * kt + h // 2) % 4
                    last = nc.tensor.matmul(ps_o[h * VW:(h + 1) * VW, :], V[:, kt, h * VW:(h + 1) * VW],
                                            prob[:, slot, (h % 2) * CH:(h % 2 + 1) * CH],
                                            start=(kt == 0), stop=(kt == KT - 1), skip_group_check=True)
                last.then_inc(pv_done, 1)

            def iteration(it, more, turn):
                def pieces(j):
                    if more:
                        for k in (2 * j, 2 * j + 1):
                            maximum_scores(it + 2, k)

                if more:
                    pe.wait_ge(kq_loaded, GROUP_LOADS * DMA * ((it + 2) // NCH + 1))
                pe.wait_ge(m_loaded, 2 * DMA * (it + 1))
                for kt in range(KT):
                    scores(it, 2 * kt)
                    pieces(2 * kt)
                    if kt == 1 and turn:
                        turn_maxima(it + 1)
                    if kt == 3:
                        turn_output(it, it + 2 if turn else it + 1)
                    scores(it, 2 * kt + 1)
                    if kt > 0:
                        add_values(it, kt - 1)
                    pieces(2 * kt + 1)
                add_values(it, KT - 1)

            pe.sem_inc(pv_done, 2)
            pe.wait_ge(rows_set, 3)
            pe.wait_ge(kq_loaded, GROUP_LOADS * DMA)
            for c in range(2):
                for k in range(NA):
                    maximum_scores(c, k)
                if c == 0:
                    turn_maxima(0)
            with pe.Fori(0, NIT - 2) as it:
                iteration(it, True, True)
            iteration(NIT - 2, False, True)
            iteration(NIT - 1, False, False)
            turn_output(NIT, NIT)



def phase_attend_band(nc, W, S):
    scale = 1.0 / C ** 0.5
    GK, GQ = G * TP, G * T
    TILES = [(kt, max(0, kt * P - REACH), min(CH, kt * P - REACH + WIN)) for kt in range(-1, TT + 1)]
    NS = len(TILES)
    NCHUNKS = NG * NCH
    with ExitStack() as ctx:
        n = Names(nc, ctx, "a1")
        K = n.sb("K", [NROWS, 2 * GK], BF16)
        Q = n.sb("Q", [NROWS, 2 * GQ], BF16)
        V = n.sb("V", [P, KT + 2, G * VW])
        prob = n.sb("prob", [P, 2, G, WIN])
        masked = n.sb("masked", [P, 4, WIN])
        maxes = n.sb("maxes", [P, G * TT])
        neg_max = n.sb("neg_max", [P, G * TT])
        m_parts = n.sb("m_parts", [G * TT, 2, P], BF16)
        oT = n.sb("oT", [P, CH])
        recip = n.sb("recip", [P, TT, G])
        o_out = n.sb("o_out", [P, TT, G, C])
        ps_a = n.ps("ps_a", 2 * CH)
        ps_s = n.ps("ps_s", 4 * CH)
        ps_o = n.ps("ps_o", CH)
        ps_m = n.ps("ps_m", CH)

        passed = n.sem("passed")
        rows_set = n.sem("rows_set")
        kq_loaded = n.sem("kq_loaded")
        v_loaded = [n.sem(f"v_loaded{q}") for q in range(4)]
        a_ready = n.sem("a_ready")
        a_done = n.sem("a_done")
        nm_ready = n.sem("nm_ready")
        mT_ready = n.sem("mT_ready")
        m_high = n.sem("m_high")
        m_low = n.sem("m_low")
        m_loaded = n.sem("m_loaded")
        s_ready = n.sem("s_ready")
        exp_done = n.sem("exp_done")
        pv_done = n.sem("pv_done")
        oT_ready = n.sem("oT_ready")
        o_turned = n.sem("o_turned")
        o_recip = n.sem("o_recip")
        o_done = n.sem("o_done")
        o_stored = n.sem("o_stored")
        out_clear = n.sem("out_clear")

        block = ctx.enter_context(nc.Block())

        def load_v(sp, g, q):
            sp.dma_start(V[:, 1 + 4 * q:5 + 4 * q, :],
                         S["v"][ds(g // NG2, 1), ds(g % NG2, 1), :, 4 * q:4 * q + 4, :]
                         .rearrange("a b p t n -> p (a b t) n")).then_inc(v_loaded[q], DMA)

        @block.sync
        def _(sp):
            load_group(sp, K, Q, S, kq_loaded, 0, 0, TP, P)
            for q in range(4):
                load_v(sp, 0, q)
            wait_apart(sp, kq_loaded, GROUP_LOADS * DMA, passed)
            load_group(sp, K, Q, S, kq_loaded, 1, 1, TP, P)

            def values(g):
                for q in range(4):
                    wait_apart(sp, pv_done, 2 + NS * (NCH * (g - 1) + min(q + 1, NCH - 1) + 1), passed)
                    load_v(sp, g, q)

            with sp.Fori(1, NG - 1) as g:
                values(g)
                wait_apart(sp, kq_loaded, GROUP_LOADS * DMA * (g + 1), passed)
                load_group(sp, K, Q, S, kq_loaded, g + 1, (g + 1) % 2, TP, P)
            values(NG - 1)

        @block.gpsimd
        def _(pool):
            def store_maxima(c):
                pool.wait_ge(m_low, c + 1)
                for part in range(2):
                    pool.dma_start(Q[ROW_M + part:ROW_M + part + 1, ds((c % (2 * NCH)) * (G * CH), G * CH)],
                                   m_parts[:, part, :]).then_inc(m_loaded, DMA)

            def store_output(c):
                pool.wait_ge(o_done, 1 + c + 1)
                pool.dma_start(S["att"][ds(c, 1)].rearrange("o (a p) c -> p (o a) c", p=P),
                               o_out[:].rearrange("p a h c -> p a (h c)")).then_inc(o_stored, DMA)

            pads = K[0:ROW_PAD, :].rearrange("r (g t) -> r g t", t=TP)
            pool.memset(pads[:, :, 0:P], 0.0).then_inc(rows_set, 1)
            pool.wait_ge(rows_set, 1)
            pool.memset(pads[:, :, P + T:TP], 0.0).then_inc(rows_set, 1)
            pool.wait_ge(rows_set, 2)
            pool.memset(V[:, 0, :], 0.0).then_inc(rows_set, 1)
            pool.wait_ge(rows_set, 3)
            pool.memset(V[:, KT + 1, :], 0.0).then_inc(rows_set, 1)
            pool.wait_ge(rows_set, 4)
            pool.memset(K[ROW_PAD:NROWS, :], 1.0).then_inc(rows_set, 1)
            pool.wait_ge(rows_set, 5)
            pool.memset(Q[ROW_PAD:NROWS, :], 1.0).then_inc(rows_set, 1)
            pool.wait_ge(rows_set, 6)
            pad_row = K[ROW_PAD:ROW_PAD + 1, :].rearrange("r (g t) -> r g t", t=TP)
            pool.memset(pad_row, NEG).then_inc(rows_set, 1)
            pool.wait_ge(rows_set, 7)
            pool.memset(pad_row[:, :, P:P + T], 0.0).then_inc(rows_set, 1)
            pool.wait_ge(rows_set, 8)
            pool.memset(o_out[:], 1.0).then_inc(out_clear, 1)
            pool.wait_ge(out_clear, 1)
            pool.dma_start(S["att"][0:1].rearrange("o (a p) c -> p (o a) c", p=P),
                           o_out[:].rearrange("p a h c -> p a (h c)")).then_inc(o_stored, DMA)
            store_maxima(0)
            with pool.Fori(0, NCHUNKS - 1) as c:
                store_maxima(c + 1)
                store_output(c)
            store_output(NCHUNKS - 1)
            store_output(NCHUNKS)
            pool.wait_ge(o_stored, DMA * (NCHUNKS + 2))

        @block.vector
        def _(dve):
            def split_maxima(c):
                dve.wait_ge(mT_ready, c + 1)
                if not isinstance(c, int) or c > 0:
                    dve.wait_ge(m_loaded, 2 * DMA * c)
                nc.vector.tensor_copy(m_parts[:, 0, :], ps_m[0:G * TT, 0:P]).then_inc(m_high, 1)
                dve.wait_ge(m_high, c + 1)
                nc.vector.tensor_tensor(m_parts[:, 1, :], ps_m[0:G * TT, 0:P], m_parts[:, 0, :],
                                        ALU.subtract).then_inc(m_low, 1)

            def maxima(c, lo, hi):
                if lo == 0 and (not isinstance(c, int) or c > 0):
                    dve.wait_ge(nm_ready, c)
                for k in range(lo, hi):
                    if k % 2 == 0:
                        wait_apart(dve, a_ready, G * TT // 2 * c + k // 2 + 1, passed)
                    nc.vector.tensor_tensor_reduce(masked[:, k % 4, :], ps_a[:, (k % 4) * WIN:(k % 4 + 1) * WIN],
                                                   W["mask"][:], 1.0, 3 * NEG, ALU.add, ALU.max,
                                                   maxes[:, k:k + 1]).then_inc(a_done, 1)

            def whole_maxima(c):
                dve.wait_ge(a_done, 4 + G * TT * (c + 1))
                if not isinstance(c, int) or c > 0:
                    dve.wait_ge(mT_ready, c)
                nc.vector.tensor_scalar(neg_max[:], maxes[:], -1.0, None, ALU.mult).then_inc(nm_ready, 1)

            def normalise(c):
                dve.wait_ge(o_turned, c + 1)
                turned = ps_m[:].rearrange("p (a h w) -> p a h w", a=TT, h=G)
                nc.vector.reciprocal(recip[:], turned[:, :, :, C]).then_inc(o_recip, 1)
                dve.wait_ge(o_recip, c + 1)
                dve.wait_ge(o_stored, DMA * (c + 1))
                nc.vector.tensor_tensor(o_out[:], turned[:, :, :, 0:C],
                                        recip[:].unsqueeze(3).broadcast_to([P, TT, G, C]), ALU.mult
                                        ).then_inc(o_done, 1)

            dve.sem_inc(a_done, 4)
            dve.sem_inc(o_done, 1)
            maxima(0, 0, G * TT)
            whole_maxima(0)
            split_maxima(0)
            maxima(1, 0, G * TT)
            whole_maxima(1)
            with dve.Fori(0, NCHUNKS - 2) as c:
                split_maxima(c + 1)
                maxima(c + 2, 0, 8)
                normalise(c)
                maxima(c + 2, 8, G * TT)
                whole_maxima(c + 2)
            split_maxima(NCHUNKS - 1)
            for c in (NCHUNKS - 2, NCHUNKS - 1, NCHUNKS):
                normalise(c)

        @block.scalar
        def _(act):
            act.sem_inc(exp_done, 2)
            nc.scalar.activation(oT[:], W["ones"][:], ACT.Copy).then_inc(oT_ready, 1)
            with act.Fori(0, NCHUNKS) as c:
                for j, (kt, lo, hi) in enumerate(TILES):
                    act.wait_ge(s_ready, NS * c + j + 1)
                    act.wait_ge(pv_done, NS * c + j + 1)
                    s = ps_s[:, (j % 2) * 2 * CH:(j % 2 + 1) * 2 * CH].rearrange("p (h q) -> p h q", h=G)
                    nc.scalar.activation(prob[:, j % 2, :, 0:hi - lo], s[:, :, 0:hi - lo], ACT.Exp,
                                         scale=scale).then_inc(exp_done, 1)
                act.wait_ge(pv_done, 2 + NS * (c + 1))
                act.wait_ge(o_turned, c + 1)
                nc.scalar.activation(oT[:], ps_o[:], ACT.Copy).then_inc(oT_ready, 1)

        @block.tensor
        def _(pe):
            def maximum_scores(g, half, qc, pair):
                c = NCH * g + qc
                pe.wait_ge(a_done, G * TT * c + 2 * pair + 2)
                for r in range(2):
                    h, qt = (2 * pair + r) // TT, (2 * pair + r) % TT
                    q0 = half * GQ + (qc * G + h) * CH + qt * P
                    k0 = half * GK + h * TP + qc * CH + qt * P + P - REACH
                    slot = (2 * pair + r) % 4
                    last = nc.tensor.matmul(ps_a[:, slot * WIN:(slot + 1) * WIN], Q[0:ROW_M, ds(q0, P)],
                                            K[0:ROW_M, ds(k0, WIN)], start=True, stop=True,
                                            skip_group_check=True)
                last.then_inc(a_ready, 1)

            def turn_maxima(c):
                pe.wait_ge(nm_ready, c + 1)
                if not isinstance(c, int) or c > 0:
                    pe.wait_ge(m_low, c)
                    pe.wait_ge(o_done, c)
                nc.tensor.transpose(ps_m[0:G * TT, 0:P], neg_max[:], W["ident"][:]).then_inc(mT_ready, 1)

            def turn_output(c, m_users):
                pe.wait_ge(oT_ready, c + 1)
                pe.wait_ge(m_low, m_users)
                pe.wait_ge(o_done, c + 1)
                for a in range(TT):
                    last = nc.tensor.transpose(ps_m[:, a * P:(a + 1) * P], oT[:, a * P:(a + 1) * P],
                                               W["ident"][:])
                last.then_inc(o_turned, 1)

            def scores(g, half, qc, j):
                kt, lo, hi = TILES[j]
                w = hi - lo
                first = lo - (kt * P - REACH)
                pe.wait_ge(exp_done, NS * (NCH * g + qc) + j + 1)
                for pair in range(2):
                    base = (j % 2) * 2 * CH + pair * CH
                    for r in range(2):
                        h = 2 * pair + r
                        nc.tensor.matmul(ps_s[:, base + r * WIN:base + r * WIN + w],
                                         K[:, ds(half * GK + h * TP + P + qc * CH + kt * P, P)],
                                         Q[:, ds(half * GQ + (qc * G + h) * CH + lo, w)],
                                         start=(r == 0), stop=False, skip_group_check=True)
                    for r in range(2):
                        last = nc.tensor.matmul(ps_s[:, base + r * WIN:base + r * WIN + w],
                                                W["ident_bf"][:], W["mask_bf"][:, first:first + w],
                                                start=False, stop=True, skip_group_check=True)
                last.then_inc(s_ready, 1)

            def add_values(g, qc, j):
                kt, lo, hi = TILES[j]
                c = NCH * g + qc
                if j == 0:
                    pe.wait_ge(oT_ready, c + 1)
                    pe.wait_ge(v_loaded[qc], DMA * (g + 1))
                if j == NS - 1 and qc < NCH - 1:
                    pe.wait_ge(v_loaded[qc + 1], DMA * (g + 1))
                pe.wait_ge(exp_done, 2 + NS * c + j + 1)
                for h in range(G):
                    last = nc.tensor.matmul(ps_o[h * VW:(h + 1) * VW, lo:hi],
                                            V[:, 1 + qc * TT + kt, h * VW:(h + 1) * VW],
                                            prob[:, j % 2, h, 0:hi - lo], start=(j == 0),
                                            stop=(j == NS - 1), skip_group_check=True)
                last.then_inc(pv_done, 1)

            def group(g, half, next_half, more):
                for qc in range(NCH):
                    c = NCH * g + qc
                    ahead = qc + 2 < NCH or more
                    turn = qc + 1 < NCH or more
                    a_g, a_half, a_qc = (g, half, qc + 2) if qc + 2 < NCH else (g + 1, next_half, qc - 2)
                    if ahead and a_qc == 0:
                        pe.wait_ge(kq_loaded, GROUP_LOADS * DMA * (a_g + 1))
                    pe.wait_ge(m_loaded, 2 * DMA * (c + 1))
                    pairs = list(range(G * TT // 2))
                    for j in range(NS):
                        scores(g, half, qc, j)
                        if j == 0 and turn:
                            turn_maxima(c + 1)
                        if ahead:
                            for _ in range(2 if j in (1, 3) else 1):
                                maximum_scores(a_g, a_half, a_qc, pairs.pop(0))
                        if j == 3:
                            turn_output(c, c + 2 if turn else c + 1)
                        if j > 0:
                            add_values(g, qc, j - 1)
                    add_values(g, qc, NS - 1)

            pe.sem_inc(pv_done, 2)
            pe.wait_ge(rows_set, 8)
            pe.wait_ge(kq_loaded, GROUP_LOADS * DMA)
            for c in range(2):
                for pair in range(G * TT // 2):
                    maximum_scores(0, 0, c, pair)
                if c == 0:
                    turn_maxima(0)
            with pe.Fori(0, NG - 1) as g:
                group(g, g % 2, (g + 1) % 2, True)
            group(NG - 1, (NG - 1) % 2, 0, False)
            turn_output(NCHUNKS, NCHUNKS)



TILES_BODY = 2 * TT


def phase_router(nc, W):
    with ExitStack() as ctx:
        n = Names(nc, ctx, "r")
        groups = B * KT * 2
        top = n.sb("top", [P, groups])
        total = n.sb("total", [P, groups])
        inv = n.sb("inv", [P, groups])
        step = n.sem("step")
        exp_done = n.sem("exp_done")
        block = ctx.enter_context(nc.Block())
        logits = W["logits"][:].rearrange("p b t r e -> p (b t r) e")
        each = lambda x: x[:].unsqueeze(2).broadcast_to([P, groups, E])

        @block.scalar
        def _(act):
            act.wait_ge(step, 2)
            nc.scalar.activation(W["logits"][:].rearrange("p b t r e -> p (b t r e)"),
                                 W["logits"][:].rearrange("p b t r e -> p (b t r e)"), ACT.Exp
                                 ).then_inc(exp_done, 1)

        @block.vector
        def _(dve):
            nc.vector.tensor_reduce(top[:], logits, AX.X, ALU.max).then_inc(step, 1)
            dve.wait_ge(step, 1)
            nc.vector.tensor_tensor(logits, logits, each(top), ALU.subtract).then_inc(step, 1)
            dve.wait_ge(exp_done, 1)
            nc.vector.tensor_reduce(total[:], logits, AX.X, ALU.add).then_inc(step, 1)
            dve.wait_ge(step, 3)
            nc.vector.reciprocal(inv[:], total[:]).then_inc(step, 1)
            dve.wait_ge(step, 4)
            per_token = inv[:].rearrange("p (b t r) -> p b t r", b=B, r=2)
            nc.vector.tensor_tensor(per_token, per_token,
                                    W["inv_n"][:].unsqueeze(1).unsqueeze(3).broadcast_to([P, B, KT, 2]),
                                    ALU.mult).then_inc(step, 1)
            dve.wait_ge(step, 5)
            inverse = inv[:].rearrange("p (t r) -> p t r", r=2)[:, :, 1]
            nc.vector.tensor_scalar(inverse, inverse, W["alpha"][:], None, ALU.mult).then_inc(step, 1)
            dve.wait_ge(step, 6)
            nc.vector.tensor_tensor(logits, logits, each(inv), ALU.mult).then_inc(step, 1)


def load_att(sp, S, att, loaded, i, u):
    for hg in range(NG2):
        slot = (u * NG2 + hg) * NCH + i + 1
        sp.dma_start(att[:, u, :, hg * G * C:(hg + 1) * G * C],
                     S["att"][ds(slot, 1)].rearrange("o (a p) c -> p (o a) c", p=P)).then_inc(loaded, DMA)


def store_and_load(sp, passed, x1_done, stored, x_io, out_dram, load):
    def store(i, u):
        wait_apart(sp, x1_done, 2 + TILES_BODY * i + TT * (u + 1), passed)
        sp.dma_start(out_dram[u, ds(i * CH, CH), :].rearrange("(t p) d -> p t d", p=P), x_io[:, u]
                     ).then_inc(stored[u], DMA)

    load(0, 0)
    load(0, 1)
    with sp.Fori(0, NCH - 1) as i:
        for u in range(2):
            store(i, u)
            wait_apart(sp, stored[u], DMA * (i + 1), passed)
            load(i + 1, u)
    for u in range(2):
        store(NCH - 1, u)
    for u in range(2):
        wait_apart(sp, stored[u], DMA * NCH, passed)


def phase_combine_experts(nc, W, S, x_dram, out_dram):
    with ExitStack() as ctx:
        n_ = Names(nc, ctx, "c0")
        x_io = n_.sb("x_io", [P, 2, TT, D])
        xn = n_.sb("xn", [P, 2, TT, D])
        att = n_.sb("att", [P, 2, TT, D])
        xT = n_.sb("xT", [P, 2, 2, DK, CH], F32R)
        cT = n_.sb("cT", [P, 2, 2, DK, CH], F32R)
        xv = n_.sb("xv", [P, 2 * KR])
        prod = n_.sb("prod", [P, 2 * KR])
        wprod = n_.sb("wprod", [P, 2 * KR])
        pT = n_.sb("pT", [P, 2, 2 * KR], F32R)
        aT = n_.sb("aT", [P, 2, D], F32R)
        wT = n_.sb("wT", [2 * E, P])
        wtile = n_.sb("wtile", [P, TILES_BODY, 2 * E])
        sums = n_.sb("sums", [P, 2, D])
        eg = n_.sb("eg", [P, D])
        gate = n_.sb("gate", [P, 2, D])
        ps_xv = n_.ps("ps_xv", 2 * CH)
        ps_cy = n_.ps("ps_cy", 2 * CH)
        ps_pt = n_.ps("ps_pt", 2 * CH)
        ps_out = n_.ps("ps_out", CH)
        ps_m = n_.ps("ps_m", CH)

        passed = n_.sem("passed")
        loaded = [n_.sem(f"loaded{u}") for u in range(2)]
        stored = [n_.sem(f"stored{u}") for u in range(2)]
        xv_ready = n_.sem("xv_ready")
        cy_ready = n_.sem("cy_ready")
        xv_copied = n_.sem("xv_copied")
        prod_done = n_.sem("prod_done")
        wprod_done = n_.sem("wprod_done")
        m_ready = n_.sem("m_ready")
        pt_ready = n_.sem("pt_ready")
        high = n_.sem("high")
        low = n_.sem("low")
        out_ready = n_.sem("out_ready")
        exp_done = n_.sem("exp_done")
        bias_done = n_.sem("bias_done")
        step = n_.sem("step")
        out_read = n_.sem("out_read")
        wtile_done = n_.sem("wtile_done")
        mixed = n_.sem("mixed")
        x1_done = n_.sem("x1_done")

        block = ctx.enter_context(nc.Block())
        n_loads = 4 * DK + 2 + NG2
        order = [(u, t) for u in range(2) for t in range(TT)]

        @block.sync
        def _(sp):
            def load(i, u):
                tok = ds(i * CH, CH)
                for part in range(2):
                    for k in range(DK):
                        sp.dma_start(f32(xT[:, u, part, k, :]), S["xT"][u, part, k, :, tok]).then_inc(loaded[u], DMA)
                        sp.dma_start(f32(cT[:, u, part, k, :]), S["cT"][u, part, k, :, tok]).then_inc(loaded[u], DMA)
                rows = lambda x: x[u, tok, :].rearrange("(t p) d -> p t d", p=P)
                sp.dma_start(x_io[:, u], rows(x_dram)).then_inc(loaded[u], DMA)
                sp.dma_start(xn[:, u], rows(S["xn"])).then_inc(loaded[u], DMA)
                load_att(sp, S, att, loaded[u], i, u)

            store_and_load(sp, passed, x1_done, stored, x_io, out_dram, load)

        @block.tensor
        def _(pe):
            def front(i, j):
                u, t = order[j]
                n = TILES_BODY * i + j
                if t == 0:
                    pe.wait_ge(loaded[u], DMA * n_loads * (i + 1))
                pe.wait_ge(xv_copied, n + 1)
                for r in range(2):
                    last = split_matmul(nc, ps_xv[:, r * CH:(r + 1) * CH],
                                        lambda s, k: xT[:, u, s, k, t * P:(t + 1) * P],
                                        lambda s, k: W["AQ"][:, s, k, r * KR:(r + 1) * KR], DK, True, True)
                last.then_inc(xv_ready, 1)
                pe.wait_ge(prod_done, n + 1)
                for r in range(2):
                    last = split_matmul(nc, ps_cy[:, r * CH:(r + 1) * CH],
                                        lambda s, k: cT[:, u, s, k, t * P:(t + 1) * P],
                                        lambda s, k: W["BK"][:, s, k, r * KR:(r + 1) * KR], DK, True, True)
                last.then_inc(cy_ready, 1)

            def turn(i, j):
                u, t = order[j]
                n = TILES_BODY * i + j
                if j == 0:
                    pe.wait_ge(wtile_done, 2 * (i + 1))
                pe.wait_ge(low, 3 * (n + 1))
                for k in range(DK):
                    nc.tensor.transpose(ps_m[:, k * P:(k + 1) * P], att[:, u, t, k * P:(k + 1) * P],
                                        W["ident"][:])
                nc.tensor.transpose(ps_m[0:2 * E, D:D + P], wtile[:, j, :], W["ident"][:]
                                    ).then_inc(m_ready, 1)
                pe.wait_ge(wprod_done, 1 + n + 1)
                for half in range(2):
                    for m in range(TT):
                        c = (half * TT + m) * P
                        last = nc.tensor.transpose(ps_pt[:, c:c + P], wprod[:, c:c + P], W["ident"][:])
                    last.then_inc(pt_ready, 1)

            def out(i, j):
                n = TILES_BODY * i + j
                pe.wait_ge(out_read, n + 1)
                pe.wait_ge(high, 4 * (n + 1))
                pe.wait_ge(low, 3 + 3 * (n + 1))
                split_matmul(nc, ps_out[:, 0:D], lambda s, k: aT[:, s, k * P:(k + 1) * P],
                             lambda s, k: W["o0"][:, s, k, :], DK, True, True)
                split_matmul(nc, ps_out[:, D:2 * D], lambda s, k: pT[:, s, k * P:(k + 1) * P],
                             lambda s, k: W["UO"][:, s, k, :], 2 * KR // P, True, False)
                nc.tensor.matmul(ps_out[:, D:2 * D], wT[:], W["bO"][:], start=False, stop=True,
                                 skip_group_check=True).then_inc(out_ready, 1)

            pe.sem_inc(out_ready, 1)
            with pe.Fori(0, NCH) as i:
                front(i, 0)
                for j in range(1, TILES_BODY):
                    turn(i, j - 1)
                    front(i, j)
                    out(i, j - 1)
                turn(i, TILES_BODY - 1)
                out(i, TILES_BODY - 1)

        @block.scalar
        def _(act):
            def copies(i, j):
                n = TILES_BODY * i + j
                act.wait_ge(out_ready, n + 1)
                act.wait_ge(m_ready, n + 1)
                nc.scalar.activation(aT[:, 0, :], ps_m[:, 0:D], ACT.Copy).then_inc(high, 1)
                nc.scalar.activation(wT[:], ps_m[0:2 * E, D:D + P], ACT.Copy).then_inc(high, 1)
                for half in range(2):
                    act.wait_ge(pt_ready, 2 * n + half + 1)
                    nc.scalar.activation(pT[:, 0, half * CH:(half + 1) * CH],
                                         ps_pt[:, half * CH:(half + 1) * CH], ACT.Copy).then_inc(high, 1)

            def left(i, j):
                n = TILES_BODY * i + j
                act.wait_ge(xv_ready, n + 1)
                act.wait_ge(prod_done, n + 1)
                nc.scalar.activation(xv[:], ps_xv[:], ACT.Copy).then_inc(xv_copied, 1)

            def exponential(i, j):
                n = TILES_BODY * i + j
                act.wait_ge(out_ready, 1 + n + 1)
                act.wait_ge(out_read, n + 1)
                nc.scalar.activation(eg[:], ps_out[:, D:2 * D], ACT.Exp, scale=-1.0).then_inc(exp_done, 1)

            act.sem_inc(xv_copied, 1)
            with act.Fori(0, NCH) as i:
                for j in range(TILES_BODY + 1):
                    if j > 0:
                        copies(i, j - 1)
                    if j < TILES_BODY:
                        left(i, j)
                    if j > 0:
                        exponential(i, j - 1)

        @block.vector
        def _(dve):
            def rests(i, j):
                n = TILES_BODY * i + j
                dve.wait_ge(high, 4 * n + 2)
                nc.vector.tensor_tensor(aT[:, 1, :], ps_m[:, 0:D], f32(aT[:, 0, :]), ALU.subtract).then_inc(low, 1)
                for half in range(2):
                    dve.wait_ge(high, 4 * n + 3 + half)
                    nc.vector.tensor_tensor(pT[:, 1, half * CH:(half + 1) * CH],
                                            ps_pt[:, half * CH:(half + 1) * CH],
                                            f32(pT[:, 0, half * CH:(half + 1) * CH]), ALU.subtract).then_inc(low, 1)

            def product(i, j):
                n = TILES_BODY * i + j
                dve.wait_ge(xv_copied, 1 + n + 1)
                dve.wait_ge(cy_ready, n + 1)
                dve.wait_ge(wprod_done, n + 1)
                nc.vector.tensor_tensor(prod[:], ps_cy[:], xv[:], ALU.mult).then_inc(prod_done, 1)

            dve.sem_inc(prod_done, 1)
            dve.sem_inc(low, 3)
            dve.sem_inc(out_read, 1)
            with dve.Fori(0, NCH) as i:
                for j in range(TILES_BODY + 1):
                    if j > 0:
                        rests(i, j - 1)
                    if j < TILES_BODY:
                        product(i, j)
                    if j > 0:
                        gate_steps(nc, dve, TILES_BODY * i + j - 1, (j - 1) % 2, ps_out[:, 0:D],
                                   ps_out[:, D:2 * D], sums, eg, gate, exp_done, bias_done, step,
                                   out_read, x1_done)

        @block.gpsimd
        def _(pool):
            def bias(i, j):
                u, t = order[j]
                n = TILES_BODY * i + j
                if t == 0:
                    pool.wait_ge(loaded[u], DMA * n_loads * (i + 1))
                pool.wait_ge(x1_done, n + 1)
                pool.tensor_tensor(sums[:, j % 2], xn[:, u, t], W["bo"][:, 0], ALU.add).then_inc(bias_done, 1)

            def weighted(i, j):
                u, t = order[j]
                n = TILES_BODY * i + j
                pool.wait_ge(prod_done, 1 + n + 1)
                if j > 0:
                    pool.wait_ge(pt_ready, 2 * n)
                pool.tensor_tensor(wprod[:].rearrange("p (e r) -> p e r", r=R),
                                   prod[:].rearrange("p (e r) -> p e r", r=R),
                                   wtile[:, j].unsqueeze(2).broadcast_to([P, 2 * E, R]), ALU.mult
                                   ).then_inc(wprod_done, 1)

            pool.sem_inc(wprod_done, 1)
            pool.sem_inc(x1_done, 2)
            with pool.Fori(0, NCH) as i:
                wait_apart(pool, out_ready, TILES_BODY * i + 1, passed)
                for u in range(2):
                    pool.tensor_copy(wtile[:, u * TT:(u + 1) * TT, :],
                                            W["logits"][:, u, ds(i * TT, TT), :, :]
                                            .rearrange("p t r e -> p t (r e)")).then_inc(wtile_done, 1)
                pool.wait_ge(wtile_done, 2 * (i + 1))
                for j in range(TILES_BODY + 1):
                    if j < TILES_BODY:
                        bias(i, j)
                        weighted(i, j)
                    if j > 0:
                        u, t = order[j - 1]
                        residual(pool, TILES_BODY * i + j - 1, x_io[:, u, t], sums[:, (j - 1) % 2],
                                 gate[:, (j - 1) % 2], out_read, mixed, x1_done)


def gate_steps(nc, dve, n, slot, ps_s, ps_g, sums, eg, gate, exp_done, bias_done, step, out_read, x1_done):
    dve.wait_ge(exp_done, n + 1)
    nc.vector.tensor_scalar(eg[:], eg[:], 1.0, None, ALU.add).then_inc(step, 1)
    dve.wait_ge(bias_done, n + 1)
    nc.vector.tensor_tensor(sums[:, slot], ps_s, sums[:, slot], ALU.add).then_inc(step, 1)
    dve.wait_ge(step, 3 * n + 1)
    nc.vector.reciprocal(eg[:], eg[:]).then_inc(step, 1)
    dve.wait_ge(x1_done, n + 1)
    dve.wait_ge(step, 3 * n + 3)
    nc.vector.tensor_tensor(gate[:, slot], ps_g, eg[:], ALU.mult).then_inc(out_read, 1)


def residual(pool, n, x, s, gate, out_read, mixed, x1_done, seed=1):
    pool.wait_ge(out_read, seed + n + 1)
    pool.tensor_tensor(s, s, gate, ALU.mult).then_inc(mixed, 1)
    pool.wait_ge(mixed, n + 1)
    pool.tensor_tensor(x, x, s, ALU.add).then_inc(x1_done, 1)


def phase_combine_lora(nc, W, S, x_dram, out_dram):
    NGT = E1 + E1 * R1
    with ExitStack() as ctx:
        n_ = Names(nc, ctx, "c1")
        x_io = n_.sb("x_io", [P, 2, TT, D])
        att = n_.sb("att", [P, 2, TT, D])
        xT = n_.sb("xT", [P, 2, 2, DK, CH], F32R)
        neg_top = n_.sb("neg_top", [P, 1])
        ge = n_.sb("ge", [P, E1])
        total = n_.sb("total", [P, 1])
        inv = n_.sb("inv", [P, 1])
        weight = n_.sb("weight", [P, E1])
        wt = n_.sb("wt", [P, E1 * R1])
        turned = n_.sb("turned", [P, 2, D + P], F32R)
        sums = n_.sb("sums", [P, 2, D])
        eg = n_.sb("eg", [P, D])
        gate = n_.sb("gate", [P, 2, D])
        ps_gt = n_.ps("ps_gt", CH)
        ps_g = n_.ps("ps_g", 2 * CH)
        ps_s = n_.ps("ps_s", 2 * CH)
        ps_m = n_.ps("ps_m", CH)

        passed = n_.sem("passed")
        loaded = [n_.sem(f"loaded{u}") for u in range(2)]
        stored = [n_.sem(f"stored{u}") for u in range(2)]
        gt_ready = n_.sem("gt_ready")
        soft = n_.sem("soft")
        ge_done = n_.sem("ge_done")
        wt_done = n_.sem("wt_done")
        m_ready = n_.sem("m_ready")
        high = n_.sem("high")
        low = n_.sem("low")
        out_ready = n_.sem("out_ready")
        exp_done = n_.sem("exp_done")
        bias_done = n_.sem("bias_done")
        step = n_.sem("step")
        out_read = n_.sem("out_read")
        mixed = n_.sem("mixed")
        x1_done = n_.sem("x1_done")

        block = ctx.enter_context(nc.Block())
        n_loads = 2 * DK + 1 + NG2
        order = [(u, t) for u in range(2) for t in range(TT)]

        @block.sync
        def _(sp):
            def load(i, u):
                tok = ds(i * CH, CH)
                for part in range(2):
                    for k in range(DK):
                        sp.dma_start(f32(xT[:, u, part, k, :]), S["xT"][u, part, k, :, tok]).then_inc(loaded[u], DMA)
                sp.dma_start(x_io[:, u], x_dram[u, tok, :].rearrange("(t p) d -> p t d", p=P)
                             ).then_inc(loaded[u], DMA)
                load_att(sp, S, att, loaded[u], i, u)

            store_and_load(sp, passed, x1_done, stored, x_io, out_dram, load)

        @block.tensor
        def _(pe):
            def front(i, j):
                u, t = order[j]
                n = TILES_BODY * i + j
                bank = (j % 2) * CH
                if t == 0:
                    pe.wait_ge(loaded[u], DMA * n_loads * (i + 1))
                x = lambda s, k: xT[:, u, s, k, t * P:(t + 1) * P]
                pe.wait_ge(wt_done, n + 1)
                split_matmul(nc, ps_gt[:, 0:NGT], x, lambda s, k: W["gate"][:, s, k, 0:NGT], DK, True, True
                             ).then_inc(gt_ready, 1)
                pe.wait_ge(out_read, n + 1)
                split_matmul(nc, ps_g[:, bank:bank + D], x, lambda s, k: W["gate"][:, s, k, NGT:], DK,
                             True, False)

            def turn(i, j):
                u, t = order[j]
                n = TILES_BODY * i + j
                pe.wait_ge(low, n + 1)
                for k in range(DK):
                    nc.tensor.transpose(ps_m[:, k * P:(k + 1) * P], att[:, u, t, k * P:(k + 1) * P],
                                        W["ident"][:])
                pe.wait_ge(wt_done, 1 + n + 1)
                nc.tensor.transpose(ps_m[:, D:D + P], wt[:], W["ident"][:]).then_inc(m_ready, 1)

            def out(i, j):
                n = TILES_BODY * i + j
                bank = (j % 2) * CH
                pe.wait_ge(high, n + 1)
                pe.wait_ge(low, 1 + n + 1)
                split_matmul(nc, ps_s[:, bank:bank + D], lambda s, k: turned[:, s, k * P:(k + 1) * P],
                             lambda s, k: W["o1"][:, s, k, :], DK, True, True)
                split_matmul(nc, ps_g[:, bank:bank + D], lambda s, k: turned[:, s, D:D + P],
                             lambda s, k: W["loraV"][:, s, 0, :], 1, False, True).then_inc(out_ready, 1)

            pe.sem_inc(out_ready, 1)
            with pe.Fori(0, NCH) as i:
                front(i, 0)
                for j in range(1, TILES_BODY):
                    turn(i, j - 1)
                    front(i, j)
                    out(i, j - 1)
                turn(i, TILES_BODY - 1)
                out(i, TILES_BODY - 1)

        @block.scalar
        def _(act):
            def softmax(i, j):
                n = TILES_BODY * i + j
                act.wait_ge(soft, 3 * n + 1)
                nc.scalar.activation(ge[:], ps_gt[:, 0:E1], ACT.Exp, bias=neg_top[:], accum_out=total[:]
                                     ).then_inc(ge_done, 1)

            def copies(i, j):
                n = TILES_BODY * i + j
                act.wait_ge(out_ready, n + 1)
                act.wait_ge(m_ready, n + 1)
                nc.scalar.activation(turned[:, 0, :], ps_m[:, 0:D + P], ACT.Copy).then_inc(high, 1)

            def exponential(i, j):
                n = TILES_BODY * i + j
                bank = (j % 2) * CH
                act.wait_ge(out_ready, 1 + n + 1)
                act.wait_ge(out_read, 1 + n + 1)
                nc.scalar.activation(eg[:], ps_g[:, bank:bank + D], ACT.Exp, scale=-1.0).then_inc(exp_done, 1)

            with act.Fori(0, NCH) as i:
                for j in range(TILES_BODY + 1):
                    if j > 0:
                        copies(i, j - 1)
                    if j < TILES_BODY:
                        softmax(i, j)
                    if j > 0:
                        exponential(i, j - 1)

        @block.vector
        def _(dve):
            def gates(i, j):
                n = TILES_BODY * i + j
                dve.wait_ge(gt_ready, n + 1)
                nc.vector.tensor_reduce(neg_top[:], ps_gt[:, 0:E1], AX.X, ALU.max, negate=True).then_inc(soft, 1)
                dve.wait_ge(ge_done, n + 1)
                nc.vector.reciprocal(inv[:], total[:]).then_inc(soft, 1)
                dve.wait_ge(soft, 3 * n + 2)
                nc.vector.tensor_scalar(weight[:], ge[:], inv[:], 1.0 / R1, ALU.mult, ALU.mult).then_inc(soft, 1)
                dve.wait_ge(soft, 3 * n + 3)
                if j > 0:
                    dve.wait_ge(m_ready, n)
                nc.vector.tensor_tensor(wt[:].rearrange("p (e r) -> p e r", r=R1),
                                        ps_gt[:, E1:NGT].rearrange("p (e r) -> p e r", r=R1),
                                        weight[:].unsqueeze(2).broadcast_to([P, E1, R1]), ALU.mult
                                        ).then_inc(wt_done, 1)

            def rest(i, j):
                n = TILES_BODY * i + j
                dve.wait_ge(high, n + 1)
                nc.vector.tensor_tensor(turned[:, 1, :], ps_m[:, 0:D + P], f32(turned[:, 0, :]), ALU.subtract
                                        ).then_inc(low, 1)

            dve.sem_inc(wt_done, 1)
            dve.sem_inc(low, 1)
            dve.sem_inc(out_read, 2)
            with dve.Fori(0, NCH) as i:
                for j in range(TILES_BODY + 1):
                    if j > 0:
                        rest(i, j - 1)
                    if j < TILES_BODY:
                        gates(i, j)
                    if j > 0:
                        bank = ((j - 1) % 2) * CH
                        gate_steps(nc, dve, TILES_BODY * i + j - 1, (j - 1) % 2, ps_s[:, bank:bank + D],
                                   ps_g[:, bank:bank + D], sums, eg, gate, exp_done, bias_done, step,
                                   out_read, x1_done)

        @block.gpsimd
        def _(pool):
            pool.sem_inc(x1_done, 2)
            with pool.Fori(0, NCH) as i:
                for j in range(TILES_BODY + 1):
                    if j < TILES_BODY:
                        wait_apart(pool, x1_done, TILES_BODY * i + j + 1, passed)
                        pool.tensor_copy(sums[:, j % 2], W["bo"][:, 1]).then_inc(bias_done, 1)
                    if j > 0:
                        u, t = order[j - 1]
                        residual(pool, TILES_BODY * i + j - 1, x_io[:, u, t], sums[:, (j - 1) % 2],
                                 gate[:, (j - 1) % 2], out_read, mixed, x1_done, 2)


def recurrent_blocks(nc, I, out):
    with ExitStack() as ctx:
        n = Names(nc, ctx, "k")
        W = {
            "AQ": n.sb("AQ", [P, 2, DK, 2 * KR], F32R), "BK": n.sb("BK", [P, 2, DK, 2 * KR], F32R),
            "RT": n.sb("RT", [P, 2, DK, 2 * D], F32R), "UO": n.sb("UO", [P, 2, 2 * KR // P, D], F32R),
            "bO": n.sb("bO", [2 * E, D]), "w2": n.sb("w2", [P, DK, E]),
            "qkv0": n.sb("qkv0", [P, 2, DK, 3 * D], F32R), "qkv1": n.sb("qkv1", [P, 2, DK, 3 * D], F32R),
            "o0": n.sb("o0", [P, 2, DK, D], F32R), "o1": n.sb("o1", [P, 2, DK, D], F32R),
            "gate": n.sb("gate", [P, 2, DK, E1 + E1 * R1 + D], F32R),
            "loraV": n.sb("loraV", [P, 2, 1, D], F32R),
            "bqk": n.sb("bqk", [P, 2, 4]), "bv": n.sb("bv", [P, 2, D]), "bo": n.sb("bo", [P, 2, D]),
            "b1": n.sb("b1", [P, DK]), "b2": n.sb("b2", [64, 1]), "alpha": n.sb("alpha", [P, 1]),
            "ident": n.sb("ident", [P, P]), "ident_bf": n.sb("ident_bf", [P, P], BF16),
            "mask": n.sb("mask", [P, WIN]), "mask_bf": n.sb("mask_bf", [P, WIN], BF16),
            "ones": n.sb("ones", [P, CH]), "half": n.sb("half", [P, TT]),
            "inv_n": n.sb("inv_n", [P, KT]),
            "logits": n.sb("logits", [P, B, KT, 2, E]),
        }
        S = {
            "xn": nc.dram_tensor("s_xn", [B, T, D], F32).ap(),
            "x1": nc.dram_tensor("s_x1", [B, T, D], F32).ap(),
            "xT": nc.dram_tensor("s_xT", [B, 2, DK, P, T], F32).ap(),
            "cT": nc.dram_tensor("s_cT", [B, 2, DK, P, T], F32).ap(),
            "parts": nc.dram_tensor("s_parts", [2, B, 3, D, T], BF16).ap(),
            "v": nc.dram_tensor("s_v", [B, NG2, P, KT, G * VW], F32).ap(),
            "att": nc.dram_tensor("s_att", [NIT + 1, CH, G * C], F32).ap(),
        }
        phase_weights(nc, W, I)
        phase_project(nc, W, S, I["x"], 0)
        phase_router(nc, W)
        phase_attend_full(nc, W, S)
        phase_combine_experts(nc, W, S, I["x"], S["x1"])
        phase_project(nc, W, S, S["x1"], 1)
        phase_attend_band(nc, W, S)
        phase_combine_lora(nc, W, S, S["x1"], out)


def layouts(a):
    import numpy as np
    wide = lambda w: w.transpose(1, 0, 2).reshape(w.shape[1], -1)
    lay = {
        "x": a["L0_attn_x"],
        "w_qkvT_0": a["L0_attn_w_qkv"].T, "w_oT_0": a["L0_attn_w_o"].T,
        "w_qkv_1": a["L1_attn_w_qkv"], "w_out_1": a["L1_attn_w_out"],
        "b_qkv_0": a["L0_attn_b_qkv"], "b_qkv_1": a["L1_attn_b_qkv"],
        "b_o_0": a["L0_attn_b_o"], "b_o_1": a["L1_attn_b_out"],
        "W_Q": a["L0_ffn_W_Q"], "W_K": a["L0_ffn_W_K"], "W_invT": a["L0_ffn_W_inv"].T,
        "W_OT": a["L0_ffn_W_O"].T, "router_w1T": a["L0_ffn_router_w1"].T,
        "V_fwd": wide(a["L0_ffn_V_fwd"]), "W_fwd": wide(a["L0_ffn_W_fwd"]), "U_fwd": wide(a["L0_ffn_U_fwd"]),
        "V_inv": wide(a["L0_ffn_V_inv"]), "W_inv_exp": wide(a["L0_ffn_W_inv_exp"]),
        "U_inv": wide(a["L0_ffn_U_inv"]),
        "b_fwdT": a["L0_ffn_b_fwd"].T, "b_invT": a["L0_ffn_b_inv"].T,
        "router_b1": a["L0_ffn_router_b1"], "router_w2T": a["L0_ffn_router_w2"].T,
        "router_b2": a["L0_ffn_router_b2"], "expert_bias": a["L0_ffn_expert_bias"],
        "alpha": a["L0_ffn_alpha_bi"].reshape(1),
        "weightT": a["L1_ffn_weight"].T, "gateT": a["L1_ffn_gate_w"].T,
        "lora_UT": a["L1_ffn_lora_U"].reshape(E1 * R1, D).T,
        "lora_V": a["L1_ffn_lora_V"].transpose(0, 2, 1).reshape(E1 * R1, D),
    }
    return {k: np.ascontiguousarray(v) for k, v in lay.items()}


def kernel(**inputs):
    import numpy as np
    import concourse.bacc as bacc
    from concourse.bass_utils import run_bass_kernel_spmd

    nc = bacc.Bacc("TRN2", target_bir_lowering=False, num_devices=1)
    arrays, I = {}, {}
    for name, a in layouts({k: np.asarray(v) for k, v in inputs.items()}).items():
        arrays[f"in_{name}"] = a
        I[name] = nc.dram_tensor(f"in_{name}", a.shape, mybir.dt.from_np(a.dtype), kind="ExternalInput").ap()
    for pair in ("b_qkv", "b_o"):
        I[pair] = (I[f"{pair}_0"], I[f"{pair}_1"])
    out = nc.dram_tensor("out", (B, T, D), F32, kind="ExternalOutput").ap()
    recurrent_blocks(nc, I, out)
    r = run_bass_kernel_spmd(nc, [arrays], core_ids=[0])
    return r.results[0]["out"]
```

```python
from contextlib import ExitStack

import concourse.bass as bass
from concourse import mybir

F32 = mybir.dt.float32
F32R = mybir.dt.float32r
BF16 = mybir.dt.bfloat16
I32 = mybir.dt.int32
ALU = mybir.AluOpType
ACT = mybir.ActivationFunctionType
AX = mybir.AxisListType

P = 128
B, T, D, H = 2, 2048, 256, 16
C = D // H
DK = D // P
CH = 512
NCH = T // CH
TT = CH // P
KT = T // P
E, R = 8, 64
KR = E * R
E1, R1 = 8, 16
G = 4
NG = B * H // G
VW = 32
REACH = 64
WIN = P + 2 * REACH
TP = T + 2 * P
EPS = 1e-5
NEG = -1e30
ROWS = 6 * C
ROW_PAD = ROWS
ROW_M = ROWS + 1
NROWS = ROWS + 3
PART_ROWS = [(0, 0, 0), (C, 1, 0), (2 * C, 2, 0), (3 * C, 0, 1), (4 * C, 1, 1), (5 * C, 0, 2)]
ROW_TILE = 2 * G * TP // P
DMA = 16

ds = bass.ds


def wait_apart(eng, sem, value, passed):
    eng.wait_ge(sem, value)
    eng.sem_inc(passed, 1)


def f32(ap):
    return ap.bitcast(F32)


def split_matmul(nc, out, stationary, moving, n_k, start, stop):
    last = None
    passes = [(k, s, m) for k in range(n_k) for s, m in ((0, 0), (0, 1), (1, 0))]
    for n, (k, s, m) in enumerate(passes):
        last = nc.tensor.matmul(out, stationary(s, k), moving(m, k), start=start and n == 0,
                                stop=stop and n == len(passes) - 1, skip_group_check=True)
    return last


class Names:

    def __init__(self, nc, ctx, tag):
        self.nc, self.ctx, self.tag = nc, ctx, tag
        self.sems = []
        ctx.callback(self.release)

    def release(self):
        if self.sems:
            self.nc.clear_and_free_semaphores(self.sems)
            self.nc.all_engine_barrier()

    def sb(self, name, shape, dt=F32):
        return self.ctx.enter_context(self.nc.sbuf_tensor(f"{self.tag}_{name}", shape, dt))

    def ps(self, name, cols):
        return self.ctx.enter_context(self.nc.psum_tensor(f"{self.tag}_{name}", [P, cols], F32))

    def sem(self, name):
        sem = self.nc.alloc_semaphore(name=f"{self.tag}_{name}")
        self.sems.append(sem)
        return sem



def phase_weights(nc, W, I):
    with ExitStack() as ctx:
        n = Names(nc, ctx, "w")
        square = {k: n.sb(k, [P, DK, D]) for k in ("WQ", "WK", "WinvT", "W1T", "WOT", "WIQ", "WIK")}
        wide = {k: n.sb(k, [P, DK, KR]) for k in ("Vf", "Wf", "Vi", "Wi", "Uf", "Ui")}
        bT = n.sb("bT", [P, DK, 2 * E])
        raw_qkv = n.sb("raw_qkv", [P, 2, DK, 3 * D])
        raw_o = n.sb("raw_o", [P, 2, DK, D])
        raw_g = n.sb("raw_g", [P, DK, E1 + E1 * R1 + D])
        raw_v = n.sb("raw_v", [P, 1, D])
        pos = n.sb("pos", [P, KT], I32)
        posf = n.sb("posf", [P, KT])
        lb = n.sb("lb", [64, 2])
        bank = n.ps("bank", 8 * CH)
        loaded = n.sem("loaded")
        drawn = n.sem("drawn")
        product = n.sem("product")
        high = n.sem("high")
        low = n.sem("low")
        step = n.sem("step")

        loads = [(square["WQ"][:], I["W_Q"], DK), (square["WK"][:], I["W_K"], DK),
                 (square["WinvT"][:], I["W_invT"], DK), (square["W1T"][:], I["router_w1T"], DK),
                 (square["WOT"][:], I["W_OT"], DK),
                 (wide["Vf"][:], I["V_fwd"], DK), (wide["Wf"][:], I["W_fwd"], DK),
                 (wide["Vi"][:], I["W_inv_exp"], DK), (wide["Wi"][:], I["V_inv"], DK),
                 (wide["Uf"][:], I["U_fwd"], DK), (wide["Ui"][:], I["U_inv"], DK),
                 (bT[:, :, 0:E], I["b_fwdT"], DK), (bT[:, :, E:2 * E], I["b_invT"], DK),
                 (raw_qkv[:, 0], I["w_qkvT_0"], DK), (raw_qkv[:, 1], I["w_qkv_1"], DK),
                 (raw_o[:, 0], I["w_oT_0"], DK), (raw_o[:, 1], I["w_out_1"], DK),
                 (raw_g[:, :, 0:E1], I["gateT"], DK),
                 (raw_g[:, :, E1:E1 + E1 * R1], I["lora_UT"], DK),
                 (raw_g[:, :, E1 + E1 * R1:], I["weightT"], DK),
                 (raw_v[:], I["lora_V"], 1),
                 (W["w2"][:], I["router_w2T"], DK)]
        rows = [(W["bqk"][:, l, :], I["b_qkv"][l][0:2 * D].rearrange("(m p) -> p m", p=P)) for l in (0, 1)]
        rows += [(W["bv"][:, l, :], I["b_qkv"][l][2 * D:3 * D].unsqueeze(0).broadcast_to([P, D])) for l in (0, 1)]
        rows += [(W["bo"][:, l, :], I["b_o"][l].unsqueeze(0).broadcast_to([P, D])) for l in (0, 1)]
        rows += [(W["b1"][:], I["router_b1"].rearrange("(m p) -> p m", p=P))]
        rows += [(W["alpha"][:], I["alpha"].unsqueeze(0).broadcast_to([P, 1]))]
        rows += [(lb[32 * r:32 * r + E, j:j + 1], I[k].rearrange("(p o) -> p o", o=1))
                 for r in (0, 1) for j, k in enumerate(("router_b2", "expert_bias"))]
        n_loads = len(loads) + len(rows)

        WQ, WK, WIQ, WIK = (square[k] for k in ("WQ", "WK", "WIQ", "WIK"))

        block = ctx.enter_context(nc.Block())

        @block.sync
        def _(sp):
            for dst, src, k in loads:
                sp.dma_start(dst, src.rearrange("(k p) n -> p k n", p=P)).then_inc(loaded, DMA)

        @block.scalar
        def _(act):
            with nc.allow_non_contiguous_dma("biases, a few hundred bytes"):
                for dst, src in rows:
                    act.dma_start(dst, src).then_inc(loaded, DMA)
            for m, dst in ((0, WIQ), (1, WIK)):
                act.wait_ge(product, m + 1)
                nc.scalar.activation(dst[:].rearrange("p k n -> p (k n)"), bank[:, m * CH:(m + 1) * CH],
                                     ACT.Copy).then_inc(high, 1)
            for j in range(N_SPLIT):
                act.wait_ge(product, 3 + j)
                dst = split_target(W, j)
                nc.scalar.activation(dst(0), bank[:, (2 + j % 6) * CH:(3 + j % 6) * CH],
                                     ACT.Copy).then_inc(high, 1)
            act.wait_ge(product, 3 + N_SPLIT)
            nc.scalar.activation(W["bO"][:], bank[0:2 * E, 0:D], ACT.Copy).then_inc(high, 1)
            act.wait_ge(loaded, DMA * n_loads)
            for dst, src in plain_splits(W, raw_qkv, raw_o, raw_g, raw_v):
                nc.scalar.activation(dst(0), src, ACT.Copy).then_inc(high, 1)

        @block.tensor
        def _(pe):
            pe.wait_ge(loaded, DMA * n_loads)
            for m, src in ((0, WQ), (1, WK)):
                for t in range(DK):
                    for k in range(DK):
                        last = nc.tensor.matmul(bank[:, m * CH + t * D:m * CH + (t + 1) * D],
                                                square["WinvT"][:, k, t * P:(t + 1) * P], src[:, k, :],
                                                start=(k == 0), stop=(k == DK - 1), skip_group_check=True)
                last.then_inc(product, 1)
            pe.wait_ge(high, 2)
            j = 0
            for left, right in ((WQ, "Vf"), (WIQ, "Vi"), (WK, "Wf"), (WIK, "Wi")):
                for t in range(DK):
                    if j >= 6:
                        pe.wait_ge(low, j - 5)
                    for k in range(DK):
                        last = nc.tensor.matmul(bank[:, (2 + j % 6) * CH:(3 + j % 6) * CH],
                                                left[:, k, t * P:(t + 1) * P], wide[right][:, k, :],
                                                start=(k == 0), stop=(k == DK - 1))
                    last.then_inc(product, 1)
                    j += 1
            for t in range(DK):
                pe.wait_ge(low, j - 5)
                for r, left in enumerate((WQ, WIQ)):
                    for k in range(DK):
                        o = (2 + j % 6) * CH + r * D
                        last = nc.tensor.matmul(bank[:, o:o + D], left[:, k, t * P:(t + 1) * P],
                                                square["W1T"][:, k, :], start=(k == 0),
                                                stop=(k == DK - 1), skip_group_check=True)
                last.then_inc(product, 1)
                j += 1
            for half in range(4):
                u = wide["Uf" if half < 2 else "Ui"]
                pe.wait_ge(low, j - 5)
                for r in range(2):
                    m = 2 * (half % 2) + r
                    for k in range(DK):
                        o = (2 + j % 6) * CH + r * D
                        last = nc.tensor.matmul(bank[:, o:o + D], u[:, k, m * P:(m + 1) * P],
                                                square["WOT"][:, k, :], start=(k == 0),
                                                stop=(k == DK - 1), skip_group_check=True)
                last.then_inc(product, 1)
                j += 1
            for k in range(DK):
                last = nc.tensor.matmul(bank[0:2 * E, 0:D], bT[:, k, :], square["WOT"][:, k, :],
                                        start=(k == 0), stop=(k == DK - 1))
            last.then_inc(product, 1)

        @block.vector
        def _(dve):
            for j in range(N_SPLIT):
                dve.wait_ge(high, 3 + j)
                dst = split_target(W, j)
                nc.vector.tensor_tensor(dst(1), bank[:, (2 + j % 6) * CH:(3 + j % 6) * CH], f32(dst(0)),
                                        ALU.subtract).then_inc(low, 1)
            for i, (dst, src) in enumerate(plain_splits(W, raw_qkv, raw_o, raw_g, raw_v)):
                dve.wait_ge(high, 4 + N_SPLIT + i)
                nc.vector.tensor_tensor(dst(1), src, f32(dst(0)), ALU.subtract).then_inc(low, 1)
            dve.wait_ge(drawn, N_DRAWN)
            nc.vector.tensor_copy(posf[:], pos[:]).then_inc(step, 1)
            for name, value in (("ones_bf", 1.0), ("zeros_bf", 0.0), ("neg_bf", NEG)):
                nc.vector.memset(W[name][:], value).then_inc(step, 1)
            nc.vector.tensor_copy(W["mask_bf"][:], W["mask"][:]).then_inc(step, 1)
            for r in (0, 1):
                nc.vector.tensor_tensor(W["b2"][32 * r:32 * r + E, :], lb[32 * r:32 * r + E, 0:1],
                                        lb[32 * r:32 * r + E, 1:2], ALU.add).then_inc(step, 1)
            nc.vector.tensor_copy(W["ident_bf"][:], W["ident"][:]).then_inc(step, 1)
            dve.wait_ge(step, 1)
            nc.vector.reciprocal(W["inv_n"][:], posf[:]).then_inc(step, 1)

        @block.gpsimd
        def _(pool):
            pool.memset(W["ident"][:], 0.0).then_inc(drawn, 1)
            pool.memset(W["mask"][:], 0.0).then_inc(drawn, 1)
            pool.memset(W["ones"][:], 1.0).then_inc(drawn, 1)
            pool.memset(W["half"][:], -0.5).then_inc(drawn, 1)
            pool.iota(pos[:], [[P, KT]], base=1, channel_multiplier=1).then_inc(drawn, 1)
            pool.wait_ge(drawn, 5)
            pool.affine_select(out=W["ident"][:], in_=W["ident"][:], compare_op=ALU.not_equal, fill=1.0,
                               base=0, pattern=[[-1, P]], channel_multiplier=1).then_inc(drawn, 1)
            pool.affine_select(out=W["mask"][:], in_=W["mask"][:], compare_op=ALU.is_ge, fill=NEG,
                               base=0, pattern=[[1, WIN]], channel_multiplier=-1).then_inc(drawn, 1)
            pool.wait_ge(drawn, 7)
            pool.affine_select(out=W["mask"][:], in_=W["mask"][:], compare_op=ALU.is_ge, fill=NEG,
                               base=2 * REACH, pattern=[[-1, WIN]], channel_multiplier=1).then_inc(drawn, 1)


N_DRAWN = 8
N_SPLIT = 14


def split_target(W, j):
    if j < 8:
        name, branch, t = ("AQ" if j < 4 else "BK"), (j // 2) % 2, j % 2
        return lambda part: W[name][:, part, t, branch * KR:(branch + 1) * KR]
    if j < 10:
        return lambda part: W["RT"][:, part, j - 8, :]
    m = 2 * (j - 10)
    return lambda part: W["UO"][:, part, m:m + 2, :].rearrange("p m n -> p (m n)")


def plain_splits(W, raw_qkv, raw_o, raw_g, raw_v):
    out = []
    for l in (0, 1):
        out.append((lambda part, l=l: W[f"qkv{l}"][:, part], raw_qkv[:, l]))
        out.append((lambda part, l=l: W[f"o{l}"][:, part], raw_o[:, l]))
    out.append((lambda part: W["gate"][:, part], raw_g[:]))
    out.append((lambda part: W["loraV"][:, part], raw_v[:]))
    return out



def phase_project(nc, W, S, x_dram, layer):
    first = layer == 0
    NQ, NV = (2, 1) if first else (4, 2)
    with ExitStack() as ctx:
        n = Names(nc, ctx, f"p{layer}")
        stats = n.sb("stats", [P, 2, TT, 6])
        mean_var = n.sb("mean_var", [P, 2, TT, 2])
        var_eps = n.sb("var_eps", [P, 2, TT])
        rstd = n.sb("rstd", [P, 2, TT])
        xn = n.sb("xn", [P, 2, TT, D])
        xT = n.sb("xT", [P, 2, 2, DK, CH], F32R)
        cum = n.sb("cum", [P, DK, CH])
        carry = n.sb("carry", [P, 2, DK])
        cT = n.sb("cT", [P, 2, 2, DK, CH], F32R) if first else None
        parts = n.sb("parts", [P, 4, 3, CH], BF16)
        rest = n.sb("rest", [P, 2, CH])
        v_out = n.sb("v_out", [P, 2, TT, H, VW])
        gelu = n.sb("gelu", [P, 2, DK, CH]) if first else None
        logT = n.sb("logT", [64, CH]) if first else None
        ps_t = n.ps("ps_t", DK * CH)
        ps_qk = n.ps("ps_qk", NQ * CH)
        ps_v = n.ps("ps_v", NV * CH)
        ps_h = n.ps("ps_h", 2 * CH) if first else None
        ps_l = n.ps("ps_l", CH) if first else None

        x_loaded = [n.sem(f"x_loaded{u}") for u in range(2)]
        stat = n.sem("stat")
        eps_ready = n.sem("eps_ready")
        rstd_ready = n.sem("rstd_ready")
        xn_ready = n.sem("xn_ready")
        t_ready = n.sem("t_ready")
        t_high = n.sem("t_high")
        t_low = n.sem("t_low")
        cum_done = n.sem("cum_done")
        carry_done = n.sem("carry_done")
        c_high = n.sem("c_high")
        c_low = n.sem("c_low")
        qk_ready = n.sem("qk_ready")
        part1 = n.sem("part1")
        rest_ready = n.sem("rest_ready")
        part2 = n.sem("part2")
        part3 = n.sem("part3")
        v_ready = n.sem("v_ready")
        v_done = n.sem("v_done")
        v_clear = n.sem("v_clear")
        h_ready = n.sem("h_ready")
        gelu_done = n.sem("gelu_done")
        log_ready = n.sem("log_ready")
        logT_clear = n.sem("logT_clear")
        logT_done = n.sem("logT_done")
        lt_ready = n.sem("lt_ready")
        log_done = n.sem("log_done")
        xn_stored = [n.sem(f"xn_stored{u}") for u in range(2)]
        passed = n.sem("passed")
        stored = [n.sem(f"stored{u}") for u in range(2)]
        v_stored = [n.sem(f"v_stored{u}") for u in range(2)]
        parts_stored = [n.sem(f"parts_stored{m}") for m in range(4)]
        chunk_stores = DMA * 2 * DK * (2 if first else 1)
        t_read = cum_done if first else t_low
        t_low_seed, cum_seed = (0, DK) if first else (DK, 0)

        block = ctx.enter_context(nc.Block())

        def load(sp, i, u):
            c = 2 * i + u
            if not isinstance(c, int) or c > 1:
                wait_apart(sp, t_ready, c - 1, passed)
                if first:
                    wait_apart(sp, xn_stored[u], DMA * i, passed)
            sp.dma_start(xn[:, u], x_dram[u, ds(i * CH, CH), :].rearrange("(t p) d -> p t d", p=P)
                         ).then_inc(x_loaded[u], DMA)

        def store_xn(sp, i, u):
            if first:
                wait_apart(sp, xn_ready, TT * (2 * i + u + 1), passed)
                sp.dma_start(S["xn"][u, ds(i * CH, CH), :].rearrange("(t p) d -> p t d", p=P), xn[:, u]
                             ).then_inc(xn_stored[u], DMA)

        def store_turned(sp, i, u):
            c = 2 * i + u
            tok = ds(i * CH, CH)
            wait_apart(sp, t_low, t_low_seed + DK * (c + 1), passed)
            for part in range(2):
                for k in range(DK):
                    sp.dma_start(S["xT"][u, part, k, :, tok], f32(xT[:, u, part, k, :])
                                 ).then_inc(stored[u], DMA)
            if first:
                wait_apart(sp, c_low, DK * (c + 1), passed)
                for part in range(2):
                    for k in range(DK):
                        sp.dma_start(S["cT"][u, part, k, :, tok], f32(cT[:, u, part, k, :])
                                     ).then_inc(stored[u], DMA)

        def store_parts(sp, i, u):
            c = 2 * i + u
            tok = ds(i * CH, CH)
            for m in range(4):
                wait_apart(sp, part3, 2 + 4 * c + m + 1, passed)
                sp.dma_start(S["parts"][m // 2, u, :, (m % 2) * P:(m % 2 + 1) * P, tok].rearrange("a p t -> p a t"),
                             parts[:, m]).then_inc(parts_stored[m], DMA)

        def store_values(sp, i, u):
            c = 2 * i + u
            wait_apart(sp, v_done, NV + 2 * (c + 1), passed)
            for t in range(TT):
                sp.dma_start(S["v"][u, :, :, ds(i * TT + t, 1), :].rearrange("g p o n -> p g (o n)"),
                             v_out[:, u, t].rearrange("p (g h) w -> p g (h w)", g=H // G)
                             ).then_inc(v_stored[u], DMA)

        @block.sync
        def _(sp):
            for u in range(2):
                sp.sem_inc(stored[u], chunk_stores)
                sp.sem_inc(v_stored[u], DMA * TT)
            for m in range(4):
                sp.sem_inc(parts_stored[m], DMA)
            load(sp, 0, 0)
            load(sp, 0, 1)
            store_xn(sp, 0, 0)
            store_turned(sp, 0, 0)

            def chunk_pair(i, more):
                for u in range(2):
                    after = (i, 1) if u == 0 else (i + 1, 0) if more else None
                    if more:
                        load(sp, i + 1, u)
                    if after:
                        store_xn(sp, *after)
                    store_parts(sp, i, u)
                    if after:
                        store_turned(sp, *after)
                    store_values(sp, i, u)

            with sp.Fori(0, NCH - 1) as i:
                chunk_pair(i, True)
            chunk_pair(NCH - 1, False)
            for u in range(2):
                wait_apart(sp, stored[u], chunk_stores * (NCH + 1), passed)
                wait_apart(sp, v_stored[u], DMA * TT * (NCH + 1), passed)
                if first:
                    wait_apart(sp, xn_stored[u], DMA * NCH, passed)
            for m in range(4):
                wait_apart(sp, parts_stored[m], DMA * (2 * NCH + 1), passed)

        @block.gpsimd
        def _(pool):
            def third_parts(i, u):
                for m in range(4):
                    pool.wait_ge(part2, 4 * (2 * i + u) + m + 1)
                    pool.tensor_tensor(parts[:, m, 2, :], rest[:, m % 2, :], parts[:, m, 1, :],
                                       ALU.subtract).then_inc(part3, 1)

            def inverse_root(c, u):
                pool.wait_ge(eps_ready, c + 1)
                pool.tensor_tensor(rstd[:, u], var_eps[:, u], W["half"][:, 0:TT], ALU.pow
                                   ).then_inc(rstd_ready, 1)

            pool.sem_inc(part3, 2)
            inverse_root(0, 0)
            inverse_root(1, 1)
            with pool.Fori(0, NCH - 1) as i:
                for u in range(2):
                    third_parts(i, u)
                    inverse_root(2 * i + 2 + u, u)
            third_parts(NCH - 1, 0)
            third_parts(NCH - 1, 1)

        @block.vector
        def _(dve):
            def statistics(i, u):
                c = 2 * i + u
                dve.wait_ge(x_loaded[u], DMA * (i + 1))
                for t in range(TT):
                    nc.vector.bn_stats(stats[:, u, t], xn[:, u, t]).then_inc(stat, 1)
                wait_apart(dve, stat, (TT + 1) * c + TT, passed)
                for t in range(TT):
                    last = nc.vector.bn_aggr(mean_var[:, u, t], stats[:, u, t])
                last.then_inc(stat, 1)
                dve.wait_ge(stat, (TT + 1) * (c + 1))
                nc.vector.tensor_scalar(var_eps[:, u], mean_var[:, u, :, 1], EPS, None, ALU.add
                                        ).then_inc(eps_ready, 1)

            def normalise(i, u):
                c = 2 * i + u
                dve.wait_ge(rstd_ready, c + 1)
                for t in range(TT):
                    nc.vector.tensor_scalar(xn[:, u, t], xn[:, u, t], mean_var[:, u, t, 0:1],
                                            rstd[:, u, t:t + 1], ALU.subtract, ALU.mult).then_inc(xn_ready, 1)

            def transposed(i, u):
                c = 2 * i + u
                if first:
                    dve.wait_ge(carry_done, c + 1)
                    if not isinstance(c, int) or c > 0:
                        dve.wait_ge(c_low, DK * c)
                for k in range(DK):
                    dve.wait_ge(t_high, DK * c + k + 1)
                    nc.vector.tensor_tensor(xT[:, u, 1, k, :], ps_t[:, k * CH:(k + 1) * CH],
                                            f32(xT[:, u, 0, k, :]), ALU.subtract).then_inc(t_low, 1)
                    if first:
                        nc.vector.tensor_tensor_scan(cum[:, k, :], W["ones"][:, 0:CH],
                                                     ps_t[:, k * CH:(k + 1) * CH], carry[:, u, k:k + 1],
                                                     ALU.mult, ALU.add).then_inc(cum_done, 1)
                if first:
                    dve.wait_ge(cum_done, cum_seed + DK * (c + 1))
                    nc.vector.tensor_copy(carry[:, u, :], cum[:, :, CH - 1]).then_inc(carry_done, 1)
                    for k in range(DK):
                        dve.wait_ge(c_high, DK * c + k + 1)
                        nc.vector.tensor_tensor(cT[:, u, 1, k, :], cum[:, k, :], f32(cT[:, u, 0, k, :]),
                                                ALU.subtract).then_inc(c_low, 1)

            def rests(i, u, ms):
                for m in ms:
                    j = 4 * (2 * i + u) + m
                    dve.wait_ge(part1, j + 1)
                    dve.wait_ge(part3, j + 1)
                    nc.vector.scalar_tensor_tensor(rest[:, m % 2, :], ps_qk[:, (m % NQ) * CH:(m % NQ + 1) * CH],
                                                   W["bqk"][:, layer, m:m + 1], parts[:, m, 0, :],
                                                   ALU.add, ALU.subtract).then_inc(rest_ready, 1)

            def values(i, u):
                for half in range(2):
                    dve.wait_ge(v_ready, 2 * (2 * i + u) + half + 1)
                    if half == 0:
                        dve.wait_ge(v_stored[u], DMA * TT * (i + 1))
                    nc.vector.tensor_tensor(
                        v_out[:, u, 2 * half:2 * half + 2, :, 0:C],
                        ps_v[:, (half % NV) * CH:(half % NV + 1) * CH].rearrange(
                            "p (t h c) -> p t h c", t=2, c=C),
                        W["bv"][:, layer].rearrange("p (h c) -> p h c", c=C).unsqueeze(1)
                        .broadcast_to([P, 2, H, C]), ALU.add).then_inc(v_done, 1)

            def logits(i, u):
                c = 2 * i + u
                dve.wait_ge(lt_ready, 1 + c + 1)
                for r in range(2):
                    last = nc.vector.tensor_copy(
                        W["logits"][:, u, ds(i * TT, TT), r, :],
                        ps_l[:].rearrange("p (t n) -> p t n", t=TT)[:, :, 32 * r:32 * r + E])
                last.then_inc(log_done, 1)

            def chunk_pair(i, more):
                for u in range(2):
                    after = (i, 1) if u == 0 else (i + 1, 0) if more else None
                    rests(i, u, (0, 1))
                    if after:
                        normalise(*after)
                    rests(i, u, (2, 3))
                    if after:
                        transposed(*after)
                    values(i, u)
                    if more:
                        statistics(i + 1, u)
                    if first:
                        logits(i, u)

            dve.sem_inc(t_read, DK)
            dve.sem_inc(rest_ready, NQ)
            dve.sem_inc(v_done, NV)
            dve.sem_inc(log_done, 1)
            nc.vector.memset(v_out[:], 1.0).then_inc(v_clear, 1)
            dve.wait_ge(v_clear, 1)
            if first:
                nc.vector.memset(carry[:], 0.0).then_inc(carry_done, 1)
            statistics(0, 0)
            statistics(0, 1)
            normalise(0, 0)
            transposed(0, 0)
            with dve.Fori(0, NCH - 1) as i:
                chunk_pair(i, True)
            chunk_pair(NCH - 1, False)

        @block.scalar
        def _(act):
            def turned(i, u):
                c = 2 * i + u
                act.wait_ge(stored[u], chunk_stores * (i + 1))
                for k in range(DK):
                    act.wait_ge(t_ready, c + 1)
                    nc.scalar.activation(xT[:, u, 0, k, :], ps_t[:, k * CH:(k + 1) * CH], ACT.Copy
                                         ).then_inc(t_high, 1)
                if first:
                    for k in range(DK):
                        act.wait_ge(cum_done, cum_seed + DK * c + k + 1)
                        nc.scalar.activation(cT[:, u, 0, k, :], cum[:, k, :], ACT.Copy).then_inc(c_high, 1)

            def chunk(i, u):
                c = 2 * i + u
                for m in range(4):
                    j = 4 * c + m
                    act.wait_ge(qk_ready, j + 1)
                    act.wait_ge(parts_stored[m], DMA * (c + 1))
                    nc.scalar.activation(parts[:, m, 0, :], ps_qk[:, (m % NQ) * CH:(m % NQ + 1) * CH],
                                         ACT.Identity, bias=W["bqk"][:, layer, m:m + 1]).then_inc(part1, 1)
                    act.wait_ge(rest_ready, NQ + j + 1)
                    nc.scalar.activation(parts[:, m, 1, :], rest[:, m % 2, :], ACT.Copy).then_inc(part2, 1)

            def router(i, u):
                c = 2 * i + u
                for r in range(2):
                    for m in range(DK):
                        act.wait_ge(h_ready, 4 * c + 2 * r + m + 1)
                        o = (m % 2) * CH
                        nc.scalar.activation(gelu[:, r, m, :], ps_h[:, o:o + CH], ACT.Gelu,
                                             bias=W["b1"][:, m:m + 1]).then_inc(gelu_done, 1)
                act.wait_ge(log_ready, c + 1)
                act.wait_ge(lt_ready, c + 1)
                for r in range(2):
                    last = nc.scalar.activation(logT[32 * r:32 * r + E, :], ps_l[32 * r:32 * r + E, :],
                                                ACT.Identity, bias=W["b2"][32 * r:32 * r + E, :])
                    last.then_inc(logT_done, 1)

            act.sem_inc(gelu_done, 2)
            if first:
                nc.scalar.activation(logT[:], W["ones"][0:64, 0:CH], ACT.Copy).then_inc(logT_clear, 1)
                act.wait_ge(logT_clear, 1)

            def chunk_pair(i, more):
                for u in range(2):
                    chunk(i, u)
                    if u == 0:
                        turned(i, 1)
                    elif more:
                        turned(i + 1, 0)
                    if first:
                        router(i, u)

            turned(0, 0)
            with act.Fori(0, NCH - 1) as i:
                chunk_pair(i, True)
            chunk_pair(NCH - 1, False)

        @block.tensor
        def _(pe):
            def transposes(i, u):
                c = 2 * i + u
                pe.wait_ge(xn_ready, TT * (c + 1))
                pe.wait_ge(t_read, DK * (c + 1))
                for k in range(DK):
                    for t in range(TT):
                        last = nc.tensor.transpose(ps_t[:, k * CH + t * P:k * CH + (t + 1) * P],
                                                   xn[:, u, t, k * P:(k + 1) * P], W["ident"][:])
                last.then_inc(t_ready, 1)

            def queries_keys(i, u):
                c = 2 * i + u
                pe.wait_ge(t_low, t_low_seed + DK * (c + 1))
                w = W[f"qkv{layer}"]
                for m in range(4):
                    pe.wait_ge(rest_ready, 4 * c + m + 1)
                    split_matmul(nc, ps_qk[:, (m % NQ) * CH:(m % NQ + 1) * CH],
                                 lambda s, k: w[:, s, k, m * P:(m + 1) * P],
                                 lambda s, k: xT[:, u, s, k, :], DK, True, True).then_inc(qk_ready, 1)

            def values(i, u, half):
                c = 2 * i + u
                w = W[f"qkv{layer}"]
                pe.wait_ge(v_done, 2 * c + half + 1)
                for t in range(2):
                    tok = (2 * half + t) * P
                    o = (half % NV) * CH + t * D
                    last = split_matmul(nc, ps_v[:, o:o + D], lambda s, k: xT[:, u, s, k, tok:tok + P],
                                        lambda s, k: w[:, s, k, 2 * D:3 * D], DK, True, True)
                last.then_inc(v_ready, 1)

            def router_hidden(i, u):
                c = 2 * i + u
                for r in range(2):
                    for m in range(DK):
                        pe.wait_ge(gelu_done, 4 * c + 2 * r + m + 1)
                        split_matmul(nc, ps_h[:, m * CH:(m + 1) * CH],
                                     lambda s, k: W["RT"][:, s, k, r * D + m * P:r * D + (m + 1) * P],
                                     lambda s, k: xT[:, u, s, k, :], DK, True, True).then_inc(h_ready, 1)

            def router_logits(i, u):
                c = 2 * i + u
                pe.wait_ge(gelu_done, 2 + 4 * (c + 1))
                pe.wait_ge(log_done, c + 1)
                for m in range(DK):
                    for r in range(2):
                        last = nc.tensor.matmul(ps_l[32 * r:32 * r + E, :], W["w2"][:, m, :], gelu[:, r, m, :],
                                                start=(m == 0), stop=(m == DK - 1), skip_group_check=True)
                last.then_inc(log_ready, 1)
                wait_apart(pe, logT_done, 2 * (c + 1), passed)
                for t in range(TT):
                    last = nc.tensor.transpose(ps_l[:, t * P:t * P + 64], logT[:, t * P:(t + 1) * P],
                                               W["ident"][0:64, 0:64])
                last.then_inc(lt_ready, 1)

            pe.sem_inc(lt_ready, 1)

            def chunk_pair(i, more):
                for u in range(2):
                    queries_keys(i, u)
                    if u == 0:
                        transposes(i, 1)
                    elif more:
                        transposes(i + 1, 0)
                    values(i, u, 0)
                    if first:
                        router_hidden(i, u)
                    values(i, u, 1)
                    if first:
                        router_logits(i, u)

            transposes(0, 0)
            with pe.Fori(0, NCH - 1) as i:
                chunk_pair(i, True)
            chunk_pair(NCH - 1, False)



def load_group(sp, K, Q, S, kq_loaded, g, par, k_cols, k_off):
    b, f0 = g // NG2, (g % NG2) * G * C
    for row, k_part, q_part in PART_ROWS:
        def rows_of(which, part, t0, n):
            return S["parts"][which, ds(b, 1), part, ds(f0, G * C), t0:t0 + n].rearrange(
                "o (h c) t -> c (o h) t", h=G)
        dst = K[row:row + C, ds(par * (G * k_cols), G * k_cols)].rearrange("c (h t) -> c h t", h=G)
        sp.dma_start(dst[:, :, k_off:k_off + T], rows_of(1, k_part, 0, T)).then_inc(kq_loaded, DMA)
        for qc in range(NCH):
            dst = Q[row:row + C, ds(par * (G * T) + qc * G * CH, G * CH)]
            sp.dma_start(dst.rearrange("c (h t) -> c h t", h=G), rows_of(0, q_part, qc * CH, CH)
                         ).then_inc(kq_loaded, DMA)


def constant_rows(act, K, Q, W, rows_set, zeros_set):
    def fill(row, const, sem):
        act.dma_start(row, W[const][:, 0:row.shape[-1] // P]).then_inc(sem, DMA)

    fill(K[ROW_PAD:ROW_PAD + 1, :], "zeros_bf", zeros_set)
    fill(K[ROW_M:ROW_M + 1, :], "ones_bf", rows_set)
    fill(K[ROW_M + 1:ROW_M + 2, :], "ones_bf", rows_set)
    fill(Q[ROW_PAD:ROW_PAD + 1, :], "ones_bf", rows_set)


CONST_ROWS = 3
GROUP_LOADS = len(PART_ROWS) * (1 + NCH)
NG2 = NG // B
NIT = NG * NCH


def phase_attend_full(nc, W, S):
    scale = 1.0 / D ** 0.5
    NS = 2 * KT
    NA = G * TT * (T // CH)
    RING = 3
    SLOT_M, SLOT_O = 6, 14
    slot_of = [k for k in range(NA + 2) if k not in (SLOT_M, SLOT_O)]
    assert (NA + 2) % RING == 0
    bank_of = lambda slot: (slot % RING) * CH
    pieces_to = lambda slot: sum(1 for x in slot_of if x <= slot) if slot >= 0 else slot + 1
    with ExitStack() as ctx:
        n = Names(nc, ctx, "a0")
        K = n.sb("K", [NROWS, 2 * G * T], BF16)
        Q = n.sb("Q", [NROWS, 2 * G * T], BF16)
        V = n.sb("V", [P, KT, G * VW])
        prob = n.sb("prob", [P, 4, 2 * CH])
        maxes = n.sb("maxes", [P, NA])
        neg_max = n.sb("neg_max", [P, G * TT])
        m_parts = n.sb("m_parts", [G * TT, 2, P], BF16)
        oT = n.sb("oT", [P, CH])
        recip = n.sb("recip", [P, TT, G])
        o_out = n.sb("o_out", [P, TT, G, C])
        ps_a = n.ps("ps_a", RING * CH)
        ps_s = n.ps("ps_s", 4 * CH)
        ps_o = n.ps("ps_o", CH)

        passed = n.sem("passed")
        rows_set = n.sem("rows_set")
        zeros_set = n.sem("zeros_set")
        kq_loaded = n.sem("kq_loaded")
        v_loaded = [n.sem(f"v_loaded{q}") for q in range(4)]
        a_ready = n.sem("a_ready")
        a_done = n.sem("a_done")
        nm_ready = n.sem("nm_ready")
        mT_ready = n.sem("mT_ready")
        m_high = n.sem("m_high")
        m_low = n.sem("m_low")
        m_loaded = n.sem("m_loaded")
        s_ready = n.sem("s_ready")
        exp_done = n.sem("exp_done")
        pv_done = n.sem("pv_done")
        oT_ready = n.sem("oT_ready")
        o_turned = n.sem("o_turned")
        o_recip = n.sem("o_recip")
        o_done = n.sem("o_done")
        o_stored = n.sem("o_stored")
        out_clear = n.sem("out_clear")

        block = ctx.enter_context(nc.Block())

        def load_v(sp, g, q):
            sp.dma_start(V[:, 4 * q:4 * q + 4, :],
                         S["v"][ds(g // NG2, 1), ds(g % NG2, 1), :, 4 * q:4 * q + 4, :]
                         .rearrange("a b p t n -> p (a b t) n")).then_inc(v_loaded[q], DMA)

        @block.sync
        def _(sp):
            load_group(sp, K, Q, S, kq_loaded, 0, 0, T, 0)
            for q in range(4):
                load_v(sp, 0, q)
            wait_apart(sp, kq_loaded, GROUP_LOADS * DMA, passed)
            load_group(sp, K, Q, S, kq_loaded, 1, 1, T, 0)

            def values(g):
                for q in range(4):
                    wait_apart(sp, pv_done, 2 + KT * (NCH * g - 1) + 4 * (q + 1), passed)
                    load_v(sp, g, q)

            with sp.Fori(1, NG - 1) as g:
                values(g)
                wait_apart(sp, kq_loaded, GROUP_LOADS * DMA * (g + 1), passed)
                load_group(sp, K, Q, S, kq_loaded, g + 1, (g + 1) % 2, T, 0)
            values(NG - 1)

        @block.gpsimd
        def _(pool):
            def store_maxima(c):
                pool.wait_ge(m_low, c + 1)
                for part in range(2):
                    pool.dma_start(Q[ROW_M + part:ROW_M + part + 1, ds((c % (2 * NCH)) * (G * CH), G * CH)],
                                   m_parts[:, part, :]).then_inc(m_loaded, DMA)

            def store_output(it):
                pool.wait_ge(o_done, 1 + it + 1)
                pool.dma_start(S["att"][ds(it, 1)].rearrange("o (a p) c -> p (o a) c", p=P),
                               o_out[:].rearrange("p a h c -> p a (h c)")).then_inc(o_stored, DMA)

            pool.memset(o_out[:], 1.0).then_inc(out_clear, 1)
            pool.wait_ge(out_clear, 1)
            pool.dma_start(S["att"][0:1].rearrange("o (a p) c -> p (o a) c", p=P),
                           o_out[:].rearrange("p a h c -> p a (h c)")).then_inc(o_stored, DMA)
            store_maxima(0)
            with pool.Fori(0, NIT - 1) as it:
                store_maxima(it + 1)
                store_output(it)
            store_output(NIT - 1)
            store_output(NIT)
            pool.wait_ge(o_stored, DMA * (NIT + 2))

        @block.vector
        def _(dve):
            def split_maxima(c):
                dve.wait_ge(mT_ready, c + 1)
                if not isinstance(c, int) or c > 0:
                    dve.wait_ge(m_loaded, 2 * DMA * c)
                turned = ps_a[0:G * TT, bank_of(SLOT_M):bank_of(SLOT_M) + P]
                nc.vector.tensor_copy(m_parts[:, 0, :], turned).then_inc(m_high, 1)
                dve.wait_ge(m_high, c + 1)
                nc.vector.tensor_tensor(m_parts[:, 1, :], turned, m_parts[:, 0, :], ALU.subtract
                                        ).then_inc(m_low, 1)

            def maxima(c, lo, hi):
                if lo == 0 and (not isinstance(c, int) or c > 0):
                    dve.wait_ge(nm_ready, c)
                for k in range(lo, hi):
                    dve.wait_ge(a_ready, NA * c + k + 1)
                    o = bank_of(slot_of[k])
                    nc.vector.tensor_reduce(maxes[:, k:k + 1], ps_a[:, o:o + CH], AX.X, ALU.max
                                            ).then_inc(a_done, 1)

            def whole_maxima(c):
                dve.wait_ge(a_done, RING + NA * (c + 1))
                if not isinstance(c, int) or c > 0:
                    dve.wait_ge(mT_ready, c)
                nc.vector.tensor_reduce(neg_max[:], maxes[:].rearrange("p (q k) -> p q k", k=T // CH),
                                        AX.X, ALU.max, negate=True).then_inc(nm_ready, 1)

            def normalise(it):
                dve.wait_ge(o_turned, it + 1)
                turned = ps_a[:, bank_of(SLOT_O):bank_of(SLOT_O) + CH].rearrange(
                    "p (a h w) -> p a h w", a=TT, h=G)
                nc.vector.reciprocal(recip[:], turned[:, :, :, C]).then_inc(o_recip, 1)
                dve.wait_ge(o_recip, it + 1)
                dve.wait_ge(o_stored, DMA * (it + 1))
                nc.vector.tensor_tensor(o_out[:], turned[:, :, :, 0:C],
                                        recip[:].unsqueeze(3).broadcast_to([P, TT, G, C]), ALU.mult
                                        ).then_inc(o_done, 1)

            dve.sem_inc(a_done, RING)
            dve.sem_inc(o_done, 1)
            maxima(0, 0, NA)
            whole_maxima(0)
            maxima(1, 0, SLOT_M)
            split_maxima(0)
            maxima(1, SLOT_M, NA)
            whole_maxima(1)
            with dve.Fori(0, NIT - 2) as it:
                maxima(it + 2, 0, SLOT_M)
                split_maxima(it + 1)
                maxima(it + 2, SLOT_M, SLOT_O - 1)
                normalise(it)
                maxima(it + 2, SLOT_O - 1, NA)
                whole_maxima(it + 2)
            split_maxima(NIT - 1)
            for it in (NIT - 2, NIT - 1, NIT):
                normalise(it)

        @block.scalar
        def _(act):
            def iteration(it):
                for j in range(NS):
                    act.wait_ge(s_ready, NS * it + j + 1)
                    if j % 2 == 0:
                        act.wait_ge(pv_done, KT * it + j // 2 + 1)
                    nc.scalar.activation(prob[:, j % 4, :], ps_s[:, (j % 2) * 2 * CH:(j % 2 + 1) * 2 * CH],
                                         ACT.Exp, scale=scale).then_inc(exp_done, 1)
                act.wait_ge(pv_done, 2 + KT * (it + 1))
                act.wait_ge(o_turned, it + 1)
                nc.scalar.activation(oT[:], ps_o[:], ACT.Copy).then_inc(oT_ready, 1)

            constant_rows(act, K, Q, W, rows_set, zeros_set)
            act.sem_inc(exp_done, 2)
            nc.scalar.activation(oT[:], W["ones"][:], ACT.Copy).then_inc(oT_ready, 1)
            with act.Fori(0, NIT) as it:
                iteration(it)

        @block.tensor
        def _(pe):
            def bank_free(c, slot):
                if isinstance(c, int) and c >= NIT:
                    pe.wait_ge(a_done, RING + NA * NIT)
                else:
                    pe.wait_ge(a_done, RING + NA * c + pieces_to(slot - RING))

            def maximum_scores(c, k, turned=True):
                h, qt, kc = k // (TT * NCH), (k // NCH) % TT, k % NCH
                half = ((c // NCH) % 2) * (G * T)
                q0 = (c % (2 * NCH)) * (G * CH) + h * CH + qt * P
                k0 = half + h * T + kc * CH
                o = bank_of(slot_of[k])
                bank_free(c, slot_of[k])
                if turned and slot_of[k] == SLOT_M + RING:
                    pe.wait_ge(m_low, c)
                if turned and slot_of[k] == SLOT_O + RING:
                    pe.wait_ge(o_done, c)
                nc.tensor.matmul(ps_a[:, o:o + CH], Q[0:ROW_M, ds(q0, P)],
                                 K[0:ROW_M, ds(k0, CH)], start=True, stop=True).then_inc(a_ready, 1)

            def turn_maxima(c, slot_chunk):
                pe.wait_ge(nm_ready, c + 1)
                if slot_chunk is not None:
                    bank_free(slot_chunk, SLOT_M)
                nc.tensor.transpose(ps_a[0:G * TT, bank_of(SLOT_M):bank_of(SLOT_M) + P], neg_max[:],
                                    W["ident"][:]).then_inc(mT_ready, 1)

            def turn_output(it):
                pe.wait_ge(oT_ready, it + 1)
                bank_free(it + 2, SLOT_O)
                pe.wait_ge(o_done, it + 1)
                for a in range(TT):
                    o = bank_of(SLOT_O) + a * P
                    last = nc.tensor.transpose(ps_a[:, o:o + P], oT[:, a * P:(a + 1) * P],
                                               W["ident"][:])
                last.then_inc(o_turned, 1)

            def scores(it, j):
                half = ((it // NCH) % 2) * (G * T)
                pe.wait_ge(exp_done, NS * it + j + 1)
                for r in range(2):
                    h = 2 * (j % 2) + r
                    last = nc.tensor.matmul(
                        ps_s[:, (2 * (j % 2) + r) * CH:(2 * (j % 2) + r + 1) * CH],
                        K[:, ds(half + h * T + (j // 2) * P, P)],
                        Q[:, ds((it % (2 * NCH)) * (G * CH) + h * CH, CH)], start=True, stop=True)
                last.then_inc(s_ready, 1)

            def add_values(it, kt):
                if kt % 4 == 0:
                    pe.wait_ge(v_loaded[kt // 4], DMA * (it // NCH + 1))
                if kt == 0:
                    pe.wait_ge(oT_ready, it + 1)
                pe.wait_ge(exp_done, 2 + NS * it + 2 * kt + 2)
                for h in range(G):
                    slot = (2 * kt + h // 2) % 4
                    last = nc.tensor.matmul(ps_o[h * VW:(h + 1) * VW, :], V[:, kt, h * VW:(h + 1) * VW],
                                            prob[:, slot, (h % 2) * CH:(h % 2 + 1) * CH],
                                            start=(kt == 0), stop=(kt == KT - 1), skip_group_check=True)
                last.then_inc(pv_done, 1)

            def iteration(it, more, turn):
                slots = iter(range(NA + 2))

                def turns(n):
                    for _ in range(n):
                        slot = next(slots)
                        if slot == SLOT_M:
                            if turn:
                                turn_maxima(it + 1, it + 2)
                        elif slot == SLOT_O:
                            turn_output(it)
                        elif more:
                            maximum_scores(it + 2, slot_of.index(slot))

                if more:
                    pe.wait_ge(kq_loaded, GROUP_LOADS * DMA * ((it + 2) // NCH + 1))
                pe.wait_ge(m_loaded, 2 * DMA * (it + 1))
                for kt in range(KT):
                    scores(it, 2 * kt)
                    turns(2 if kt in (1, 3) else 1)
                    scores(it, 2 * kt + 1)
                    turns(2)
                    if kt > 0:
                        add_values(it, kt - 1)
                    turns(1)
                add_values(it, KT - 1)

            pe.sem_inc(pv_done, 2)
            pe.wait_ge(rows_set, CONST_ROWS * DMA)
            pe.wait_ge(zeros_set, DMA)
            pe.wait_ge(kq_loaded, GROUP_LOADS * DMA)
            for k in range(NA):
                maximum_scores(0, k, False)
            for k in range(NA):
                if slot_of[k] == SLOT_M + 1:
                    turn_maxima(0, 1)
                maximum_scores(1, k, False)
                if slot_of[k] == SLOT_M + RING - 1:
                    pe.wait_ge(m_low, 1)
            with pe.Fori(0, NIT - 2) as it:
                iteration(it, True, True)
            iteration(NIT - 2, False, True)
            iteration(NIT - 1, False, False)
            turn_output(NIT)



def phase_attend_band(nc, W, S):
    scale = 1.0 / C ** 0.5
    GK, GQ = G * TP, G * T
    TILES = [(kt, max(0, kt * P - REACH), min(CH, kt * P - REACH + WIN)) for kt in range(-1, TT + 1)]
    NS = len(TILES)
    PROBS = 3
    assert NS % PROBS == 0
    NCHUNKS = NG * NCH
    with ExitStack() as ctx:
        n = Names(nc, ctx, "a1")
        K = n.sb("K", [NROWS, 2 * GK], BF16)
        Q = n.sb("Q", [NROWS, 2 * GQ], BF16)
        V = n.sb("V", [P, KT + 2, G * VW])
        prob = n.sb("prob", [P, PROBS, G, WIN])
        masked = n.sb("masked", [P, 4, WIN])
        maxes = n.sb("maxes", [P, G * TT])
        neg_max = n.sb("neg_max", [P, G * TT])
        m_parts = n.sb("m_parts", [G * TT, 2, P], BF16)
        oT = n.sb("oT", [P, CH])
        recip = n.sb("recip", [P, TT, G])
        o_out = n.sb("o_out", [P, TT, G, C])
        ps_a = n.ps("ps_a", 2 * CH)
        ps_s = n.ps("ps_s", 4 * CH)
        ps_o = n.ps("ps_o", CH)
        ps_m = n.ps("ps_m", CH)

        passed = n.sem("passed")
        rows_set = n.sem("rows_set")
        zeros_set = n.sem("zeros_set")
        pads_set = n.sem("pads_set")
        kq_loaded = n.sem("kq_loaded")
        v_loaded = [n.sem(f"v_loaded{q}") for q in range(4)]
        a_ready = n.sem("a_ready")
        a_done = n.sem("a_done")
        nm_ready = n.sem("nm_ready")
        mT_ready = n.sem("mT_ready")
        m_high = n.sem("m_high")
        m_low = n.sem("m_low")
        m_loaded = n.sem("m_loaded")
        s_ready = n.sem("s_ready")
        exp_done = n.sem("exp_done")
        pv_done = n.sem("pv_done")
        oT_ready = n.sem("oT_ready")
        o_turned = n.sem("o_turned")
        o_recip = n.sem("o_recip")
        o_done = n.sem("o_done")
        o_stored = n.sem("o_stored")
        out_clear = n.sem("out_clear")

        block = ctx.enter_context(nc.Block())

        def load_v(sp, g, q):
            sp.dma_start(V[:, 1 + 4 * q:5 + 4 * q, :],
                         S["v"][ds(g // NG2, 1), ds(g % NG2, 1), :, 4 * q:4 * q + 4, :]
                         .rearrange("a b p t n -> p (a b t) n")).then_inc(v_loaded[q], DMA)

        @block.sync
        def _(sp):
            load_group(sp, K, Q, S, kq_loaded, 0, 0, TP, P)
            for q in range(4):
                load_v(sp, 0, q)
            wait_apart(sp, kq_loaded, GROUP_LOADS * DMA, passed)
            load_group(sp, K, Q, S, kq_loaded, 1, 1, TP, P)

            def values(g):
                for q in range(4):
                    wait_apart(sp, pv_done, PROBS + NS * (NCH * (g - 1) + min(q + 1, NCH - 1) + 1), passed)
                    load_v(sp, g, q)

            with sp.Fori(1, NG - 1) as g:
                values(g)
                wait_apart(sp, kq_loaded, GROUP_LOADS * DMA * (g + 1), passed)
                load_group(sp, K, Q, S, kq_loaded, g + 1, (g + 1) % 2, TP, P)
            values(NG - 1)

        @block.gpsimd
        def _(pool):
            def store_maxima(c):
                pool.wait_ge(m_low, c + 1)
                for part in range(2):
                    pool.dma_start(Q[ROW_M + part:ROW_M + part + 1, ds((c % (2 * NCH)) * (G * CH), G * CH)],
                                   m_parts[:, part, :]).then_inc(m_loaded, DMA)

            def store_output(c):
                pool.wait_ge(o_done, 1 + c + 1)
                pool.dma_start(S["att"][ds(c, 1)].rearrange("o (a p) c -> p (o a) c", p=P),
                               o_out[:].rearrange("p a h c -> p a (h c)")).then_inc(o_stored, DMA)

            pads = K[0:ROW_PAD, :].rearrange("r (g t) -> r g t", t=TP)
            pool.memset(pads[:, :, 0:P], 0.0).then_inc(pads_set, 1)
            pool.wait_ge(pads_set, 1)
            pool.memset(pads[:, :, P + T:TP], 0.0).then_inc(pads_set, 1)
            pool.wait_ge(pads_set, 2)
            pool.memset(V[:, 0, :], 0.0).then_inc(pads_set, 1)
            pool.wait_ge(pads_set, 3)
            pool.memset(V[:, KT + 1, :], 0.0).then_inc(pads_set, 1)
            pool.wait_ge(pads_set, 4)
            pool.memset(o_out[:], 1.0).then_inc(out_clear, 1)
            pool.wait_ge(out_clear, 1)
            pool.dma_start(S["att"][0:1].rearrange("o (a p) c -> p (o a) c", p=P),
                           o_out[:].rearrange("p a h c -> p a (h c)")).then_inc(o_stored, DMA)
            store_maxima(0)
            with pool.Fori(0, NCHUNKS - 1) as c:
                store_maxima(c + 1)
                store_output(c)
            store_output(NCHUNKS - 1)
            store_output(NCHUNKS)
            pool.wait_ge(o_stored, DMA * (NCHUNKS + 2))

        @block.vector
        def _(dve):
            def split_maxima(c):
                dve.wait_ge(mT_ready, c + 1)
                if not isinstance(c, int) or c > 0:
                    dve.wait_ge(m_loaded, 2 * DMA * c)
                nc.vector.tensor_copy(m_parts[:, 0, :], ps_m[0:G * TT, 0:P]).then_inc(m_high, 1)
                dve.wait_ge(m_high, c + 1)
                nc.vector.tensor_tensor(m_parts[:, 1, :], ps_m[0:G * TT, 0:P], m_parts[:, 0, :],
                                        ALU.subtract).then_inc(m_low, 1)

            def maxima(c, lo, hi):
                if lo == 0 and (not isinstance(c, int) or c > 0):
                    dve.wait_ge(nm_ready, c)
                for k in range(lo, hi):
                    if k % 2 == 0:
                        wait_apart(dve, a_ready, G * TT // 2 * c + k // 2 + 1, passed)
                    nc.vector.tensor_tensor_reduce(masked[:, k % 4, :], ps_a[:, (k % 4) * WIN:(k % 4 + 1) * WIN],
                                                   W["mask"][:], 1.0, 3 * NEG, ALU.add, ALU.max,
                                                   maxes[:, k:k + 1]).then_inc(a_done, 1)

            def whole_maxima(c):
                dve.wait_ge(a_done, 4 + G * TT * (c + 1))
                if not isinstance(c, int) or c > 0:
                    dve.wait_ge(mT_ready, c)
                nc.vector.tensor_scalar(neg_max[:], maxes[:], -1.0, None, ALU.mult).then_inc(nm_ready, 1)

            def normalise(c):
                dve.wait_ge(o_turned, c + 1)
                turned = ps_m[:].rearrange("p (a h w) -> p a h w", a=TT, h=G)
                nc.vector.reciprocal(recip[:], turned[:, :, :, C]).then_inc(o_recip, 1)
                dve.wait_ge(o_recip, c + 1)
                dve.wait_ge(o_stored, DMA * (c + 1))
                nc.vector.tensor_tensor(o_out[:], turned[:, :, :, 0:C],
                                        recip[:].unsqueeze(3).broadcast_to([P, TT, G, C]), ALU.mult
                                        ).then_inc(o_done, 1)

            dve.sem_inc(a_done, 4)
            dve.sem_inc(o_done, 1)
            maxima(0, 0, G * TT)
            whole_maxima(0)
            split_maxima(0)
            maxima(1, 0, G * TT)
            whole_maxima(1)
            with dve.Fori(0, NCHUNKS - 2) as c:
                split_maxima(c + 1)
                maxima(c + 2, 0, G * TT)
                whole_maxima(c + 2)
                normalise(c)
            split_maxima(NCHUNKS - 1)
            for c in (NCHUNKS - 2, NCHUNKS - 1, NCHUNKS):
                normalise(c)

        @block.scalar
        def _(act):
            def exponential(c, j):
                kt, lo, hi = TILES[j]
                act.wait_ge(s_ready, NS * c + j + 1)
                act.wait_ge(pv_done, NS * c + j + 1)
                s = ps_s[:, (j % 2) * 2 * CH:(j % 2 + 1) * 2 * CH].rearrange("p (h q) -> p h q", h=G)
                nc.scalar.activation(prob[:, j % PROBS, :, 0:hi - lo], s[:, :, 0:hi - lo], ACT.Exp,
                                     scale=scale).then_inc(exp_done, 1)

            def copy_output(c):
                act.wait_ge(pv_done, PROBS + NS * (c + 1))
                act.wait_ge(o_turned, c + 1)
                nc.scalar.activation(oT[:], ps_o[:], ACT.Copy).then_inc(oT_ready, 1)

            constant_rows(act, K, Q, W, rows_set, zeros_set)
            act.wait_ge(zeros_set, DMA)
            pad_row = K[ROW_PAD:ROW_PAD + 1, :].rearrange("r (g t) -> r g t", t=TP)
            for o in (0, P + T):
                act.dma_start(pad_row[:, :, o:o + P], W["neg_bf"][:]).then_inc(rows_set, DMA)
            act.sem_inc(exp_done, 2)
            nc.scalar.activation(oT[:], W["ones"][:], ACT.Copy).then_inc(oT_ready, 1)
            for j in range(NS):
                exponential(0, j)
            with act.Fori(1, NCHUNKS) as c:
                exponential(c, 0)
                exponential(c, 1)
                copy_output(c - 1)
                for j in range(2, NS):
                    exponential(c, j)
            copy_output(NCHUNKS - 1)

        @block.tensor
        def _(pe):
            def maximum_scores(g, half, qc, pair):
                c = NCH * g + qc
                pe.wait_ge(a_done, G * TT * c + 2 * pair + 2)
                for r in range(2):
                    h, qt = (2 * pair + r) // TT, (2 * pair + r) % TT
                    q0 = half * GQ + (qc * G + h) * CH + qt * P
                    k0 = half * GK + h * TP + qc * CH + qt * P + P - REACH
                    slot = (2 * pair + r) % 4
                    last = nc.tensor.matmul(ps_a[:, slot * WIN:(slot + 1) * WIN], Q[0:ROW_M, ds(q0, P)],
                                            K[0:ROW_M, ds(k0, WIN)], start=True, stop=True,
                                            skip_group_check=True)
                last.then_inc(a_ready, 1)

            def turn_maxima(c):
                pe.wait_ge(nm_ready, c + 1)
                if not isinstance(c, int) or c > 0:
                    pe.wait_ge(m_low, c)
                    pe.wait_ge(o_done, c)
                nc.tensor.transpose(ps_m[0:G * TT, 0:P], neg_max[:], W["ident"][:]).then_inc(mT_ready, 1)

            def turn_output(c, m_users):
                pe.wait_ge(oT_ready, c + 1)
                pe.wait_ge(m_low, m_users)
                pe.wait_ge(o_done, c + 1)
                for a in range(TT):
                    last = nc.tensor.transpose(ps_m[:, a * P:(a + 1) * P], oT[:, a * P:(a + 1) * P],
                                               W["ident"][:])
                last.then_inc(o_turned, 1)

            def scores(g, half, qc, j):
                kt, lo, hi = TILES[j]
                w = hi - lo
                first = lo - (kt * P - REACH)
                pe.wait_ge(exp_done, NS * (NCH * g + qc) + j + 1)
                for pair in range(2):
                    base = (j % 2) * 2 * CH + pair * CH
                    for r in range(2):
                        h = 2 * pair + r
                        nc.tensor.matmul(ps_s[:, base + r * WIN:base + r * WIN + w],
                                         K[:, ds(half * GK + h * TP + P + qc * CH + kt * P, P)],
                                         Q[:, ds(half * GQ + (qc * G + h) * CH + lo, w)],
                                         start=(r == 0), stop=False, skip_group_check=True)
                    for r in range(2):
                        last = nc.tensor.matmul(ps_s[:, base + r * WIN:base + r * WIN + w],
                                                W["ident_bf"][:], W["mask_bf"][:, first:first + w],
                                                start=False, stop=True, skip_group_check=True)
                last.then_inc(s_ready, 1)

            def add_values(g, qc, j):
                kt, lo, hi = TILES[j]
                c = NCH * g + qc
                if j == 0:
                    pe.wait_ge(oT_ready, c + 1)
                    pe.wait_ge(v_loaded[qc], DMA * (g + 1))
                if j == NS - 1 and qc < NCH - 1:
                    pe.wait_ge(v_loaded[qc + 1], DMA * (g + 1))
                pe.wait_ge(exp_done, 2 + NS * c + j + 1)
                for h in range(G):
                    last = nc.tensor.matmul(ps_o[h * VW:(h + 1) * VW, lo:hi],
                                            V[:, 1 + qc * TT + kt, h * VW:(h + 1) * VW],
                                            prob[:, j % PROBS, h, 0:hi - lo], start=(j == 0),
                                            stop=(j == NS - 1), skip_group_check=True)
                last.then_inc(pv_done, 1)

            def group(g, half, next_half, more):
                for qc in range(NCH):
                    c = NCH * g + qc
                    ahead = qc + 2 < NCH or more
                    turn = qc + 1 < NCH or more
                    a_g, a_half, a_qc = (g, half, qc + 2) if qc + 2 < NCH else (g + 1, next_half, qc - 2)
                    if ahead and a_qc == 0:
                        pe.wait_ge(kq_loaded, GROUP_LOADS * DMA * (a_g + 1))
                    pe.wait_ge(m_loaded, 2 * DMA * (c + 1))
                    pairs = list(range(G * TT // 2))
                    for j in range(NS):
                        scores(g, half, qc, j)
                        if j == 0 and turn:
                            turn_maxima(c + 1)
                        if ahead:
                            for _ in range(2 if 0 < j < NS - 1 else 0):
                                maximum_scores(a_g, a_half, a_qc, pairs.pop(0))
                        if j == 4:
                            turn_output(c, c + 2 if turn else c + 1)
                        if j > 1:
                            add_values(g, qc, j - 2)
                        elif qc > 0:
                            add_values(g, qc - 1, NS + j - 2)
                add_values(g, NCH - 1, NS - 2)
                add_values(g, NCH - 1, NS - 1)

            pe.sem_inc(pv_done, PROBS)
            pe.wait_ge(rows_set, CONST_ROWS * DMA + 2 * DMA)
            pe.wait_ge(pads_set, 4)
            pe.wait_ge(kq_loaded, GROUP_LOADS * DMA)
            for c in range(2):
                for pair in range(G * TT // 2):
                    maximum_scores(0, 0, c, pair)
                if c == 0:
                    turn_maxima(0)
            with pe.Fori(0, NG - 1) as g:
                group(g, g % 2, (g + 1) % 2, True)
            group(NG - 1, (NG - 1) % 2, 0, False)
            turn_output(NCHUNKS, NCHUNKS)



TILES_BODY = 2 * TT


def ahead(i, j, k, more):
    return (i, j + k) if j + k < TILES_BODY else (i + 1, j + k - TILES_BODY) if more else None


def phase_router(nc, W):
    with ExitStack() as ctx:
        n = Names(nc, ctx, "r")
        groups = B * KT * 2
        top = n.sb("top", [P, groups])
        total = n.sb("total", [P, groups])
        inv = n.sb("inv", [P, groups])
        step = n.sem("step")
        exp_done = n.sem("exp_done")
        block = ctx.enter_context(nc.Block())
        logits = W["logits"][:].rearrange("p b t r e -> p (b t r) e")
        each = lambda x: x[:].unsqueeze(2).broadcast_to([P, groups, E])

        @block.scalar
        def _(act):
            act.wait_ge(step, 2)
            nc.scalar.activation(W["logits"][:].rearrange("p b t r e -> p (b t r e)"),
                                 W["logits"][:].rearrange("p b t r e -> p (b t r e)"), ACT.Exp
                                 ).then_inc(exp_done, 1)

        @block.vector
        def _(dve):
            nc.vector.tensor_reduce(top[:], logits, AX.X, ALU.max).then_inc(step, 1)
            dve.wait_ge(step, 1)
            nc.vector.tensor_tensor(logits, logits, each(top), ALU.subtract).then_inc(step, 1)
            dve.wait_ge(exp_done, 1)
            nc.vector.tensor_reduce(total[:], logits, AX.X, ALU.add).then_inc(step, 1)
            dve.wait_ge(step, 3)
            nc.vector.reciprocal(inv[:], total[:]).then_inc(step, 1)
            dve.wait_ge(step, 4)
            per_token = inv[:].rearrange("p (b t r) -> p b t r", b=B, r=2)
            nc.vector.tensor_tensor(per_token, per_token,
                                    W["inv_n"][:].unsqueeze(1).unsqueeze(3).broadcast_to([P, B, KT, 2]),
                                    ALU.mult).then_inc(step, 1)
            dve.wait_ge(step, 5)
            inverse = inv[:].rearrange("p (t r) -> p t r", r=2)[:, :, 1]
            nc.vector.tensor_scalar(inverse, inverse, W["alpha"][:], None, ALU.mult).then_inc(step, 1)
            dve.wait_ge(step, 6)
            nc.vector.tensor_tensor(logits, logits, each(inv), ALU.mult).then_inc(step, 1)


def load_att(sp, S, att, loaded, i, u):
    for hg in range(NG2):
        slot = (u * NG2 + hg) * NCH + i + 1
        sp.dma_start(att[:, u, :, hg * G * C:(hg + 1) * G * C],
                     S["att"][ds(slot, 1)].rearrange("o (a p) c -> p (o a) c", p=P)).then_inc(loaded, DMA)


def store_and_load(sp, passed, x1_done, stored, x_io, out_dram, load):
    def store(i, u):
        wait_apart(sp, x1_done, 2 + TILES_BODY * i + TT * (u + 1), passed)
        sp.dma_start(out_dram[u, ds(i * CH, CH), :].rearrange("(t p) d -> p t d", p=P), x_io[:, u]
                     ).then_inc(stored[u], DMA)

    load(0, 0)
    load(0, 1)
    with sp.Fori(0, NCH - 1) as i:
        for u in range(2):
            store(i, u)
            wait_apart(sp, stored[u], DMA * (i + 1), passed)
            load(i + 1, u)
    for u in range(2):
        store(NCH - 1, u)
    for u in range(2):
        wait_apart(sp, stored[u], DMA * NCH, passed)


def phase_combine_experts(nc, W, S, x_dram, out_dram):
    with ExitStack() as ctx:
        n_ = Names(nc, ctx, "c0")
        x_io = n_.sb("x_io", [P, 2, TT, D])
        xn = n_.sb("xn", [P, 2, TT, D])
        att = n_.sb("att", [P, 2, TT, D])
        xT = n_.sb("xT", [P, 2, 2, DK, CH], F32R)
        cT = n_.sb("cT", [P, 2, 2, DK, CH], F32R)
        xv = n_.sb("xv", [P, 2 * KR])
        prod = n_.sb("prod", [P, 2 * KR])
        wprod = n_.sb("wprod", [P, 2 * KR])
        pT = n_.sb("pT", [P, 2, 2 * KR], F32R)
        aT = n_.sb("aT", [P, 2, D], F32R)
        wT = n_.sb("wT", [2 * E, P])
        wtile = n_.sb("wtile", [P, TILES_BODY, 2 * E])
        sums = n_.sb("sums", [P, 2, D])
        eg = n_.sb("eg", [P, D])
        gate = n_.sb("gate", [P, 2, D])
        ps_xv = n_.ps("ps_xv", 2 * CH)
        ps_cy = n_.ps("ps_cy", 2 * CH)
        ps_pt = n_.ps("ps_pt", 2 * CH)
        ps_out = n_.ps("ps_out", CH)
        ps_m = n_.ps("ps_m", CH)

        passed = n_.sem("passed")
        loaded = [n_.sem(f"loaded{u}") for u in range(2)]
        stored = [n_.sem(f"stored{u}") for u in range(2)]
        xv_ready = n_.sem("xv_ready")
        cy_ready = n_.sem("cy_ready")
        xv_copied = n_.sem("xv_copied")
        prod_done = n_.sem("prod_done")
        wprod_done = n_.sem("wprod_done")
        m_ready = n_.sem("m_ready")
        pt_ready = n_.sem("pt_ready")
        high = n_.sem("high")
        low = n_.sem("low")
        out_ready = n_.sem("out_ready")
        exp_done = n_.sem("exp_done")
        bias_done = n_.sem("bias_done")
        step = n_.sem("step")
        out_read = n_.sem("out_read")
        wtile_done = n_.sem("wtile_done")
        mixed = n_.sem("mixed")
        x1_done = n_.sem("x1_done")

        block = ctx.enter_context(nc.Block())
        n_loads = 4 * DK + 2 + NG2
        order = [(u, t) for u in range(2) for t in range(TT)]

        @block.sync
        def _(sp):
            def load(i, u):
                tok = ds(i * CH, CH)
                for part in range(2):
                    for k in range(DK):
                        sp.dma_start(f32(xT[:, u, part, k, :]), S["xT"][u, part, k, :, tok]).then_inc(loaded[u], DMA)
                        sp.dma_start(f32(cT[:, u, part, k, :]), S["cT"][u, part, k, :, tok]).then_inc(loaded[u], DMA)
                rows = lambda x: x[u, tok, :].rearrange("(t p) d -> p t d", p=P)
                sp.dma_start(x_io[:, u], rows(x_dram)).then_inc(loaded[u], DMA)
                sp.dma_start(xn[:, u], rows(S["xn"])).then_inc(loaded[u], DMA)
                load_att(sp, S, att, loaded[u], i, u)

            store_and_load(sp, passed, x1_done, stored, x_io, out_dram, load)

        @block.tensor
        def _(pe):
            def front(i, j):
                u, t = order[j]
                n = TILES_BODY * i + j
                if t == 0:
                    pe.wait_ge(loaded[u], DMA * n_loads * (i + 1))
                pe.wait_ge(xv_copied, n + 1)
                for r in range(2):
                    last = split_matmul(nc, ps_xv[:, r * CH:(r + 1) * CH],
                                        lambda s, k: xT[:, u, s, k, t * P:(t + 1) * P],
                                        lambda s, k: W["AQ"][:, s, k, r * KR:(r + 1) * KR], DK, True, True)
                last.then_inc(xv_ready, 1)
                pe.wait_ge(prod_done, n + 1)
                for r in range(2):
                    last = split_matmul(nc, ps_cy[:, r * CH:(r + 1) * CH],
                                        lambda s, k: cT[:, u, s, k, t * P:(t + 1) * P],
                                        lambda s, k: W["BK"][:, s, k, r * KR:(r + 1) * KR], DK, True, True)
                last.then_inc(cy_ready, 1)

            def turn(i, j):
                u, t = order[j]
                n = TILES_BODY * i + j
                if t == 0:
                    pe.wait_ge(wtile_done, 2 * i + u + 1)
                pe.wait_ge(low, 3 * (n + 1))
                for k in range(DK):
                    nc.tensor.transpose(ps_m[:, k * P:(k + 1) * P], att[:, u, t, k * P:(k + 1) * P],
                                        W["ident"][:])
                nc.tensor.transpose(ps_m[0:2 * E, D:D + P], wtile[:, j, :], W["ident"][:]
                                    ).then_inc(m_ready, 1)
                pe.wait_ge(wprod_done, 1 + n + 1)
                for half in range(2):
                    for m in range(TT):
                        c = (half * TT + m) * P
                        last = nc.tensor.transpose(ps_pt[:, c:c + P], wprod[:, c:c + P], W["ident"][:])
                    last.then_inc(pt_ready, 1)

            def out(i, j):
                n = TILES_BODY * i + j
                pe.wait_ge(out_read, n + 1)
                pe.wait_ge(high, 4 * (n + 1))
                pe.wait_ge(low, 3 + 3 * (n + 1))
                split_matmul(nc, ps_out[:, 0:D], lambda s, k: aT[:, s, k * P:(k + 1) * P],
                             lambda s, k: W["o0"][:, s, k, :], DK, True, True)
                split_matmul(nc, ps_out[:, D:2 * D], lambda s, k: pT[:, s, k * P:(k + 1) * P],
                             lambda s, k: W["UO"][:, s, k, :], 2 * KR // P, True, False)
                nc.tensor.matmul(ps_out[:, D:2 * D], wT[:], W["bO"][:], start=False, stop=True,
                                 skip_group_check=True).then_inc(out_ready, 1)

            pe.sem_inc(out_ready, 1)

            def body(i, more):
                for j in range(TILES_BODY):
                    turn(i, j)
                    if ahead(i, j, 1, more):
                        front(*ahead(i, j, 1, more))
                    out(i, j)

            front(0, 0)
            with pe.Fori(0, NCH - 1) as i:
                body(i, True)
            body(NCH - 1, False)

        @block.scalar
        def _(act):
            def copies(i, j):
                n = TILES_BODY * i + j
                act.wait_ge(out_ready, n + 1)
                act.wait_ge(m_ready, n + 1)
                nc.scalar.activation(aT[:, 0, :], ps_m[:, 0:D], ACT.Copy).then_inc(high, 1)
                nc.scalar.activation(wT[:], ps_m[0:2 * E, D:D + P], ACT.Copy).then_inc(high, 1)
                for half in range(2):
                    act.wait_ge(pt_ready, 2 * n + half + 1)
                    nc.scalar.activation(pT[:, 0, half * CH:(half + 1) * CH],
                                         ps_pt[:, half * CH:(half + 1) * CH], ACT.Copy).then_inc(high, 1)

            def left(i, j):
                n = TILES_BODY * i + j
                act.wait_ge(xv_ready, n + 1)
                act.wait_ge(prod_done, n + 1)
                nc.scalar.activation(xv[:], ps_xv[:], ACT.Copy).then_inc(xv_copied, 1)

            def exponential(i, j):
                n = TILES_BODY * i + j
                act.wait_ge(out_ready, 1 + n + 1)
                act.wait_ge(out_read, n + 1)
                nc.scalar.activation(eg[:], ps_out[:, D:2 * D], ACT.Exp, scale=-1.0).then_inc(exp_done, 1)

            act.sem_inc(xv_copied, 1)

            def body(i, more):
                for j in range(TILES_BODY):
                    copies(i, j)
                    if ahead(i, j, 1, more):
                        left(*ahead(i, j, 1, more))
                    exponential(i, j)

            left(0, 0)
            with act.Fori(0, NCH - 1) as i:
                body(i, True)
            body(NCH - 1, False)

        @block.vector
        def _(dve):
            def rests(i, j):
                n = TILES_BODY * i + j
                dve.wait_ge(high, 4 * n + 2)
                nc.vector.tensor_tensor(aT[:, 1, :], ps_m[:, 0:D], f32(aT[:, 0, :]), ALU.subtract).then_inc(low, 1)
                for half in range(2):
                    dve.wait_ge(high, 4 * n + 3 + half)
                    nc.vector.tensor_tensor(pT[:, 1, half * CH:(half + 1) * CH],
                                            ps_pt[:, half * CH:(half + 1) * CH],
                                            f32(pT[:, 0, half * CH:(half + 1) * CH]), ALU.subtract).then_inc(low, 1)

            def product(i, j):
                n = TILES_BODY * i + j
                dve.wait_ge(xv_copied, 1 + n + 1)
                dve.wait_ge(cy_ready, n + 1)
                dve.wait_ge(wprod_done, n + 1)
                nc.vector.tensor_tensor(prod[:], ps_cy[:], xv[:], ALU.mult).then_inc(prod_done, 1)

            dve.sem_inc(prod_done, 1)
            dve.sem_inc(low, 3)
            dve.sem_inc(out_read, 1)

            def body(i, more):
                for j in range(TILES_BODY):
                    n, slot = TILES_BODY * i + j, j % 2
                    rests(i, j)
                    if ahead(i, j, 1, more):
                        product(*ahead(i, j, 1, more))
                    gate_steps(nc, dve, n, sums[:, slot], sums[:, slot], (bias_done, n + 1),
                               gate[:, slot], eg[:], ps_out[:, 0:D], ps_out[:, D:2 * D],
                               exp_done, step, out_read, x1_done)

            product(0, 0)
            with dve.Fori(0, NCH - 1) as i:
                body(i, True)
            body(NCH - 1, False)

        @block.gpsimd
        def _(pool):
            def bias(i, j):
                u, t = order[j]
                n = TILES_BODY * i + j
                if t == 0:
                    pool.wait_ge(loaded[u], DMA * n_loads * (i + 1))
                pool.wait_ge(x1_done, n + 1)
                pool.tensor_tensor(sums[:, j % 2], xn[:, u, t], W["bo"][:, 0], ALU.add).then_inc(bias_done, 1)

            def weighted(i, j):
                u, t = order[j]
                n = TILES_BODY * i + j
                pool.wait_ge(prod_done, 1 + n + 1)
                if not isinstance(n, int) or n > 0:
                    pool.wait_ge(pt_ready, 2 * n)
                pool.tensor_tensor(wprod[:].rearrange("p (e r) -> p e r", r=R),
                                   prod[:].rearrange("p (e r) -> p e r", r=R),
                                   wtile[:, j].unsqueeze(2).broadcast_to([P, 2 * E, R]), ALU.mult
                                   ).then_inc(wprod_done, 1)

            pool.sem_inc(wprod_done, 1)
            pool.sem_inc(x1_done, 2)

            def router_weights(i, u, tiles_out):
                if tiles_out is not None:
                    wait_apart(pool, out_ready, 1 + tiles_out, passed)
                pool.tensor_copy(wtile[:, u * TT:(u + 1) * TT, :],
                                 W["logits"][:, u, ds(i * TT, TT), :, :]
                                 .rearrange("p t r e -> p t (r e)")).then_inc(wtile_done, 1)
                pool.wait_ge(wtile_done, 2 * i + u + 1)

            def body(i, more):
                for j in range(TILES_BODY):
                    u, t = order[j]
                    if j == TT - 2:
                        router_weights(i, 1, TILES_BODY * i)
                    if j == TILES_BODY - 2 and more:
                        router_weights(i + 1, 0, TILES_BODY * i + TT)
                    if ahead(i, j, 1, more):
                        bias(*ahead(i, j, 1, more))
                        weighted(*ahead(i, j, 1, more))
                    residual(pool, TILES_BODY * i + j, x_io[:, u, t], sums[:, j % 2], gate[:, j % 2],
                             out_read, mixed, x1_done)

            router_weights(0, 0, None)
            bias(0, 0)
            weighted(0, 0)
            with pool.Fori(0, NCH - 1) as i:
                body(i, True)
            body(NCH - 1, False)


def gate_steps(nc, dve, n, s_sum, bias, bias_ready, gate, eg, ps_s, ps_g, exp_done, step, out_read, x1_done):
    dve.wait_ge(exp_done, n + 1)
    nc.vector.tensor_scalar(eg, eg, 1.0, None, ALU.add).then_inc(step, 1)
    dve.wait_ge(*bias_ready)
    nc.vector.tensor_tensor(s_sum, ps_s, bias, ALU.add).then_inc(step, 1)
    dve.wait_ge(step, 3 * n + 1)
    nc.vector.reciprocal(eg, eg).then_inc(step, 1)
    dve.wait_ge(x1_done, n + 1)
    dve.wait_ge(step, 3 * n + 3)
    nc.vector.tensor_tensor(gate, ps_g, eg, ALU.mult).then_inc(out_read, 1)


def residual(pool, n, x, s, gate, out_read, mixed, x1_done, seed=1):
    pool.wait_ge(out_read, seed + n + 1)
    pool.tensor_tensor(s, s, gate, ALU.mult).then_inc(mixed, 1)
    pool.wait_ge(mixed, n + 1)
    pool.tensor_tensor(x, x, s, ALU.add).then_inc(x1_done, 1)


def phase_combine_lora(nc, W, S, x_dram, out_dram):
    NGT = E1 + E1 * R1
    with ExitStack() as ctx:
        n_ = Names(nc, ctx, "c1")
        x_io = n_.sb("x_io", [P, 2, TT, D])
        att = n_.sb("att", [P, 2, TT, D])
        xT = n_.sb("xT", [P, 2, 2, DK, CH], F32R)
        neg_top = n_.sb("neg_top", [P, 1])
        ge = n_.sb("ge", [P, E1])
        total = n_.sb("total", [P, 1])
        inv = n_.sb("inv", [P, 1])
        weight = n_.sb("weight", [P, E1])
        wt = n_.sb("wt", [P, 2, E1 * R1])
        turned = n_.sb("turned", [P, 2, 2, D + P], F32R)
        sums = n_.sb("sums", [P, 2, D])
        eg = n_.sb("eg", [P, 2, D])
        gate = n_.sb("gate", [P, 2, D])
        OUTS = 4
        ps_gt = n_.ps("ps_gt", 2 * CH)
        ps_out = n_.ps("ps_out", OUTS * CH)
        ps_m = n_.ps("ps_m", 2 * CH)

        passed = n_.sem("passed")
        loaded = [n_.sem(f"loaded{u}") for u in range(2)]
        x_loaded = [n_.sem(f"x_loaded{u}") for u in range(2)]
        stored = [n_.sem(f"stored{u}") for u in range(2)]
        gt_ready = n_.sem("gt_ready")
        soft = n_.sem("soft")
        ge_done = n_.sem("ge_done")
        wt_done = n_.sem("wt_done")
        m_ready = n_.sem("m_ready")
        high = n_.sem("high")
        low = n_.sem("low")
        out_ready = n_.sem("out_ready")
        exp_done = n_.sem("exp_done")
        step = n_.sem("step")
        out_read = n_.sem("out_read")
        mixed = n_.sem("mixed")
        x1_done = n_.sem("x1_done")

        block = ctx.enter_context(nc.Block())
        n_loads = 2 * DK + NG2
        order = [(u, t) for u in range(2) for t in range(TT)]

        @block.sync
        def _(sp):
            def load(i, u):
                tok = ds(i * CH, CH)
                for part in range(2):
                    for k in range(DK):
                        sp.dma_start(f32(xT[:, u, part, k, :]), S["xT"][u, part, k, :, tok]).then_inc(loaded[u], DMA)
                load_att(sp, S, att, loaded[u], i, u)

            def load_x(i, u):
                sp.dma_start(x_io[:, u], x_dram[u, ds(i * CH, CH), :].rearrange("(t p) d -> p t d", p=P)
                             ).then_inc(x_loaded[u], DMA)

            def store(i, u):
                wait_apart(sp, x1_done, 2 + TILES_BODY * i + TT * (u + 1), passed)
                sp.dma_start(out_dram[u, ds(i * CH, CH), :].rearrange("(t p) d -> p t d", p=P), x_io[:, u]
                             ).then_inc(stored[u], DMA)

            for u in range(2):
                load(0, u)
                load_x(0, u)
            with sp.Fori(0, NCH - 1) as i:
                for u in range(2):
                    wait_apart(sp, out_ready, 2 + TILES_BODY * i + TT * (u + 1), passed)
                    load(i + 1, u)
                    store(i, u)
                    wait_apart(sp, stored[u], DMA * (i + 1), passed)
                    load_x(i + 1, u)
            for u in range(2):
                store(NCH - 1, u)
            for u in range(2):
                wait_apart(sp, stored[u], DMA * NCH, passed)

        @block.tensor
        def _(pe):
            def front(i, j):
                u, t = order[j]
                n = TILES_BODY * i + j
                gt, g = (j % 2) * CH, (j % OUTS) * CH
                if t == 0:
                    pe.wait_ge(loaded[u], DMA * n_loads * (i + 1))
                x = lambda s, k: xT[:, u, s, k, t * P:(t + 1) * P]
                pe.wait_ge(wt_done, n + 1)
                split_matmul(nc, ps_gt[:, gt:gt + NGT], x, lambda s, k: W["gate"][:, s, k, 0:NGT], DK,
                             True, True).then_inc(gt_ready, 1)
                pe.wait_ge(out_read, n + 1)
                split_matmul(nc, ps_out[:, g:g + D], x, lambda s, k: W["gate"][:, s, k, NGT:], DK,
                             True, False)

            def turn(i, j):
                u, t = order[j]
                n = TILES_BODY * i + j
                o = (j % 2) * CH
                pe.wait_ge(low, n + 1)
                for k in range(DK):
                    nc.tensor.transpose(ps_m[:, o + k * P:o + (k + 1) * P], att[:, u, t, k * P:(k + 1) * P],
                                        W["ident"][:])
                pe.wait_ge(wt_done, 2 + n + 1)
                nc.tensor.transpose(ps_m[:, o + D:o + D + P], wt[:, j % 2], W["ident"][:]
                                    ).then_inc(m_ready, 1)

            def out(i, j):
                n = TILES_BODY * i + j
                g = (j % OUTS) * CH
                pe.wait_ge(high, n + 1)
                pe.wait_ge(low, 2 + n + 1)
                split_matmul(nc, ps_out[:, g + D:g + 2 * D], lambda s, k: turned[:, j % 2, s, k * P:(k + 1) * P],
                             lambda s, k: W["o1"][:, s, k, :], DK, False, True)
                split_matmul(nc, ps_out[:, g:g + D], lambda s, k: turned[:, j % 2, s, D:D + P],
                             lambda s, k: W["loraV"][:, s, 0, :], 1, False, True).then_inc(out_ready, 1)

            pe.sem_inc(out_ready, 2)

            def body(i, more):
                for j in range(TILES_BODY):
                    if ahead(i, j, 2, more):
                        front(*ahead(i, j, 2, more))
                    if ahead(i, j, 1, more):
                        turn(*ahead(i, j, 1, more))
                    out(i, j)

            front(0, 0)
            front(0, 1)
            turn(0, 0)
            with pe.Fori(0, NCH - 1) as i:
                body(i, True)
            body(NCH - 1, False)

        @block.scalar
        def _(act):
            def softmax(i, j):
                n = TILES_BODY * i + j
                gt = (j % 2) * CH
                act.wait_ge(soft, 3 * n + 1)
                nc.scalar.activation(ge[:], ps_gt[:, gt:gt + E1], ACT.Exp, bias=neg_top[:], accum_out=total[:]
                                     ).then_inc(ge_done, 1)

            def copies(i, j):
                n = TILES_BODY * i + j
                act.wait_ge(out_ready, n + 1)
                act.wait_ge(m_ready, n + 1)
                o = (j % 2) * CH
                nc.scalar.activation(turned[:, j % 2, 0, :], ps_m[:, o:o + D + P], ACT.Copy).then_inc(high, 1)

            def exponential(i, j):
                n = TILES_BODY * i + j
                g = (j % OUTS) * CH
                act.wait_ge(out_ready, 2 + n + 1)
                act.wait_ge(out_read, OUTS + n - 1)
                nc.scalar.activation(eg[:, j % 2], ps_out[:, g:g + D], ACT.Exp, scale=-1.0
                                     ).then_inc(exp_done, 1)

            def body(i, more):
                for j in range(TILES_BODY):
                    if ahead(i, j, 2, more):
                        softmax(*ahead(i, j, 2, more))
                    if ahead(i, j, 1, more):
                        copies(*ahead(i, j, 1, more))
                    exponential(i, j)

            softmax(0, 0)
            softmax(0, 1)
            copies(0, 0)
            with act.Fori(0, NCH - 1) as i:
                body(i, True)
            body(NCH - 1, False)

        @block.vector
        def _(dve):
            def maximum(i, j):
                n = TILES_BODY * i + j
                gt = (j % 2) * CH
                dve.wait_ge(gt_ready, n + 1)
                nc.vector.tensor_reduce(neg_top[:], ps_gt[:, gt:gt + E1], AX.X, ALU.max, negate=True
                                        ).then_inc(soft, 1)

            def gates(i, j):
                n = TILES_BODY * i + j
                gt = (j % 2) * CH
                dve.wait_ge(ge_done, n + 1)
                nc.vector.reciprocal(inv[:], total[:]).then_inc(soft, 1)
                dve.wait_ge(soft, 3 * n + 2)
                nc.vector.tensor_scalar(weight[:], ge[:], inv[:], 1.0 / R1, ALU.mult, ALU.mult).then_inc(soft, 1)
                dve.wait_ge(soft, 3 * n + 3)
                if not isinstance(n, int) or n > 1:
                    dve.wait_ge(m_ready, n - 1)
                nc.vector.tensor_tensor(wt[:, j % 2].rearrange("p (e r) -> p e r", r=R1),
                                        ps_gt[:, gt + E1:gt + NGT].rearrange("p (e r) -> p e r", r=R1),
                                        weight[:].unsqueeze(2).broadcast_to([P, E1, R1]), ALU.mult
                                        ).then_inc(wt_done, 1)

            def rest(i, j):
                n = TILES_BODY * i + j
                o = (j % 2) * CH
                dve.wait_ge(high, n + 1)
                nc.vector.tensor_tensor(turned[:, j % 2, 1, :], ps_m[:, o:o + D + P],
                                        f32(turned[:, j % 2, 0, :]), ALU.subtract).then_inc(low, 1)

            dve.sem_inc(wt_done, 2)
            dve.sem_inc(low, 2)
            dve.sem_inc(out_read, OUTS)

            def body(i, more):
                for j in range(TILES_BODY):
                    two, one = ahead(i, j, 2, more), ahead(i, j, 1, more)
                    if two:
                        maximum(*two)
                    if one:
                        rest(*one)
                    if two:
                        gates(*two)
                    n, slot, g = TILES_BODY * i + j, j % 2, (j % OUTS) * CH
                    gate_steps(nc, dve, n, sums[:, slot], W["bo"][:, 1], (x1_done, n + 1),
                               gate[:, slot], eg[:, slot], ps_out[:, g + D:g + 2 * D],
                               ps_out[:, g:g + D], exp_done, step, out_read, x1_done)

            maximum(0, 0)
            gates(0, 0)
            maximum(0, 1)
            rest(0, 0)
            gates(0, 1)
            with dve.Fori(0, NCH - 1) as i:
                body(i, True)
            body(NCH - 1, False)

        @block.gpsimd
        def _(pool):
            pool.sem_inc(x1_done, 2)
            with pool.Fori(0, NCH) as i:
                for j in range(TILES_BODY):
                    u, t = order[j]
                    if t == 0:
                        wait_apart(pool, x_loaded[u], DMA * (i + 1), passed)
                    residual(pool, TILES_BODY * i + j, x_io[:, u, t], sums[:, j % 2], gate[:, j % 2],
                             out_read, mixed, x1_done, OUTS)


def recurrent_blocks(nc, I, out):
    with ExitStack() as ctx:
        n = Names(nc, ctx, "k")
        W = {
            "AQ": n.sb("AQ", [P, 2, DK, 2 * KR], F32R), "BK": n.sb("BK", [P, 2, DK, 2 * KR], F32R),
            "RT": n.sb("RT", [P, 2, DK, 2 * D], F32R), "UO": n.sb("UO", [P, 2, 2 * KR // P, D], F32R),
            "bO": n.sb("bO", [2 * E, D]), "w2": n.sb("w2", [P, DK, E]),
            "qkv0": n.sb("qkv0", [P, 2, DK, 3 * D], F32R), "qkv1": n.sb("qkv1", [P, 2, DK, 3 * D], F32R),
            "o0": n.sb("o0", [P, 2, DK, D], F32R), "o1": n.sb("o1", [P, 2, DK, D], F32R),
            "gate": n.sb("gate", [P, 2, DK, E1 + E1 * R1 + D], F32R),
            "loraV": n.sb("loraV", [P, 2, 1, D], F32R),
            "bqk": n.sb("bqk", [P, 2, 4]), "bv": n.sb("bv", [P, 2, D]), "bo": n.sb("bo", [P, 2, D]),
            "b1": n.sb("b1", [P, DK]), "b2": n.sb("b2", [64, 1]), "alpha": n.sb("alpha", [P, 1]),
            "ident": n.sb("ident", [P, P]), "ident_bf": n.sb("ident_bf", [P, P], BF16),
            "mask": n.sb("mask", [P, WIN]), "mask_bf": n.sb("mask_bf", [P, WIN], BF16),
            "ones_bf": n.sb("ones_bf", [P, ROW_TILE], BF16), "zeros_bf": n.sb("zeros_bf", [P, ROW_TILE], BF16),
            "neg_bf": n.sb("neg_bf", [2 * G, P], BF16),
            "ones": n.sb("ones", [P, CH]), "half": n.sb("half", [P, TT]),
            "inv_n": n.sb("inv_n", [P, KT]),
            "logits": n.sb("logits", [P, B, KT, 2, E]),
        }
        S = {
            "xn": nc.dram_tensor("s_xn", [B, T, D], F32).ap(),
            "x1": nc.dram_tensor("s_x1", [B, T, D], F32).ap(),
            "xT": nc.dram_tensor("s_xT", [B, 2, DK, P, T], F32).ap(),
            "cT": nc.dram_tensor("s_cT", [B, 2, DK, P, T], F32).ap(),
            "parts": nc.dram_tensor("s_parts", [2, B, 3, D, T], BF16).ap(),
            "v": nc.dram_tensor("s_v", [B, NG2, P, KT, G * VW], F32).ap(),
            "att": nc.dram_tensor("s_att", [NIT + 1, CH, G * C], F32).ap(),
        }
        phase_weights(nc, W, I)
        phase_project(nc, W, S, I["x"], 0)
        phase_router(nc, W)
        phase_attend_full(nc, W, S)
        phase_combine_experts(nc, W, S, I["x"], S["x1"])
        phase_project(nc, W, S, S["x1"], 1)
        phase_attend_band(nc, W, S)
        phase_combine_lora(nc, W, S, S["x1"], out)


def layouts(a):
    import numpy as np
    wide = lambda w: w.transpose(1, 0, 2).reshape(w.shape[1], -1)
    lay = {
        "x": a["L0_attn_x"],
        "w_qkvT_0": a["L0_attn_w_qkv"].T, "w_oT_0": a["L0_attn_w_o"].T,
        "w_qkv_1": a["L1_attn_w_qkv"], "w_out_1": a["L1_attn_w_out"],
        "b_qkv_0": a["L0_attn_b_qkv"], "b_qkv_1": a["L1_attn_b_qkv"],
        "b_o_0": a["L0_attn_b_o"], "b_o_1": a["L1_attn_b_out"],
        "W_Q": a["L0_ffn_W_Q"], "W_K": a["L0_ffn_W_K"], "W_invT": a["L0_ffn_W_inv"].T,
        "W_OT": a["L0_ffn_W_O"].T, "router_w1T": a["L0_ffn_router_w1"].T,
        "V_fwd": wide(a["L0_ffn_V_fwd"]), "W_fwd": wide(a["L0_ffn_W_fwd"]), "U_fwd": wide(a["L0_ffn_U_fwd"]),
        "V_inv": wide(a["L0_ffn_V_inv"]), "W_inv_exp": wide(a["L0_ffn_W_inv_exp"]),
        "U_inv": wide(a["L0_ffn_U_inv"]),
        "b_fwdT": a["L0_ffn_b_fwd"].T, "b_invT": a["L0_ffn_b_inv"].T,
        "router_b1": a["L0_ffn_router_b1"], "router_w2T": a["L0_ffn_router_w2"].T,
        "router_b2": a["L0_ffn_router_b2"], "expert_bias": a["L0_ffn_expert_bias"],
        "alpha": a["L0_ffn_alpha_bi"].reshape(1),
        "weightT": a["L1_ffn_weight"].T, "gateT": a["L1_ffn_gate_w"].T,
        "lora_UT": a["L1_ffn_lora_U"].reshape(E1 * R1, D).T,
        "lora_V": a["L1_ffn_lora_V"].transpose(0, 2, 1).reshape(E1 * R1, D),
    }
    return {k: np.ascontiguousarray(v) for k, v in lay.items()}


def kernel(**inputs):
    import numpy as np
    import concourse.bacc as bacc
    from concourse.bass_utils import run_bass_kernel_spmd

    nc = bacc.Bacc("TRN2", target_bir_lowering=False, num_devices=1)
    arrays, I = {}, {}
    for name, a in layouts({k: np.asarray(v) for k, v in inputs.items()}).items():
        arrays[f"in_{name}"] = a
        I[name] = nc.dram_tensor(f"in_{name}", a.shape, mybir.dt.from_np(a.dtype), kind="ExternalInput").ap()
    for pair in ("b_qkv", "b_o"):
        I[pair] = (I[f"{pair}_0"], I[f"{pair}_1"])
    out = nc.dram_tensor("out", (B, T, D), F32, kind="ExternalOutput").ap()
    recurrent_blocks(nc, I, out)
    r = run_bass_kernel_spmd(nc, [arrays], core_ids=[0])
    return r.results[0]["out"]
```
